# Optimizing a Trainium2 kernel written in Bass

```python
import numpy as np
import jax
import jax.numpy as jnp

def _softmax(x, axis=-1):
    return jax.nn.softmax(x, axis=axis)

def _gelu(x):
    return jax.nn.gelu(x, approximate=True)

def _silu(x):
    return jax.nn.silu(x)

def _sigmoid(x):
    return jax.nn.sigmoid(x)

def _layernorm(x, axis=-1, eps=1e-05):
    m = jnp.mean(x, axis=axis, keepdims=True)
    v = jnp.var(x, axis=axis, keepdims=True)
    return (x - m) / jnp.sqrt(v + eps)

def _scatter_add(tgt, idx, src, axis=0):
    return tgt.at[idx].add(src)

def _segment_sum(src, seg, n):
    return jax.ops.segment_sum(src, seg, n)
kernel_name = 'mk_gnn_preln_d4_gnn_r64_acff18'

def setup_inputs(seed: int=0):
    np.random.seed(seed)
    _w = jnp.asarray

    def _rec_inputs():
        import jax
        import jax.numpy as jnp
        _gk = jax.random.key(seed)
        x = -0.0005121 + 1.001 * jax.random.normal(jax.random.fold_in(_gk, 1), (100000, 32), jnp.float32)
        src = jax.random.randint(jax.random.fold_in(_gk, 2), (25000,), 0, 100000, jnp.int32)
        dst = jnp.minimum((100000 * jax.random.uniform(jax.random.fold_in(_gk, 3), (25000,)) ** 2.0).astype(jnp.int32), 99999)
        _o = jnp.argsort(dst, stable=True)
        src = src[_o]
        dst = dst[_o]
        edge_type_86 = jax.random.randint(jax.random.fold_in(_gk, 13), (25000,), 0, 86, jnp.int32)
        return (x, src, dst, edge_type_86)
    x, src, dst, edge_type_86 = _rec_inputs()

    def _L0_gnn_setup():
        import jax, jax.numpy as jnp
        import numpy as np
        N_NODES = 100000
        N_EDGES = 25000
        D_FEAT = 32
        key = jax.random.key(seed)
        k1, k2, k3 = jax.random.split(key, 3)
        x = jax.random.normal(k1, (N_NODES, D_FEAT), dtype=jnp.float32)
        edge_row = jax.random.randint(k2, (N_EDGES,), 0, N_NODES, dtype=jnp.int64)
        edge_col = jax.random.randint(k3, (N_EDGES,), 0, N_NODES, dtype=jnp.int64)
        return {'x': x, 'edge_row': edge_row, 'edge_col': edge_col}
    _L0_gnn_all = _L0_gnn_setup()
    _L0_gnn_in = {k: v for k, v in _L0_gnn_all.items() if k in ()}
    del _L0_gnn_all

    def _L1_gnn_setup():
        import jax, jax.numpy as jnp
        import numpy as np
        N_NODES = 100000
        N_EDGES = 25000
        D_FEAT = 32
        THETA = np.array([1.0, -0.55, 0.3, -0.15, 0.075], dtype=np.float32)
        key = jax.random.key(seed)
        k1, k2 = jax.random.split(key)
        h = jax.random.normal(k1, (N_NODES, D_FEAT), dtype=jnp.float32)
        edge_index = jax.random.randint(k2, (2, N_EDGES), 0, N_NODES, dtype=jnp.int64)
        theta = jnp.asarray(THETA)
        return {'h': h, 'edge_index': edge_index, 'theta': theta}
    _L1_gnn_all = _L1_gnn_setup()
    _L1_gnn_in = {k: v for k, v in _L1_gnn_all.items() if k in ('theta',)}
    del _L1_gnn_all

    def _L2_gnn_setup():
        import jax, jax.numpy as jnp
        import numpy as np
        N_NODES = 50000
        N_EDGES = 12500
        INP_DIM = 32
        OUT_DIM = 32
        ATTN_DIM = 32
        NUM_RELS = 86
        NUM_BASES = 16
        GAMMA = 0.0
        key = jax.random.key(seed)
        ks = jax.random.split(key, 12)
        return {'h': jax.random.normal(ks[0], (N_NODES, INP_DIM), jnp.float32), 'weight': jax.random.normal(ks[1], (NUM_BASES, INP_DIM, OUT_DIM), jnp.float32), 'w_comp': jax.random.normal(ks[2], (NUM_RELS, NUM_BASES), jnp.float32), 'self_loop_weight': jax.random.normal(ks[3], (INP_DIM, OUT_DIM), jnp.float32), 'A1_w': jax.random.normal(ks[4], (ATTN_DIM, INP_DIM), jnp.float32), 'A1_b': jax.random.normal(ks[5], (ATTN_DIM,), jnp.float32), 'A2_w': jax.random.normal(ks[6], (ATTN_DIM, INP_DIM), jnp.float32), 'A2_b': jax.random.normal(ks[7], (ATTN_DIM,), jnp.float32), 'rel_emb': jax.random.normal(ks[8], (NUM_RELS, ATTN_DIM), jnp.float32), 'src': jax.random.randint(ks[9], (N_EDGES,), 0, N_NODES, jnp.int32), 'dst': jax.random.randint(ks[10], (N_EDGES,), 0, N_NODES, jnp.int32), 'etype': jax.random.randint(ks[11], (N_EDGES,), 0, NUM_RELS, jnp.int32)}
    _L2_gnn_all = _L2_gnn_setup()
    _L2_gnn_in = {k: v for k, v in _L2_gnn_all.items() if k in ('weight', 'w_comp', 'self_loop_weight', 'A1_w', 'A1_b', 'A2_w', 'A2_b', 'rel_emb')}
    del _L2_gnn_all

    def _L3_gnn_setup():
        import jax, jax.numpy as jnp
        import numpy as np
        ALPHA = 0.1
        K = 10
        key = jax.random.key(seed)
        k1, k2, k3 = jax.random.split(key, 3)
        N, E, D = (100000, 25000, 32)
        feat = jax.random.normal(k1, (N, D), dtype=jnp.float32)
        src = jax.random.randint(k2, (E,), 0, N)
        dst = jax.random.randint(k3, (E,), 0, N)
        return {'feat': feat, 'src': src, 'dst': dst}
    _L3_gnn_all = _L3_gnn_setup()
    _L3_gnn_in = {k: v for k, v in _L3_gnn_all.items() if k in ()}
    del _L3_gnn_all
    return {'x': x, 'src': src, 'dst': dst, 'edge_type_86': edge_type_86, 'L1_gnn_theta': _L1_gnn_in['theta'], 'L2_gnn_weight': _L2_gnn_in['weight'], 'L2_gnn_w_comp': _L2_gnn_in['w_comp'], 'L2_gnn_self_loop_weight': _L2_gnn_in['self_loop_weight'], 'L2_gnn_A1_w': _L2_gnn_in['A1_w'], 'L2_gnn_A1_b': _L2_gnn_in['A1_b'], 'L2_gnn_A2_w': _L2_gnn_in['A2_w'], 'L2_gnn_A2_b': _L2_gnn_in['A2_b'], 'L2_gnn_rel_emb': _L2_gnn_in['rel_emb']}

def reference(x, src, dst, edge_type_86, L1_gnn_theta, L2_gnn_weight, L2_gnn_w_comp, L2_gnn_self_loop_weight, L2_gnn_A1_w, L2_gnn_A1_b, L2_gnn_A2_w, L2_gnn_A2_b, L2_gnn_rel_emb):
    import jax
    import jax.numpy as jnp

    def _L0_gnn_ref(x, edge_row, edge_col):
        import jax, jax.numpy as jnp
        import numpy as np
        N_NODES = 100000
        N_EDGES = 25000
        D_FEAT = 32
        n = x.shape[0]
        deg = jax.ops.segment_sum(jnp.ones(edge_row.shape[0], dtype=x.dtype), edge_row, num_segments=n)
        norm = jax.lax.rsqrt(1.0 + deg)[:, None]
        xs = norm * x
        agg = jax.ops.segment_sum(xs[edge_col], edge_row, num_segments=n)
        return norm * (agg + xs)

    def _L1_gnn_ref(h, edge_index, theta):
        import jax, jax.numpy as jnp
        import numpy as np
        N_NODES = 100000
        N_EDGES = 25000
        D_FEAT = 32
        THETA = np.array([1.0, -0.55, 0.3, -0.15, 0.075], dtype=np.float32)
        n = h.shape[0]
        row, col = (edge_index[0], edge_index[1])
        deg = jax.ops.segment_sum(jnp.ones(row.shape[0], h.dtype), row, num_segments=n)
        dis = jnp.where(deg > 0, jax.lax.rsqrt(deg), 0.0)
        w = -dis[row] * dis[col]

        def lap_mm(feat):
            msg = w[:, None] * feat[col]
            return feat + jax.ops.segment_sum(msg, row, num_segments=n)
        feat = h
        out = theta[0] * feat
        for k in range(1, theta.shape[0]):
            feat = lap_mm(feat)
            out = out + theta[k] * feat
        return out

    def _L2_gnn_ref(h, weight, w_comp, self_loop_weight, A1_w, A1_b, A2_w, A2_b, rel_emb, src, dst, etype):
        import jax, jax.numpy as jnp
        import numpy as np
        N_NODES = 50000
        N_EDGES = 12500
        INP_DIM = 32
        OUT_DIM = 32
        ATTN_DIM = 32
        NUM_RELS = 86
        NUM_BASES = 16
        GAMMA = 0.0
        E = src.shape[0]
        N = h.shape[0]
        x = h[src]
        y = h[dst]
        c = w_comp[etype]
        xb = jnp.einsum('ei,bio->ebo', x, weight)
        msg = jnp.einsum('eb,ebo->eo', c, xb)
        x_hat = x @ A1_w.T + A1_b
        y_hat = y @ A2_w.T + A2_b + rel_emb[etype]
        scale = jnp.sqrt(jnp.asarray(INP_DIM, h.dtype))
        a = jnp.tanh(jax.nn.relu(jnp.sum(x_hat * y_hat, axis=-1) / scale))
        a = jnp.where(a > GAMMA, a, jnp.zeros_like(a))
        nei = jax.ops.segment_sum(a[:, None] * msg, dst, num_segments=N)
        last_e = jax.ops.segment_max(jnp.arange(E, dtype=jnp.int32), dst, num_segments=N)
        last_e = jnp.clip(last_e, 0, E - 1)
        curr = h[src[last_e]] @ self_loop_weight
        in_deg = jax.ops.segment_sum(jnp.ones((E,), h.dtype), dst, num_segments=N)
        h_new = jnp.where((in_deg > 0)[:, None], nei + curr, jnp.zeros_like(nei))
        return jax.nn.relu(h_new)

    def _L3_gnn_ref(feat, src, dst):
        import jax, jax.numpy as jnp
        import numpy as np
        ALPHA = 0.1
        K = 10
        N = feat.shape[0]
        deg = jax.ops.segment_sum(jnp.ones_like(dst, dtype=feat.dtype), dst, num_segments=N)
        norm = jnp.where(deg > 0, deg ** (-0.5), 0.0)[:, None]
        feat_0 = feat

        def step(h, _):
            h = h * norm
            h = jax.ops.segment_sum(h[src], dst, num_segments=N)
            h = h * norm
            h = (1.0 - ALPHA) * h + ALPHA * feat_0
            return (h, None)
        h, _ = jax.lax.scan(step, feat, None, length=K)
        return h
    edge_index = jnp.stack([src, dst])
    h = jnp.maximum(_layernorm(x, axis=-1), 0.0)
    x = x + _L0_gnn_ref(h, src, dst)
    h = jnp.maximum(_layernorm(x, axis=-1), 0.0)
    x = x + _L1_gnn_ref(h, edge_index, L1_gnn_theta)
    h = jnp.maximum(_layernorm(x, axis=-1), 0.0)
    x = x + _L2_gnn_ref(h, L2_gnn_weight, L2_gnn_w_comp, L2_gnn_self_loop_weight, L2_gnn_A1_w, L2_gnn_A1_b, L2_gnn_A2_w, L2_gnn_A2_b, L2_gnn_rel_emb, src, dst, edge_type_86)
    h = jnp.maximum(_layernorm(x, axis=-1), 0.0)
    x = x + _L3_gnn_ref(h, src, dst)
    return x

_drawn_inputs = setup_inputs


def setup_inputs(seed=0):
    import zlib

    import numpy as np

    out = dict(_drawn_inputs(seed))
    spreads = {}
    factors = {}
    for name, (base, spread) in spreads.items():
        noise = np.random.default_rng([zlib.crc32(name.encode()), seed]).standard_normal(out[name].shape)
        drawn = base * np.exp(spread * noise) if base else spread * noise
        out[name] = jnp.asarray(drawn.astype(out[name].dtype))
    for name, factor in factors.items():
        out[name] = (out[name] * factor).astype(out[name].dtype)
    return out
```

```python
import concourse.bass as bass
from concourse import mybir
from contextlib import ExitStack

N = 100000
E = 25000
D = 32
NREL, NBAS = 86, 16
L1_STEPS, L3_STEPS = 4, 10
ALPHA = 0.1
EPS = 1e-5

P = 128
EC = -(-E // P)
EW = EC * D
NCOL = -(-N // P)
NPAD = P * NCOL
PADNODE = NPAD - 1
FAR = 1.0e6
MAGIC = 12582912.0
PAYLOAD = D + 4 + 4 + 1
LAST_ROWS = E - (P - 1) * EC

DCH = 39
DCHUNKS = 20
DROWS = DCH * DCHUNKS
TAIL_P, TAIL_C = 32, 5
assert P * DROWS + TAIL_P * TAIL_C == N
UNROLL = 4


def build(nc, x, src, dst, etype, theta, w_basis, w_comp, w_self, a1t, a1b, a2t, a2b, rel, out):
    f32, f16, i32 = mybir.dt.float32, mybir.dt.float16, mybir.dt.int32
    ALU, ACT, AX = mybir.AluOpType, mybir.ActivationFunctionType, mybir.AxisListType
    V, S, T, G = nc.vector, nc.scalar, nc.tensor, nc.gpsimd

    rec_dram = nc.dram_tensor("node_records", (NPAD, 4), f32, kind="Internal").ap()
    pay_dram = nc.dram_tensor("payload_by_src", (P * EC, PAYLOAD), f32, kind="Internal").ap()
    u1_dram = nc.dram_tensor("l1_rows", (P * EC, D), f32, kind="Internal").ap()
    x2_dram = nc.dram_tensor("x2_rows", (P * EC, D), f32, kind="Internal").ap()
    h2_dram = nc.dram_tensor("h2_rows", (P * EC, D), f32, kind="Internal").ap()
    u3_dram = nc.dram_tensor("l3_rows", (P * EC, D), f32, kind="Internal").ap()

    ctx = ExitStack()
    with ctx:
        def sb(name, cols, dt=f32, parts=P):
            return ctx.enter_context(nc.sbuf_tensor(name, [parts, cols], dt))

        def sem(name):
            return ctx.enter_context(nc.semaphore(name))

        pay = sb("pay", EC * PAYLOAD)
        mf = sb("mf", 2 * EW + 2 * D)
        xd_t = sb("xd", EW)
        xs_t = sb("xs", EW)
        z_t = sb("z", EW)
        out_t = sb("outs", EW)

        def rows(ap):
            return ap.rearrange("p (c f) -> p c f", f=D)

        PAY = pay[:].rearrange("p (c w) -> p c w", w=PAYLOAD)
        M_f, F_f = mf[:, 0:EW], mf[:, EW:2 * EW]
        M, F = rows(M_f), rows(F_f)
        XY = mf[:].rearrange("p (c w) -> p c w", w=2 * D)
        XD, XS, Z, OUT = rows(xd_t[:]), rows(xs_t[:]), rows(z_t[:]), rows(out_t[:])
        U_f = pay[:, 0:EW]
        U = rows(U_f)

        names = ["kn", "kp0", "kc0", "et", "tmp", "tmp2", "st1", "st2", "sq_in", "sq_out", "linear", "cont", "head",
                 "dis", "nsrc", "scalef", "score", "dcnt"]
        c = {n: sb(n, EC + 4) for n in names}
        c["kp1"], c["kc1"] = c["dis"], c["scalef"]

        def col(n):
            return c[n][:, 0:EC]

        icols = {n: sb("i_" + n, EC, i32) for n in ["src", "dst", "et", "rank", "srcX", "dstX", "outD", "outS"]}
        icols["srcS"] = icols["src"]
        icols["l1"] = icols["rank"]
        icols["l3"] = icols["et"]

        iota_c = sb("iota_c", NCOL, f16)
        iota_p = sb("iota_p", P, f16)
        iota_r = sb("iota_r", NREL)
        ident = sb("ident", P)
        ident16 = sb("ident16", P, f16)
        upper = sb("upper", P)
        lower = sb("lower", P)
        wcarry = sb("wcarry", P)
        theta_sb = sb("theta_sb", L1_STEPS + 1)
        theta_sum = sb("theta_sum", 1)
        w_sb = sb("w_sb", NBAS * D, f32, D)
        RC = NBAS + 3 * D
        rw_sb = sb("rw_sb", RC, f32, NREL)
        rxy_sb = sb("rxy_sb", RC, f32, 2 * D)
        b2_sb = sb("b2_sb", D, f32, NREL)
        small = sb("small", 4)
        last_row = sb("last_row", D)
        idle = sb("idle", 3)
        key_col = sb("key_col", 2)
        sums = sb("sums", 4)

        h16 = z_t[:].bitcast(f16)
        ONEHOT_W = P + NCOL

        def onehot(b, k):
            o = (2 * b + k) * ONEHOT_W
            return h16[:, o:o + P], h16[:, o + P:o + P + NCOL]

        z16 = h16[:, 4 * ONEHOT_W:4 * ONEHOT_W + 512]
        rs = [out_t[:, b * NCOL:(b + 1) * NCOL] for b in range(2)]
        ot = [out_t[:, 2 * NCOL + b * P:2 * NCOL + (b + 1) * P] for b in range(2)]
        start_tab = out_t[:, 2 * NCOL + 2 * P:3 * NCOL + 2 * P]
        scratch_b = out_t[:, 3 * NCOL + 2 * P:4 * NCOL + 2 * P]
        same = [out_t[:, 4 * NCOL + (2 + b) * P:4 * NCOL + (3 + b) * P] for b in range(2)]
        rec_sb = mf[:, 0:4 * NCOL]
        REC = rec_sb.rearrange("p (c w) -> p c w", w=4)
        cnt = mf[:, 4 * NCOL:5 * NCOL]
        inc = mf[:, 5 * NCOL:6 * NCOL]
        none = mf[:, 6 * NCOL:7 * NCOL]
        onesn = mf[:, 7 * NCOL:8 * NCOL]

        DW = DCH * D
        dx = [z_t[:, b * DW:(b + 1) * DW] for b in range(4)]
        dxc = [out_t[:, b * DW:(b + 1) * DW] for b in range(2)]
        dsq = [out_t[:, (2 + b) * DW:(3 + b) * DW] for b in range(2)]
        dst1 = [mf[:, b * DCH:(b + 1) * DCH] for b in range(2)]
        dst2 = [mf[:, (2 + b) * DCH:(3 + b) * DCH] for b in range(2)]
        dst3 = [mf[:, (4 + b) * DCH:(5 + b) * DCH] for b in range(2)]

        oh = [pay[:, b * NREL:(b + 1) * NREL] for b in range(2)]
        o1 = 2 * NREL
        xyt = [pay[0:2 * D, o1 + b * P:o1 + (b + 1) * P] for b in range(2)]
        o2 = o1 + 2 * P
        oht = [pay[0:NREL, o2 + b * P:o2 + (b + 1) * P] for b in range(2)]
        o3 = o2 + 2 * P
        cs = [pay[:, o3 + b * RC:o3 + (b + 1) * RC] for b in range(2)]
        o4 = o3 + 2 * RC
        prod = [pay[:, o4 + b * NBAS * D:o4 + (b + 1) * NBAS * D] for b in range(2)]
        o5 = o4 + 2 * NBAS * D
        o6 = o5 + 2 * D
        xyc = [pay[:, o6 + b * 2 * D:o6 + (b + 1) * 2 * D] for b in range(2)]
        sprod = [pay[:, o5 + b * D:o5 + (b + 1) * D] for b in range(2)]

        ps = [ctx.enter_context(nc.psum_tensor(f"ps{k}", [P, 1024], f32)) for k in range(4)]
        hist = [ps[0], ps[1]]
        R = ps[0]
        LK = [ps[1], ps[2]]
        KR = [ps[3][:, b * P:(b + 1) * P] for b in range(2)]
        TP = [ps[3][:, 512 + 64 * b:512 + 64 * (b + 1)].bitcast(f16) for b in range(2)]
        MISC = ps[3][:, 256:384]
        CAR = ps[3][:, 384:384 + D]
        PWm = [ps[0][:, 0:512], ps[0][:, 512:1024]]
        PSm = [ps[1][:, 0:RC], ps[1][:, 512:512 + RC]]
        XYTp = [ps[2][0:2 * D, 0:P], ps[2][0:2 * D, 512:512 + P]]
        OTp = [ps[2][0:NREL, P:2 * P], ps[2][0:NREL, 512 + P:512 + 2 * P]]

        SEMS = """padded edges_in weights_in pool_filled pool_consts dve_setup dve
            hist_free hist_built hist_done prefix_in prefix_out rec_ready rec_stored
            tile_free tile_built tile_turned tile_copied tile_counted tile_looked ranked
            xdst_in rec_src_in rec_dst_in payload_ready payload_out payload_in srows_idx xsrc_in
            root_in root_out
            dense_go tail_in dense_in0 dense_in1 dense_xc dense_sq dense_var dense_root dense_done dense_out dense_chain
            keys_in keys_out carry_in carry_out carry1_in carry1_out carry3_in carry3_out
            u1_ready u1_stored m1_in l1_chain s2_ready s2_stored s_final
            h2src_in x2dst_in l2_oh l2_xin l2_xy l2_tr l2_tc l2_mm l2_cs l2_prod l2_done gate_in gate_out
            turn1 turn3 u3_ready u3_stored m3_in l3_chain d_final outs_scattered outd_scattered""".split()
        s = {n: sem(n) for n in SEMS}

        block = ctx.enter_context(nc.Block())

        class Chain:
            def __init__(self, eng, sm, base=0, loop=None, per=0):
                self.eng, self.sm, self.n, self.base, self.loop, self.per = eng, sm, 0, base, loop, per

            def at(self, n):
                v = self.base + n
                return v if self.loop is None else self.loop * self.per + v

            def __call__(self, ins):
                self.n += 1
                ins.then_inc(self.sm, 1)
                self.eng.wait_ge(self.sm, self.at(self.n))

            def many(self, inss):
                for ins in inss:
                    self.n += 1
                    ins.then_inc(self.sm, 1)
                self.eng.wait_ge(self.sm, self.at(self.n))

        def bc(ap, n=D):
            return ap.unsqueeze(2).to_broadcast([ap.shape[0], ap.shape[1], n])

        def bf(ap, n=EC):
            return ap.unsqueeze(1).to_broadcast([ap.shape[0], n, ap.shape[1]])

        @block.sync
        def _(sp):
            for tile, arr in ((icols["src"], src), (icols["dst"], dst), (icols["et"], etype)):
                sp.wait_ge(s["padded"], 1)
                full = P - 16
                sp.dma_start(tile[0:full, :], arr[0:full * EC].rearrange("(p c) -> p c", c=EC)).then_inc(s["edges_in"], 16)
                sp.dma_start(tile[full:P - 1, :],
                             arr[full * EC:(P - 1) * EC].rearrange("(p c) -> p c", c=EC)).then_inc(s["edges_in"], 16)
                sp.dma_start(tile[P - 1:P, 0:LAST_ROWS],
                             arr[(P - 1) * EC:E].rearrange("(p c) -> p c", p=1)).then_inc(s["edges_in"], 16)
            sp.wait_ge(s["dve_setup"], 1)
            sp.dma_start(w_sb[:], w_basis.rearrange("i b o -> i (b o)")).then_inc(s["weights_in"], 16)
            sp.dma_start(rw_sb[:, 0:NBAS], w_comp).then_inc(s["weights_in"], 16)
            sp.dma_start(rw_sb[:, NBAS:NBAS + D], rel).then_inc(s["weights_in"], 16)
            sp.dma_start(rw_sb[:, NBAS + D:NBAS + 2 * D],
                         a1b.unsqueeze(0).to_broadcast([NREL, D])).then_inc(s["weights_in"], 16)
            sp.dma_start(b2_sb[:], a2b.unsqueeze(0).to_broadcast([NREL, D])).then_inc(s["weights_in"], 16)
            sp.dma_start(rxy_sb[0:D, NBAS + D:NBAS + 2 * D], a1t).then_inc(s["weights_in"], 16)
            sp.dma_start(rxy_sb[0:D, NBAS + 2 * D:RC], w_self).then_inc(s["weights_in"], 16)
            sp.dma_start(rxy_sb[D:2 * D, NBAS:NBAS + D], a2t).then_inc(s["weights_in"], 16)
            sp.dma_start(theta_sb[:], theta.unsqueeze(0).to_broadcast([P, L1_STEPS + 1])).then_inc(s["weights_in"], 16)
            sp.wait_ge(s["rec_ready"], 1)
            sp.dma_start(rec_dram.rearrange("(p c) w -> p (c w)", p=P), rec_sb).then_inc(s["rec_stored"], 16)
            sp.wait_ge(s["payload_out"], 16 * EC)
            sp.dma_start(pay[:], pay_dram.rearrange("(p c) w -> p (c w)", p=P)).then_inc(s["payload_in"], 16)
            with sp.Fori(0, L1_STEPS) as i:
                sp.wait_ge(s["u1_ready"], i + 1)
                sp.dma_start(u1_dram.rearrange("(p c) w -> p (c w)", p=P), U_f).then_inc(s["u1_stored"], 16)
            sp.wait_ge(s["s2_ready"], 1)
            sp.dma_start(x2_dram.rearrange("(p c) w -> p (c w)", p=P), xs_t[:]).then_inc(s["s2_stored"], 16)
            sp.dma_start(h2_dram.rearrange("(p c) w -> p (c w)", p=P), F_f).then_inc(s["s2_stored"], 16)
            with sp.Fori(0, L3_STEPS) as i:
                sp.wait_ge(s["u3_ready"], i + 1)
                sp.dma_start(u3_dram.rearrange("(p c) w -> p (c w)", p=P), U_f).then_inc(s["u3_stored"], 16)

        @block.gpsimd
        def _(pool):
            def gather(dest, table, idx, bound, sm):
                for k in range(EC):
                    G.indirect_dma_start(out=dest(k), out_offset=None, in_=table,
                                         in_offset=bass.IndirectOffsetOnAxis(ap=idx[:, k:k + 1], axis=0),
                                         bounds_check=bound, oob_is_err=False).then_inc(sm, 16)

            def scatter(table, source, idx, bound, sm):
                for k in range(EC):
                    G.indirect_dma_start(out=table, out_offset=bass.IndirectOffsetOnAxis(ap=idx[:, k:k + 1], axis=0),
                                         in_=source(k), in_offset=None,
                                         bounds_check=bound, oob_is_err=False).then_inc(sm, 16)

            for k in ("src", "dst"):
                G.memset(icols[k][:], PADNODE)
            G.memset(icols["et"][:], 0).then_inc(s["padded"], 1)
            G.iota(iota_c[:], [[1, NCOL]], base=0, channel_multiplier=0, allow_small_or_imprecise_dtypes=True)
            G.iota(iota_p[:], [[1, P]], base=0, channel_multiplier=0, allow_small_or_imprecise_dtypes=True)
            G.iota(iota_r[:], [[1, NREL]], base=0, channel_multiplier=0, allow_small_or_imprecise_dtypes=True)
            G.iota(col("linear"), [[1, EC]], base=0, channel_multiplier=EC, allow_small_or_imprecise_dtypes=True)
            G.memset(ident[:], 0.0)
            G.memset(upper[:], 1.0)
            G.memset(idle[:], 0.0).then_inc(s["turn1"], 1)
            G.memset(ident16[:], 0.0).then_inc(s["turn3"], 1)
            G.memset(lower[:], 1.0).then_inc(s["pool_filled"], 1)
            pool.wait_ge(s["pool_filled"], 1)
            for t in (ident, ident16):
                G.affine_select(out=t[:], in_=t[:], compare_op=ALU.not_equal, fill=1.0, base=0,
                                pattern=[[-1, P]], channel_multiplier=1)
            G.affine_select(out=upper[:], in_=upper[:], compare_op=ALU.is_gt, fill=0.0, base=0,
                            pattern=[[1, P]], channel_multiplier=-1)
            G.affine_select(out=lower[:], in_=lower[:], compare_op=ALU.is_gt, fill=0.0, base=0,
                            pattern=[[-1, P]], channel_multiplier=1).then_inc(s["pool_consts"], 1)
            pool.wait_ge(s["edges_in"], 16 * 9)
            pool.wait_ge(s["dve"], 1)
            gather(lambda k: XD[:, k, :], x, icols["dst"], N - 1, s["xdst_in"])
            pool.wait_ge(s["rec_stored"], 16)
            gather(lambda k: PAY[:, k, D:D + 4], rec_dram, icols["src"], NPAD - 1, s["rec_src_in"])
            gather(lambda k: PAY[:, k, D + 4:D + 8], rec_dram, icols["dst"], NPAD - 1, s["rec_dst_in"])
            pool.wait_ge(s["payload_ready"], 1)
            scatter(pay_dram, lambda k: PAY[:, k, :], icols["rank"], P * EC - 1, s["payload_out"])
            pool.wait_ge(s["srows_idx"], 1)
            gather(lambda k: XS[:, k, :], x, icols["srcS"], N - 1, s["xsrc_in"])
            with pool.Fori(0, L1_STEPS) as i:
                pool.wait_ge(s["u1_stored"], 16 * i + 16)
                pool.wait_ge(s["turn1"], i + 1)
                G.tensor_tensor(idle[:, 0:1], idle[:, 1:2], idle[:, 1:2], ALU.add).then_inc(s["turn1"], 1)
                gather(lambda k: M[:, k, :], u1_dram, icols["l1"], P * EC - 1, s["m1_in"])
            pool.wait_ge(s["s2_stored"], 32)
            gather(lambda k: XD[:, k, :], x2_dram, icols["dstX"], P * EC - 1, s["x2dst_in"])
            pool.wait_ge(s["s_final"], 1)
            gather(lambda k: XY[:, k, 0:D], h2_dram, icols["srcX"], P * EC - 1, s["h2src_in"])
            pool.wait_ge(s["dense_out"], 16 * (DCHUNKS + 1))
            scatter(out, lambda k: OUT[:, k, :], icols["outS"], N - 1, s["outs_scattered"])
            with pool.Fori(0, L3_STEPS) as i:
                pool.wait_ge(s["u3_stored"], 16 * i + 16)
                pool.wait_ge(s["turn3"], i + 1)
                G.tensor_tensor(idle[:, 2:3], idle[:, 1:2], idle[:, 1:2], ALU.add).then_inc(s["turn3"], 1)
                gather(lambda k: M[:, k, :], u3_dram, icols["l3"], P * EC - 1, s["m3_in"])
            pool.wait_ge(s["d_final"], 1)
            scatter(out, lambda k: XD[:, k, :], icols["outD"], N - 1, s["outd_scattered"])
            pool.wait_ge(s["outs_scattered"], 16 * EC)
            pool.wait_ge(s["outd_scattered"], 16 * EC)

        @block.vector
        def _(dve):
            link = Chain(dve, s["dve"])

            def tt(o, a, b, op):
                return V.tensor_tensor(o, a, b, op)

            def ts(o, a, s1, s2, op0, op1=None):
                return V.tensor_scalar(o, a, s1, s2, op0, op1) if op1 is not None else V.tensor_scalar(o, a, s1, None, op0)

            roots = [0]

            def root(o, a):
                roots[0] += 1
                V.tensor_copy(col("sq_in"), a).then_inc(s["root_in"], 1)
                dve.wait_ge(s["root_out"], roots[0])
                link(V.reciprocal(o, col("sq_out")))

            def layernorm(xin, hout, tmp, chain=link):
                chain(V.tensor_reduce(col("st1"), xin, AX.X, ALU.add))
                chain(ts(col("st1"), col("st1"), 1.0 / D, None, ALU.mult))
                chain(tt(tmp, xin, bc(col("st1")), ALU.subtract))
                chain(tt(hout, tmp, tmp, ALU.mult))
                chain(V.tensor_reduce(col("st2"), hout, AX.X, ALU.add))
                chain(ts(col("st2"), col("st2"), 1.0 / D, EPS, ALU.mult, ALU.add))
                root(col("st1"), col("st2"))
                chain(V.scalar_tensor_tensor(out=hout, in0=tmp, scalar=0.0, in1=bc(col("st1")), op0=ALU.max, op1=ALU.mult))

            link(V.memset(xd_t[:], 0.0))
            link(V.memset(xs_t[:], 0.0))
            link(V.memset(z16, 0.0))
            link(V.memset(onesn, 1.0))
            for n in ("kp0", "kc0", "kn", "et"):
                link(V.memset(c[n][:], 0.0))
            link(V.memset(XY[:, EC, :], 0.0))
            link(V.memset(rxy_sb[:], 0.0))
            link(V.memset(rw_sb[:, NBAS + 2 * D:RC], 0.0))
            V.memset(small[:], 0.0).then_inc(s["dve_setup"], 1)
            dve.wait_ge(s["edges_in"], 16 * 9)
            dve.wait_ge(s["pool_consts"], 1)
            for k, name in enumerate(("src", "dst")):
                kp, kc = col(f"kp{k}"), col(f"kc{k}")
                link(V.tensor_copy(col("kn"), icols[name][:]))
                link(ts(kp, col("kn"), 1.0 / NCOL, 0.5 / NCOL - 0.5, ALU.mult, ALU.add))
                link(ts(kp, kp, MAGIC, None, ALU.add))
                link(ts(kp, kp, MAGIC, None, ALU.subtract))
                link(V.scalar_tensor_tensor(out=kc, in0=kp, scalar=-float(NCOL), in1=col("kn"), op0=ALU.mult, op1=ALU.add))
            link(V.tensor_copy(col("kn"), icols["src"][:]))
            link(V.tensor_copy(col("et"), icols["et"][:]))
            hist_keys = [("kp0", "kc0"), ("kp1", "kc1")]
            with dve.Fori(0, EC // 2) as i:
                for b in range(2):
                    t = 2 * i + b
                    dve.wait_ge(s["hist_free"], t + 1)
                    for k, (kp, kc) in enumerate(hist_keys):
                        op_, oc_ = onehot(b, k)
                        V.tensor_scalar(op_, iota_p[:], c[kp][:, bass.ds(t, 1)], None, ALU.is_equal)
                        last = V.tensor_scalar(oc_, iota_c[:], c[kc][:, bass.ds(t, 1)], None, ALU.is_equal)
                    last.then_inc(s["hist_built"], 1)
            dve.wait_ge(s["hist_done"], 1)
            for k in range(2):
                link(V.tensor_copy(cnt, hist[k][:, 0:NCOL]))
                link(V.tensor_tensor_scan(inc, onesn, cnt, 0.0, ALU.mult, ALU.add))
                V.tensor_copy(small[:, 0:1], inc[:, NCOL - 1:NCOL]).then_inc(s["prefix_in"], 1)
                dve.wait_ge(s["prefix_out"], k + 1)
                link(V.tensor_copy(small[:, 1:2], MISC[:, 0:1]))
                link(ts(inc, inc, small[:, 1:2], None, ALU.add))
                if k == 0:
                    link(tt(start_tab, inc, cnt, ALU.subtract))
                link(ts(none, cnt, 0.0, FAR, ALU.is_equal, ALU.mult))
                link(V.scalar_tensor_tensor(out=REC[:, :, 2 * k], in0=inc, scalar=-1.0, in1=none, op0=ALU.add, op1=ALU.add))
                link(V.tensor_copy(REC[:, :, 2 * k + 1], cnt))
            V.memset(small[:, 2:3], 0.0).then_inc(s["rec_ready"], 1)
            def build_tile(t, b):
                dve.wait_ge(s["tile_free"], t + 1)
                op_, oc_ = onehot(b, 0)
                V.tensor_scalar(op_, iota_p[:], c["kp0"][:, bass.ds(t, 1)], None, ALU.is_equal)
                V.tensor_copy(key_col[:, b:b + 1], c["kn"][:, bass.ds(t, 1)])
                V.tensor_scalar(oc_, iota_c[:], c["kc0"][:, bass.ds(t, 1)], None, ALU.is_equal).then_inc(s["tile_built"], 1)

            build_tile(0, 0)
            with dve.Fori(0, EC // 2) as i:
                for b in range(2):
                    t = 2 * i + b
                    build_tile(t + 1, 1 - b)
                    dve.wait_ge(s["tile_counted"], t + 1)
                    dve.wait_ge(s["tile_built"], t + 1)
                    V.tensor_tensor_reduce(out=scratch_b, in0=LK[b][:, 0:NCOL], in1=onehot(b, 0)[1], scale=1.0, scalar=0.0,
                                           op0=ALU.mult, op1=ALU.add, accum_out=sums[:, b:b + 1])
                    V.scalar_tensor_tensor(out=same[b], in0=KR[b], scalar=c["kn"][:, bass.ds(t, 1)], in1=lower[:],
                                           op0=ALU.is_equal, op1=ALU.mult,
                                           accum_out=sums[:, 2 + b:3 + b]).then_inc(s["tile_looked"], 1)
                    dve.wait_ge(s["tile_looked"], t + 1)
                    tt(c["score"][:, bass.ds(t, 1)], sums[:, b:b + 1], sums[:, 2 + b:3 + b], ALU.add).then_inc(s["ranked"], 1)
            dve.wait_ge(s["ranked"], EC)
            link(V.tensor_copy(icols["rank"][:], col("score")))
            dve.wait_ge(s["xdst_in"], 16 * EC)
            layernorm(XD, OUT, Z)
            dve.wait_ge(s["rec_src_in"], 16 * EC)
            dve.wait_ge(s["rec_dst_in"], 16 * EC)
            link(ts(col("tmp"), PAY[:, :, D + 5], 1.0, None, ALU.add))
            root(col("nsrc"), col("tmp"))
            link(tt(PAY[:, :, 0:D], OUT, bc(col("nsrc")), ALU.mult))
            link(V.tensor_copy(PAY[:, :, PAYLOAD - 1], col("kn")))
            link(V.tensor_copy(icols["srcX"][:], PAY[:, :, D]))
            link(V.tensor_copy(icols["l3"][:], PAY[:, :, D + 2]))
            link(V.tensor_copy(icols["dstX"][:], PAY[:, :, D + 4]))
            link(tt(col("tmp"), PAY[:, :, D + 6], col("linear"), ALU.not_equal))
            link(V.tensor_copy(col("score"), icols["dst"][:]))
            link(V.scalar_tensor_tensor(out=icols["outD"][:], in0=col("tmp"), scalar=FAR, in1=col("score"), op0=ALU.mult, op1=ALU.add))
            link(V.tensor_copy(col("dcnt"), PAY[:, :, D + 7]))
            V.memset(small[:, 3:4], 0.0).then_inc(s["payload_ready"], 1)
            link(tt(XD, XD, OUT, ALU.add))
            dve.wait_ge(s["weights_in"], 16 * 9)
            link(V.tensor_reduce(theta_sum[:], theta_sb[:], AX.X, ALU.add))
            link(tt(rw_sb[:, NBAS:NBAS + D], rw_sb[:, NBAS:NBAS + D], b2_sb[:], ALU.add))
            layernorm(XD, OUT, Z)
            link(V.scalar_tensor_tensor(out=XD, in0=OUT, scalar=theta_sum[:], in1=XD, op0=ALU.mult, op1=ALU.add))
            def dense_pair(slots, pn, cn, chain, number):
                nb = len(slots)
                w = cn * D
                X = [dx[sl][0:pn, 0:w] for sl in slots]
                for l in range(3):
                    for b in range(nb):
                        X3 = X[b].rearrange("p (c f) -> p c f", f=D)
                        chain(V.tensor_reduce(dst1[b][0:pn, 0:cn], X3, AX.X, ALU.add))
                        chain(ts(dst1[b][0:pn, 0:cn], dst1[b][0:pn, 0:cn], 1.0 / D, None, ALU.mult))
                        tt(rows(dxc[b][0:pn, 0:w]), X3, bc(dst1[b][0:pn, 0:cn]), ALU.subtract).then_inc(s["dense_xc"], 1)
                    for b in range(nb):
                        dve.wait_ge(s["dense_sq"], number(l, b))
                        chain(V.tensor_reduce(dst2[b][0:pn, 0:cn], rows(dsq[b][0:pn, 0:w]), AX.X, ALU.add))
                        ts(dst2[b][0:pn, 0:cn], dst2[b][0:pn, 0:cn], 1.0 / D, EPS, ALU.mult, ALU.add).then_inc(s["dense_var"], 1)
                    for b in range(nb):
                        X3 = X[b].rearrange("p (c f) -> p c f", f=D)
                        dve.wait_ge(s["dense_root"], number(l, b))
                        chain(V.reciprocal(dst1[b][0:pn, 0:cn], dst3[b][0:pn, 0:cn]))
                        if l == 1:
                            chain(ts(dst1[b][0:pn, 0:cn], dst1[b][0:pn, 0:cn], theta_sum[0:pn], None, ALU.mult))
                        if l == 2:
                            chain(ts(dst1[b][0:pn, 0:cn], dst1[b][0:pn, 0:cn], ALPHA, None, ALU.mult))
                        dve.wait_ge(s["dense_xc"], number(l, b))
                        chain(V.scalar_tensor_tensor(out=rows(dxc[b][0:pn, 0:w]), in0=rows(dxc[b][0:pn, 0:w]), scalar=0.0,
                                                     in1=bc(dst1[b][0:pn, 0:cn]), op0=ALU.max, op1=ALU.mult))
                        if l < 2:
                            chain(tt(X[b], X[b], dxc[b][0:pn, 0:w], ALU.add))
                        else:
                            tt(X[b], X[b], dxc[b][0:pn, 0:w], ALU.add).then_inc(s["dense_done"], 1)

            tail_chain = Chain(dve, s["dense_chain"])
            V.memset(small[:, 2:3], 0.0).then_inc(s["dense_go"], 1)
            dve.wait_ge(s["tail_in"], 16)
            dense_pair([0], TAIL_P, TAIL_C, tail_chain, lambda l, b: l + 1)
            dve.wait_ge(s["dense_done"], 1)
            PER = 2 * 2 * (3 * 5 + 2 + 2)
            with dve.Fori(0, DCHUNKS // UNROLL) as i:
                ch = Chain(dve, s["dense_chain"], tail_chain.n, i, PER)
                for h in range(2):
                    dve.wait_ge(s[f"dense_in{h}"], 32 * i + 32)
                    dense_pair([2 * h, 2 * h + 1], P, DCH, ch,
                               lambda l, b: 12 * i + (3 + 6 * h + 2 * l + b + 1))
                assert ch.n == PER, ch.n
            dve.wait_ge(s["payload_in"], 16)
            SRC, SEND_S, CNT_S, CNT_D = PAY[:, :, PAYLOAD - 1], PAY[:, :, D], PAY[:, :, D + 1], PAY[:, :, D + 3]
            V.tensor_copy(icols["srcS"][:], SRC).then_inc(s["srows_idx"], 1)
            link(V.tensor_copy(icols["l1"][:], PAY[:, :, D + 4]))
            link(tt(col("tmp"), SEND_S, col("linear"), ALU.not_equal))
            link(ts(col("tmp2"), CNT_D, 0.0, None, ALU.is_gt))
            link(tt(col("tmp"), col("tmp"), col("tmp2"), ALU.max))
            link(V.scalar_tensor_tensor(out=icols["outS"][:], in0=col("tmp"), scalar=FAR, in1=SRC, op0=ALU.mult, op1=ALU.add))
            link(V.tensor_copy(col("kn"), SRC))
            link(ts(col("scalef"), CNT_S, 1.0, None, ALU.add))
            root(col("nsrc"), col("scalef"))
            link(V.tensor_copy(col("scalef"), CNT_S))
            root(col("dis"), col("scalef"))

            seg = [0]

            def segments():
                seg[0] += 1
                kn = col("kn")
                link(V.memset(c["cont"][:], 0.0))
                link(tt(c["cont"][:, 1:EC], kn[:, 1:EC], kn[:, 0:EC - 1], ALU.is_equal))
                link(ts(col("head"), kn, kn[:, 0:1], None, ALU.is_equal))
                V.tensor_copy(small[:, 0:1], kn[:, 0:1]).then_inc(s["keys_in"], 1)
                dve.wait_ge(s["keys_out"], seg[0])
                link(V.scalar_tensor_tensor(out=wcarry[:], in0=MISC, scalar=kn[:, EC - 1:EC], in1=upper[:],
                                            op0=ALU.is_equal, op1=ALU.mult))

            def segment_sums(chain, m, ins, outs, number, tmp):
                chain.many([V.tensor_tensor_scan(Z[:, :, f], col("cont"), m[:, :, f], 0.0, ALU.mult, ALU.add)
                            for f in range(D)])
                V.tensor_copy(last_row[:], Z[:, EC - 1, :]).then_inc(ins, 1)
                dve.wait_ge(outs, number)
                chain(tt(tmp, bf(CAR), bc(col("head")), ALU.mult))
                chain(tt(Z, Z, tmp, ALU.add))

            segments()
            dve.wait_ge(s["dense_out"], 16 * (DCHUNKS + 1))
            segment_sums(link, PAY[:, :, 0:D], s["carry_in"], s["carry_out"], 1, OUT)
            dve.wait_ge(s["xsrc_in"], 16 * EC)
            layernorm(XS, F, OUT)
            link(tt(OUT, F, bc(col("nsrc")), ALU.mult))
            link(tt(Z, Z, OUT, ALU.add))
            link(tt(Z, Z, bc(col("nsrc")), ALU.mult))
            link(tt(XS, XS, Z, ALU.add))
            layernorm(XS, F, Z)
            link(V.memset(M_f, 0.0))
            link(tt(U, F, bc(col("dis")), ALU.mult))
            V.tensor_copy(small[:, 2:3], small[:, 3:4]).then_inc(s["u1_ready"], 1)
            link(ts(OUT, F, theta_sb[:, 0:1], None, ALU.mult))
            PER1 = D + 2 + 4
            with dve.Fori(0, L1_STEPS) as i:
                ch = Chain(dve, s["l1_chain"], 0, i, PER1)
                dve.wait_ge(s["m1_in"], 16 * EC * i + 16 * EC)
                segment_sums(ch, M, s["carry1_in"], s["carry1_out"], i + 1, U)
                ch(tt(Z, Z, bc(col("dis")), ALU.mult))
                ch(tt(F, F, Z, ALU.subtract))
                ch(tt(U, F, bc(col("dis")), ALU.mult))
                V.tensor_copy(small[:, 2:3], small[:, 3:4]).then_inc(s["u1_ready"], 1)
                ch(V.scalar_tensor_tensor(out=OUT, in0=F, scalar=theta_sb[:, bass.ds(i + 1, 1)], in1=OUT, op0=ALU.mult, op1=ALU.add))
                assert ch.n == PER1
            link(tt(XS, XS, OUT, ALU.add))
            layernorm(XS, F, Z)
            V.tensor_copy(small[:, 2:3], small[:, 3:4]).then_inc(s["s2_ready"], 1)
            V.scalar_tensor_tensor(out=OUT, in0=F, scalar=ALPHA, in1=XS, op0=ALU.mult, op1=ALU.add).then_inc(s["s_final"], 1)
            link(V.tensor_copy(col("kn"), icols["dst"][:]))
            segments()
            root(col("dis"), col("dcnt"))
            dve.wait_ge(s["x2dst_in"], 16 * EC)
            dve.wait_ge(s["h2src_in"], 16 * EC)
            dve.wait_ge(s["s2_stored"], 32)
            layernorm(XD, XY[:, 0:EC, D:2 * D], Z)

            def build_types(t, b):
                V.tensor_scalar(oh[b], iota_r[:], c["et"][:, bass.ds(t, 1)], None, ALU.is_equal).then_inc(s["l2_oh"], 1)

            CUR = XS
            V.memset(small[:, 2:3], 0.0).then_inc(s["l2_xin"], 1)
            V.memset(sums[:, 3:4], 0.0).then_inc(s["l2_prod"], 1)
            build_types(0, 0)
            with dve.Fori(0, EC // 2) as i:
                for b in range(2):
                    t = 2 * i + b
                    dve.wait_ge(s["l2_tr"], t + 1)
                    build_types(t + 1, 1 - b)
                    dve.wait_ge(s["l2_cs"], t + 1)
                    V.tensor_tensor_reduce(out=sprod[b], in0=cs[b][:, NBAS:NBAS + D], in1=cs[b][:, NBAS + D:NBAS + 2 * D],
                                           scale=1.0, scalar=0.0, op0=ALU.mult, op1=ALU.add,
                                           accum_out=sums[:, b:b + 1])
                    tt(prod[b].rearrange("p (b o) -> p b o", o=D), PWm[b].rearrange("p (b o) -> p b o", o=D),
                       bc(cs[b][:, 0:NBAS]), ALU.mult).then_inc(s["l2_prod"], 1)
                    dve.wait_ge(s["l2_prod"], t + 2)
                    V.tensor_copy(c["score"][:, bass.ds(t, 1)], sums[:, b:b + 1])
                    V.tensor_reduce(Z[:, bass.ds(t, 1), :], prod[b].rearrange("p (b o) -> p o b", o=D),
                                    AX.X, ALU.add).then_inc(s["l2_done"], 1)
            dve.wait_ge(s["l2_done"], EC)
            ts(col("score"), col("score"), float(D) ** -0.5, 0.0, ALU.mult, ALU.max).then_inc(s["gate_in"], 1)
            dve.wait_ge(s["gate_out"], 1)
            link(tt(M, Z, bc(col("sq_out")), ALU.mult))
            segment_sums(link, M, s["carry_in"], s["carry_out"], 2, F)
            dve.wait_ge(s["l2_cs"], EC)
            link(tt(Z, Z, CUR, ALU.add))
            link(V.scalar_tensor_tensor(out=XD, in0=Z, scalar=0.0, in1=XD, op0=ALU.max, op1=ALU.add))
            layernorm(XD, F, Z)
            link(tt(U, F, bc(col("dis")), ALU.mult))
            link(V.memset(M_f, 0.0))
            V.tensor_copy(small[:, 2:3], small[:, 3:4]).then_inc(s["u3_ready"], 1)
            link(ts(col("scalef"), col("dis"), 1.0 - ALPHA, None, ALU.mult))
            link(ts(F, F, ALPHA, None, ALU.mult))
            PER3 = D + 2 + 3
            with dve.Fori(0, L3_STEPS) as i:
                ch = Chain(dve, s["l3_chain"], 0, i, PER3)
                dve.wait_ge(s["m3_in"], 16 * EC * i + 16 * EC)
                segment_sums(ch, M, s["carry3_in"], s["carry3_out"], i + 1, U)
                ch(tt(Z, Z, bc(col("scalef")), ALU.mult))
                ch(tt(Z, Z, F, ALU.add))
                ch(tt(U, Z, bc(col("dis")), ALU.mult))
                V.tensor_copy(small[:, 2:3], small[:, 3:4]).then_inc(s["u3_ready"], 1)
                assert ch.n == PER3
            tt(XD, XD, Z, ALU.add).then_inc(s["d_final"], 1)

        @block.scalar
        def _(act):
            roots = [0]

            def root(n):
                for _ in range(n):
                    roots[0] += 1
                    act.wait_ge(s["root_in"], roots[0])
                    S.activation(col("sq_out"), col("sq_in"), ACT.Sqrt).then_inc(s["root_out"], 1)

            with act.Fori(0, EC // 2) as i:
                for b in range(2):
                    t = 2 * i + b
                    act.wait_ge(s["tile_turned"], t + 1)
                    S.copy(ot[b], TP[b])
                    act.wait_ge(s["tile_free"], t + 2)
                    S.copy(rs[b], R[:, 0:NCOL]).then_inc(s["tile_copied"], 1)
            root(3)
            xt = x[P * DROWS:N].rearrange("(p c) f -> p (c f)", p=TAIL_P)
            outt = out[P * DROWS:N].rearrange("(p c) f -> p (c f)", p=TAIL_P)
            xflat = x[0:P * DROWS].rearrange("(p q) f -> p (q f)", p=P)
            oflat = out[0:P * DROWS].rearrange("(p q) f -> p (q f)", p=P)

            def dense_act(nb, pn, cn, number):
                w = cn * D
                for l in range(3):
                    for b in range(nb):
                        act.wait_ge(s["dense_xc"], number(l, b))
                        S.activation(dsq[b][0:pn, 0:w], dxc[b][0:pn, 0:w], ACT.Square).then_inc(s["dense_sq"], 1)
                    for b in range(nb):
                        act.wait_ge(s["dense_var"], number(l, b))
                        S.activation(dst3[b][0:pn, 0:cn], dst2[b][0:pn, 0:cn], ACT.Sqrt).then_inc(s["dense_root"], 1)

            act.wait_ge(s["dense_go"], 1)
            act.dma_start(dx[0][0:TAIL_P, 0:TAIL_C * D], xt).then_inc(s["tail_in"], 16)
            dense_act(1, TAIL_P, TAIL_C, lambda l, b: l + 1)
            act.wait_ge(s["dense_done"], 1)
            act.dma_start(outt, dx[0][0:TAIL_P, 0:TAIL_C * D]).then_inc(s["dense_out"], 16)
            act.wait_ge(s["dense_out"], 16)
            for b in range(2):
                act.dma_start(dx[b], xflat[:, b * DW:(b + 1) * DW]).then_inc(s["dense_in0"], 16)

            def dense_turn(i, last):
                for h in range(2):
                    if not (last and h == 1):
                        act.wait_ge(s["dense_out"], 64 * i + 16 * (1 + 2 * h))
                        for b in range(2):
                            act.dma_start(dx[(2 * h + 2 + b) % 4],
                                          xflat[:, bass.ds(UNROLL * DW * i + DW * (2 * h + 2 + b), DW)]
                                          ).then_inc(s[f"dense_in{1 - h}"], 16)
                    dense_act(2, P, DCH, lambda l, b: 12 * i + (3 + 6 * h + 2 * l + b + 1))
                    for b in range(2):
                        act.wait_ge(s["dense_done"], 4 * i + (1 + 2 * h + b + 1))
                        act.dma_start(oflat[:, bass.ds(UNROLL * DW * i + DW * (2 * h + b), DW)],
                                      dx[2 * h + b]).then_inc(s["dense_out"], 16)

            with act.Fori(0, DCHUNKS // UNROLL - 1) as i:
                dense_turn(i, False)
            dense_turn(DCHUNKS // UNROLL - 1, True)
            root(2)
            root(1)
            root(1)
            root(1)
            root(1)
            root(1)
            act.wait_ge(s["h2src_in"], 16 * EC)
            act.wait_ge(s["l2_xin"], 1)
            S.copy(xyc[0], XY[:, 0, :]).then_inc(s["l2_xy"], 1)
            with act.Fori(0, EC // 2) as i:
                for b in range(2):
                    t = 2 * i + b
                    act.wait_ge(s["l2_tr"], t + 1)
                    S.copy(xyc[1 - b].unsqueeze(1), XY[:, bass.ds(t + 1, 1), :]).then_inc(s["l2_xy"], 1)
                    S.copy(xyt[b], XYTp[b])
                    S.copy(oht[b], OTp[b]).then_inc(s["l2_tc"], 1)
                    act.wait_ge(s["l2_mm"], t + 1)
                    act.wait_ge(s["l2_prod"], t)
                    S.copy(XS[:, bass.ds(t, 1), :], PSm[b][:, RC - D:RC].unsqueeze(1))
                    S.copy(cs[b][:, 0:RC - D], PSm[b][:, 0:RC - D]).then_inc(s["l2_cs"], 1)
            act.wait_ge(s["gate_in"], 1)
            S.activation(col("sq_out"), col("score"), ACT.Tanh).then_inc(s["gate_out"], 1)
            root(1)

        @block.tensor
        def _(pe):
            H0 = 512
            halves = ((0, H0), (H0, NCOL))

            def zeros(start, k):
                for a, b in halves:
                    ins = T.matmul(hist[k][:, a:b], z16[:, 0:P], z16[:, 0:b - a], start=start, stop=not start)
                return ins

            pe.wait_ge(s["pool_consts"], 1)
            pe.wait_ge(s["dve_setup"], 1)
            zeros(True, 0)
            zeros(True, 1).then_inc(s["hist_free"], 2)
            with pe.Fori(0, EC // 2) as i:
                for b in range(2):
                    pe.wait_ge(s["hist_built"], 2 * i + (b + 1))
                    for k in range(2):
                        op_, oc_ = onehot(b, k)
                        for lo, hi in halves:
                            ins = T.matmul(hist[k][:, lo:hi], op_, oc_[:, lo:hi], start=False, stop=False)
                    ins.then_inc(s["hist_free"], 1)
            zeros(False, 0)
            zeros(False, 1).then_inc(s["hist_done"], 1)
            for k in range(2):
                pe.wait_ge(s["prefix_in"], k + 1)
                T.matmul(MISC[:, 0:1], upper[:], small[:, 0:1], start=True, stop=True).then_inc(s["prefix_out"], 1)
            pe.wait_ge(s["rec_ready"], 1)
            for lo, hi in halves:
                ins = T.matmul(R[:, lo:hi], ident[:], start_tab[:, lo:hi], start=True, stop=True, skip_group_check=True)
            ins.then_inc(s["tile_free"], 2)

            def turn(t, b):
                pe.wait_ge(s["tile_built"], t + 1)
                T.transpose(TP[b], onehot(b, 0)[0], ident16[:])
                T.matmul(KR[b], key_col[:, b:b + 1].to_broadcast([P, P]), ident[:], start=True, stop=True).then_inc(s["tile_turned"], 1)

            turn(0, 0)
            with pe.Fori(0, EC // 2) as i:
                for b in range(2):
                    t = 2 * i + b
                    op_, oc_ = onehot(b, 0)
                    pe.wait_ge(s["tile_copied"], t + 1)
                    for lo, hi in halves:
                        ins = T.matmul(R[:, lo:hi], op_, oc_[:, lo:hi], start=False, stop=True, skip_group_check=True)
                    ins.then_inc(s["tile_free"], 1)
                    pe.wait_ge(s["tile_looked"], t)
                    turn(t + 1, 1 - b)
                    for lo, hi in halves:
                        ins = T.matmul(LK[b][:, lo:hi], ot[b], rs[b][:, lo:hi], start=True, stop=True)
                    ins.then_inc(s["tile_counted"], 1)

            def first_keys(k):
                pe.wait_ge(s["keys_in"], k)
                T.matmul(MISC, small[:, 0:1].to_broadcast([P, P]), ident[:], start=True, stop=True).then_inc(s["keys_out"], 1)

            def carry(ins, outs, number):
                pe.wait_ge(ins, number)
                T.matmul(CAR, wcarry[:], last_row[:], start=True, stop=True).then_inc(outs, 1)

            first_keys(1)
            carry(s["carry_in"], s["carry_out"], 1)
            with pe.Fori(0, L1_STEPS) as i:
                carry(s["carry1_in"], s["carry1_out"], i + 1)
            first_keys(2)
            pe.wait_ge(s["h2src_in"], 16 * EC)

            def l2_turn(t, b):
                pe.wait_ge(s["l2_oh"], t + 1)
                pe.wait_ge(s["l2_xy"], t + 1)
                T.transpose(OTp[b], oh[b], ident[:])
                T.transpose(XYTp[b], xyc[b], ident[:]).then_inc(s["l2_tr"], 1)

            l2_turn(0, 0)
            with pe.Fori(0, EC // 2) as i:
                for b in range(2):
                    t = 2 * i + b
                    l2_turn(t + 1, 1 - b)
                    pe.wait_ge(s["l2_tc"], t + 1)
                    pe.wait_ge(s["l2_prod"], t)
                    T.matmul(PWm[b], xyt[b][0:D, :], w_sb[:], start=True, stop=True)
                    T.matmul(PSm[b], oht[b], rw_sb[:], start=True, stop=False)
                    T.matmul(PSm[b], xyt[b], rxy_sb[:], start=False, stop=True).then_inc(s["l2_mm"], 1)
            carry(s["carry_in"], s["carry_out"], 2)
            with pe.Fori(0, L3_STEPS) as i:
                carry(s["carry3_in"], s["carry3_out"], i + 1)


def kernel(x, src, dst, edge_type_86, L1_gnn_theta, L2_gnn_weight, L2_gnn_w_comp, L2_gnn_self_loop_weight,
           L2_gnn_A1_w, L2_gnn_A1_b, L2_gnn_A2_w, L2_gnn_A2_b, L2_gnn_rel_emb):
    import numpy as np
    import concourse.bacc as bacc
    from concourse.bass_utils import run_bass_kernel_spmd

    nc = bacc.Bacc("TRN2", target_bir_lowering=False, num_devices=1)
    given = {
        "x": x, "src": src, "dst": dst, "etype": edge_type_86, "theta": L1_gnn_theta,
        "w_basis": np.transpose(np.asarray(L2_gnn_weight), (1, 0, 2)), "w_comp": L2_gnn_w_comp,
        "w_self": L2_gnn_self_loop_weight, "a1t": np.transpose(np.asarray(L2_gnn_A1_w)), "a1b": L2_gnn_A1_b,
        "a2t": np.transpose(np.asarray(L2_gnn_A2_w)), "a2b": L2_gnn_A2_b, "rel": L2_gnn_rel_emb,
    }
    arrays, args = {}, {}
    for name, a in given.items():
        a = np.ascontiguousarray(a)
        arrays["in_" + name] = a
        args[name] = nc.dram_tensor("in_" + name, a.shape, mybir.dt.from_np(a.dtype), kind="ExternalInput").ap()
    args["out"] = nc.dram_tensor("out_0", (N, D), mybir.dt.float32, kind="ExternalOutput").ap()
    build(nc, **args)
    r = run_bass_kernel_spmd(nc, [arrays], core_ids=[0])
    return r.results[0]["out_0"]
```

```python
import concourse.bass as bass
from concourse import mybir
from contextlib import ExitStack

N = 100000
E = 25000
D = 32
NREL, NBAS = 86, 16
L1_STEPS, L3_STEPS = 4, 10
ALPHA = 0.1
EPS = 1e-5

P = 128
EC = -(-E // P)
EW = EC * D
NCOL = -(-N // P)
NPAD = P * NCOL
PADNODE = NPAD - 1
FAR = 1.0e6
MAGIC = 12582912.0
PAYLOAD = D + 4 + 4 + 1
W = 64
GW = 60
SPLIT = 32768.0
OWNW = D + 2
LAST_ROWS = E - (P - 1) * EC

DCH = 39
DCHUNKS = 20
DROWS = DCH * DCHUNKS
TAIL_P, TAIL_C = 32, 5
assert P * DROWS + TAIL_P * TAIL_C == N
UNROLL = 4


def build(nc, x, src, dst, etype, theta, w_basis, w_comp, w_self, a1t, a1b, a2t, a2b, rel, out):
    f32, f16, i32 = mybir.dt.float32, mybir.dt.float16, mybir.dt.int32
    ALU, ACT, AX = mybir.AluOpType, mybir.ActivationFunctionType, mybir.AxisListType
    V, S, T, G = nc.vector, nc.scalar, nc.tensor, nc.gpsimd

    rec_dram = nc.dram_tensor("node_records", (NPAD, 4), f32, kind="Internal").ap()
    pay_dram = nc.dram_tensor("payload_by_src", (P * EC, PAYLOAD), f32, kind="Internal").ap()
    u1_dram = nc.dram_tensor("l1_rows", (P * EC, D), f32, kind="Internal").ap()
    x2_dram = nc.dram_tensor("x2_rows", (P * EC, D), f32, kind="Internal").ap()
    h2_dram = nc.dram_tensor("h2_rows", (P * EC, D), f32, kind="Internal").ap()
    u0_dram = nc.dram_tensor("l3_first_rows", (P * EC, D), f32, kind="Internal").ap()
    own_dram = nc.dram_tensor("l3_own_rows", (P * EC, OWNW), f32, kind="Internal").ap()
    map_dram = nc.dram_tensor("l3_slots", (P * EC, 1), f32, kind="Internal").ap()
    u3_dram = nc.dram_tensor("l3_rows", (P * EC + P * W, D), f32, kind="Internal").ap()

    ctx = ExitStack()
    with ctx:
        def sb(name, cols, dt=f32, parts=P):
            return ctx.enter_context(nc.sbuf_tensor(name, [parts, cols], dt))

        def sem(name):
            return ctx.enter_context(nc.semaphore(name))

        pay = sb("pay", EC * PAYLOAD)
        mf = sb("mf", 2 * EW + 4 * D)
        xd_t = sb("xd", EW)
        xs_t = sb("xs", EW)
        z_t = sb("z", EW)
        out_t = sb("outs", EW)

        def rows(ap):
            return ap.rearrange("p (c f) -> p c f", f=D)

        PAY = pay[:].rearrange("p (c w) -> p c w", w=PAYLOAD)
        M_f, F_f = mf[:, 0:EW], mf[:, EW:2 * EW]
        M, F = rows(M_f), rows(F_f)
        XY = mf[:].rearrange("p (c w) -> p c w", w=2 * D)
        XD, XS, Z, OUT = rows(xd_t[:]), rows(xs_t[:]), rows(z_t[:]), rows(out_t[:])
        U_f = pay[:, 0:EW]
        U = rows(U_f)

        names = ["kn", "kp0", "kc0", "et", "tmp", "tmp2", "st1", "st2", "sq_in", "sq_out", "linear", "cont", "head",
                 "dis", "nsrc", "scalef", "score", "dcnt"]
        c = {n: sb(n, EC + 4) for n in names}
        c["kp1"], c["kc1"] = c["dis"], c["scalef"]

        def col(n):
            return c[n][:, 0:EC]

        icols = {n: sb("i_" + n, EC, i32) for n in ["src", "dst", "et", "rank", "srcX", "dstX", "outD", "outS"]}
        icols["srcS"] = icols["src"]
        icols["l1"] = icols["rank"]
        icols["l3"] = icols["et"]

        c["own"] = c["kp0"]
        c["dst_out"] = c["scalef"]
        iota_c = sb("iota_c", NCOL, f16)
        lists = iota_c[:].bitcast(f32)
        listi = iota_c[:].bitcast(i32)
        extra = sb("extra", 2 * W)
        pf0, pf1, owni, homei = (listi[:, k * W:(k + 1) * W] for k in range(4))
        contc, headc = lists[:, 4 * W:5 * W], lists[:, 5 * W:6 * W]
        disc, ac, ahc = (c["kc0"][:, k * W:(k + 1) * W] for k in range(3))
        slotf, nohome = extra[:, 0:W], extra[:, W:2 * W]
        fits = sb("fits", 1, i32, 1)

        iota_p = sb("iota_p", P, f16)
        iota_r = sb("iota_r", NREL)
        ident = sb("ident", P)
        ident16 = sb("ident16", P, f16)
        upper = sb("upper", P)
        lower = sb("lower", P)
        wcarry = sb("wcarry", P)
        theta_sb = sb("theta_sb", L1_STEPS + 1)
        theta_sum = sb("theta_sum", 1)
        w_sb = sb("w_sb", NBAS * D, f32, D)
        RC = NBAS + 3 * D
        rw_sb = sb("rw_sb", RC, f32, NREL)
        rxy_sb = sb("rxy_sb", RC, f32, 2 * D)
        b2_sb = sb("b2_sb", D, f32, NREL)
        small = sb("small", 4)
        last_row = sb("last_row", D)
        idle = sb("idle", 3)
        key_col = sb("key_col", 4)
        sums = sb("sums", 8)

        h16 = z_t[:].bitcast(f16)
        ONEHOT_W = P + NCOL

        def onehot(b):
            o = b * ONEHOT_W
            return h16[:, o:o + P], h16[:, o + P:o + P + NCOL]

        z16 = h16[:, 4 * ONEHOT_W:4 * ONEHOT_W + 512]
        rs = [out_t[:, b * NCOL:(b + 1) * NCOL] for b in range(2)]
        start_tab = out_t[:, 2 * NCOL:3 * NCOL]
        scratch_b = [out_t[:, (3 + b) * NCOL:(4 + b) * NCOL] for b in range(2)]
        ot = [out_t[:, 5 * NCOL + b * P:5 * NCOL + (b + 1) * P] for b in range(4)]
        same = [out_t[:, 5 * NCOL + (4 + b) * P:5 * NCOL + (5 + b) * P] for b in range(2)]
        rec_sb = mf[:, 0:4 * NCOL]
        REC = rec_sb.rearrange("p (c w) -> p c w", w=4)
        cnt = mf[:, 4 * NCOL:5 * NCOL]
        inc = mf[:, 5 * NCOL:6 * NCOL]
        none = mf[:, 6 * NCOL:7 * NCOL]
        onesn = mf[:, 7 * NCOL:8 * NCOL]

        DW = DCH * D
        dx = [z_t[:, b * DW:(b + 1) * DW] for b in range(4)]
        dxc = [out_t[:, b * DW:(b + 1) * DW] for b in range(2)]
        dsq = [out_t[:, (2 + b) * DW:(3 + b) * DW] for b in range(2)]
        dst1 = [mf[:, b * DCH:(b + 1) * DCH] for b in range(2)]
        dst2 = [mf[:, (2 + b) * DCH:(3 + b) * DCH] for b in range(2)]
        dst3 = [mf[:, (4 + b) * DCH:(5 + b) * DCH] for b in range(2)]

        CW = W * D
        wc = lower
        Mc_f, Uc_f = mf[:, 0:CW], mf[:, CW:2 * CW]
        Mc, Uc, Bc = (rows(mf[:, k * CW:(k + 1) * CW]) for k in range(3))
        ownc_f = xs_t[:, 0:W * OWNW]
        OWNC = ownc_f.rearrange("p (q w) -> p q w", w=OWNW)
        Fc = rows(pay[:, 0:CW])
        Zc, Tc, Oc = (rows(z_t[:, k * CW:(k + 1) * CW]) for k in range(3))
        ownt_f = pay[:, 0:EC * OWNW]
        OWNT = ownt_f.rearrange("p (c w) -> p c w", w=OWNW)
        wt = pay[:, EC * OWNW:EC * OWNW + P]

        oh = [pay[:, b * NREL:(b + 1) * NREL] for b in range(4)]
        o1 = 4 * NREL
        xyt = [pay[0:2 * D, o1 + b * P:o1 + (b + 1) * P] for b in range(4)]
        o2 = o1 + 4 * P
        oht = [pay[0:NREL, o2 + b * P:o2 + (b + 1) * P] for b in range(4)]
        o3 = o2 + 4 * P
        cs = [pay[:, o3 + b * RC:o3 + (b + 1) * RC] for b in range(4)]
        o4 = o3 + 4 * RC
        prod = [pay[:, o4 + b * NBAS * D:o4 + (b + 1) * NBAS * D] for b in range(2)]
        o5 = o4 + 2 * NBAS * D
        o6 = o5 + 2 * D
        xyc = [pay[:, o6 + b * 2 * D:o6 + (b + 1) * 2 * D] for b in range(4)]
        sprod = [pay[:, o5 + b * D:o5 + (b + 1) * D] for b in range(2)]

        ps = [ctx.enter_context(nc.psum_tensor(f"ps{k}", [P, 1024], f32)) for k in range(4)]
        hist = [ps[0], ps[1]]
        R = ps[0]
        LK = [ps[1], ps[2]]
        KR = [LK[b][:, NCOL:NCOL + P] for b in range(2)]
        TP = [ps[3][:, 512 * b:512 * b + 64].bitcast(f16) for b in range(2)]
        MISC = ps[3][:, 768:768 + P]
        CAR = ps[3][:, 768 + P:768 + P + D]
        PWm = [ps[0][:, 0:512], ps[0][:, 512:1024]]
        PSm = [ps[1][:, 0:RC], ps[1][:, 512:512 + RC]]
        XYTp = [ps[2][0:2 * D, 512 * b:512 * b + P] for b in range(2)]
        OTp = [ps[2][0:NREL, 512 * b + P:512 * b + 2 * P] for b in range(2)]

        SEMS = """padded edges_in weights_in pool_filled pool_consts dve_setup dve
            hist_free hist_built hist_done prefix_in prefix_out rec_ready rec_stored
            tile_free tile_built tile_turned tile_copied tile_counted tile_looked ranked
            xdst_in rec_src_in rec_dst_in payload_ready payload_out payload_in srows_idx xsrc_in
            root_in root_out
            dense_go tail_in dense_in0 dense_in1 dense_xc dense_sq dense_var dense_root dense_done dense_out dense_chain
            keys_in keys_out carry_in carry_out carry1_in carry1_out carry3_in carry3_out
            u1_ready u1_stored m1_in l1_chain s2_ready s2_stored s_final
            h2src_in x2dst_in l2_oh l2_xin l2_xy l2_tr l2_tc l2_mm l2_cs l2_prod l2_done l2_scored gate_in gate_out
            list_in list_out fits_set map_stored list_ready
            own_ready own_stored own_in u0_stored uc_ready uc_stored mc_in lc_chain lc_carry_in lc_carry_out
            map_out slots_in slots_ready first_zero dfull_ready dfull_out dc_ready dc_out rootc_in rootc_out rootf_in rootf_out
            turn1 turn3 u3_ready u3_stored m3_in l3_chain d_final outs_scattered outd_scattered""".split()
        s = {n: sem(n) for n in SEMS}

        block = ctx.enter_context(nc.Block())

        class Chain:
            def __init__(self, eng, sm, base=0, loop=None, per=0):
                self.eng, self.sm, self.n, self.base, self.loop, self.per = eng, sm, 0, base, loop, per

            def at(self, n):
                v = self.base + n
                return v if self.loop is None else self.loop * self.per + v

            def __call__(self, ins):
                self.n += 1
                ins.then_inc(self.sm, 1)
                self.eng.wait_ge(self.sm, self.at(self.n))

            def many(self, inss):
                for ins in inss:
                    self.n += 1
                    ins.then_inc(self.sm, 1)
                self.eng.wait_ge(self.sm, self.at(self.n))

        def bc(ap, n=D):
            return ap.unsqueeze(2).to_broadcast([ap.shape[0], ap.shape[1], n])

        def bf(ap, n=EC):
            return ap.unsqueeze(1).to_broadcast([ap.shape[0], n, ap.shape[1]])

        @block.sync
        def _(sp):
            for tile, arr in ((icols["src"], src), (icols["dst"], dst), (icols["et"], etype)):
                sp.wait_ge(s["padded"], 1)
                full = P - 16
                sp.dma_start(tile[0:full, :], arr[0:full * EC].rearrange("(p c) -> p c", c=EC)).then_inc(s["edges_in"], 16)
                sp.dma_start(tile[full:P - 1, :],
                             arr[full * EC:(P - 1) * EC].rearrange("(p c) -> p c", c=EC)).then_inc(s["edges_in"], 16)
                sp.dma_start(tile[P - 1:P, 0:LAST_ROWS],
                             arr[(P - 1) * EC:E].rearrange("(p c) -> p c", p=1)).then_inc(s["edges_in"], 16)
            sp.wait_ge(s["dve_setup"], 1)
            sp.dma_start(w_sb[:], w_basis.rearrange("i b o -> i (b o)")).then_inc(s["weights_in"], 16)
            sp.dma_start(rw_sb[:, 0:NBAS], w_comp).then_inc(s["weights_in"], 16)
            sp.dma_start(rw_sb[:, NBAS:NBAS + D], rel).then_inc(s["weights_in"], 16)
            sp.dma_start(rw_sb[:, NBAS + D:NBAS + 2 * D],
                         a1b.unsqueeze(0).to_broadcast([NREL, D])).then_inc(s["weights_in"], 16)
            sp.dma_start(b2_sb[:], a2b.unsqueeze(0).to_broadcast([NREL, D])).then_inc(s["weights_in"], 16)
            sp.dma_start(rxy_sb[0:D, NBAS + D:NBAS + 2 * D], a1t).then_inc(s["weights_in"], 16)
            sp.dma_start(rxy_sb[0:D, NBAS + 2 * D:RC], w_self).then_inc(s["weights_in"], 16)
            sp.dma_start(rxy_sb[D:2 * D, NBAS:NBAS + D], a2t).then_inc(s["weights_in"], 16)
            sp.dma_start(theta_sb[:], theta.unsqueeze(0).to_broadcast([P, L1_STEPS + 1])).then_inc(s["weights_in"], 16)
            sp.wait_ge(s["pool_consts"], 1)
            sp.dma_start(map_dram.rearrange("(p c) w -> p (c w)", p=P), col("linear")).then_inc(s["map_stored"], 16)
            sp.wait_ge(s["rec_ready"], 1)
            sp.dma_start(rec_dram.rearrange("(p c) w -> p (c w)", p=P), rec_sb).then_inc(s["rec_stored"], 16)
            sp.wait_ge(s["payload_out"], 16 * EC)
            sp.dma_start(pay[:], pay_dram.rearrange("(p c) w -> p (c w)", p=P)).then_inc(s["payload_in"], 16)
            with sp.Fori(0, L1_STEPS) as i:
                sp.wait_ge(s["u1_ready"], i + 1)
                sp.dma_start(u1_dram.rearrange("(p c) w -> p (c w)", p=P), U_f).then_inc(s["u1_stored"], 16)
            sp.wait_ge(s["s2_ready"], 1)
            sp.dma_start(x2_dram.rearrange("(p c) w -> p (c w)", p=P), xs_t[:]).then_inc(s["s2_stored"], 16)
            sp.dma_start(h2_dram.rearrange("(p c) w -> p (c w)", p=P), F_f).then_inc(s["s2_stored"], 16)
            sp.wait_ge(s["fits_set"], 1)
            longest = sp.value_load(fits[0:1, 0:1], min_val=0, max_val=EC)
            with sp.If(longest <= GW):
                sp.wait_ge(s["own_ready"], 1)
                sp.dma_start(own_dram.rearrange("(p c) w -> p (c w)", p=P), ownt_f).then_inc(s["own_stored"], 16)
                sp.wait_ge(s["uc_ready"], 1)
                sp.dma_start(u0_dram.rearrange("(p c) w -> p (c w)", p=P), z_t[:]).then_inc(s["u0_stored"], 16)
                sp.wait_ge(s["uc_ready"], 2)
                sp.dma_start(u3_dram[0:P * EC].rearrange("(p c) w -> p (c w)", p=P), F_f).then_inc(s["uc_stored"], 16)
                with sp.Fori(0, L3_STEPS - 1) as i:
                    sp.wait_ge(s["uc_ready"], i + 3)
                    sp.dma_start(u3_dram[P * EC:P * EC + P * W].rearrange("(p c) w -> p (c w)", p=P),
                                 Uc_f).then_inc(s["uc_stored"], 16)
            with sp.Else():
                with sp.Fori(0, L3_STEPS) as i:
                    sp.wait_ge(s["u3_ready"], i + 1)
                    sp.dma_start(u3_dram[0:P * EC].rearrange("(p c) w -> p (c w)", p=P), U_f).then_inc(s["u3_stored"], 16)

        @block.gpsimd
        def _(pool):
            def gather(dest, table, idx, bound, sm, n=EC):
                for k in range(n):
                    G.indirect_dma_start(out=dest(k), out_offset=None, in_=table,
                                         in_offset=bass.IndirectOffsetOnAxis(ap=idx[:, k:k + 1], axis=0),
                                         bounds_check=bound, oob_is_err=False).then_inc(sm, 16)

            def scatter(table, source, idx, bound, sm, n=EC, first=0):
                for k in range(first, first + n):
                    G.indirect_dma_start(out=table, out_offset=bass.IndirectOffsetOnAxis(ap=idx[:, k:k + 1], axis=0),
                                         in_=source(k), in_offset=None,
                                         bounds_check=bound, oob_is_err=False).then_inc(sm, 16)

            for k in ("src", "dst"):
                G.memset(icols[k][:], PADNODE)
            G.memset(icols["et"][:], 0).then_inc(s["padded"], 1)
            G.iota(iota_c[:], [[1, NCOL]], base=0, channel_multiplier=0, allow_small_or_imprecise_dtypes=True)
            G.iota(iota_p[:], [[1, P]], base=0, channel_multiplier=0, allow_small_or_imprecise_dtypes=True)
            G.iota(slotf, [[1, W]], base=P * EC, channel_multiplier=W, allow_small_or_imprecise_dtypes=True)
            G.iota(iota_r[:], [[1, NREL]], base=0, channel_multiplier=0, allow_small_or_imprecise_dtypes=True)
            G.iota(col("linear"), [[1, EC]], base=0, channel_multiplier=EC, allow_small_or_imprecise_dtypes=True)
            G.memset(ident[:], 0.0)
            G.memset(upper[:], 1.0)
            G.memset(idle[:], 0.0).then_inc(s["turn1"], 1)
            G.memset(ident16[:], 0.0).then_inc(s["turn3"], 1)
            G.memset(lower[:], 1.0).then_inc(s["pool_filled"], 1)
            pool.wait_ge(s["pool_filled"], 1)
            for t in (ident, ident16):
                G.affine_select(out=t[:], in_=t[:], compare_op=ALU.not_equal, fill=1.0, base=0,
                                pattern=[[-1, P]], channel_multiplier=1)
            G.affine_select(out=upper[:], in_=upper[:], compare_op=ALU.is_gt, fill=0.0, base=0,
                            pattern=[[1, P]], channel_multiplier=-1)
            G.affine_select(out=lower[:], in_=lower[:], compare_op=ALU.is_gt, fill=0.0, base=0,
                            pattern=[[-1, P]], channel_multiplier=1).then_inc(s["pool_consts"], 1)
            pool.wait_ge(s["edges_in"], 16 * 9)
            pool.wait_ge(s["dve"], 1)
            gather(lambda k: XD[:, k, :], x, icols["dst"], N - 1, s["xdst_in"])
            pool.wait_ge(s["rec_stored"], 16)
            gather(lambda k: PAY[:, k, D:D + 4], rec_dram, icols["src"], NPAD - 1, s["rec_src_in"])
            gather(lambda k: PAY[:, k, D + 4:D + 8], rec_dram, icols["dst"], NPAD - 1, s["rec_dst_in"])
            pool.wait_ge(s["payload_ready"], 1)
            scatter(pay_dram, lambda k: PAY[:, k, :], icols["rank"], P * EC - 1, s["payload_out"])
            pool.wait_ge(s["payload_in"], 16)
            G.tensor_copy(icols["srcS"][:], PAY[:, :, PAYLOAD - 1]).then_inc(s["srows_idx"], 1)
            pool.wait_ge(s["srows_idx"], 1)
            gather(lambda k: XS[:, k, :], x, icols["srcS"], N - 1, s["xsrc_in"])
            with pool.Fori(0, L1_STEPS) as i:
                pool.wait_ge(s["u1_stored"], 16 * i + 16)
                pool.wait_ge(s["turn1"], i + 1)
                G.tensor_tensor(idle[:, 0:1], idle[:, 1:2], idle[:, 1:2], ALU.add).then_inc(s["turn1"], 1)
                gather(lambda k: M[:, k, :], u1_dram, icols["l1"], P * EC - 1, s["m1_in"])
            pool.wait_ge(s["s2_stored"], 32)
            gather(lambda k: XD[:, k, :], x2_dram, icols["dstX"], P * EC - 1, s["x2dst_in"])
            pool.wait_ge(s["s_final"], 1)
            gather(lambda k: XY[:, k, 0:D], h2_dram, icols["srcX"], P * EC - 1, s["h2src_in"])
            pool.wait_ge(s["dense_out"], 16 * (DCHUNKS + 1))
            scatter(out, lambda k: OUT[:, k, :], icols["outS"], N - 1, s["outs_scattered"])
            pool.wait_ge(s["list_ready"], 1)
            longest = pool.value_load(fits[0:1, 0:1], min_val=0, max_val=EC)
            with pool.If(longest <= GW):
                pool.wait_ge(s["map_stored"], 16)
                scatter(map_dram, lambda k: slotf[:, k:k + 1], homei, P * EC - 1, s["map_out"], GW)
                pool.wait_ge(s["map_out"], 16 * GW)
                gather(lambda k: ac[:, k:k + 1], map_dram, pf0, P * EC - 1, s["slots_in"], GW)
                pool.wait_ge(s["u0_stored"], 16)
                pool.wait_ge(s["first_zero"], 1)
                gather(lambda k: Mc[:, k, :], u0_dram, pf0, P * EC - 1, s["mc_in"], GW)
                pool.wait_ge(s["own_stored"], 16)
                gather(lambda k: OWNC[:, k, :], own_dram, owni, P * EC - 1, s["own_in"], GW)
                pool.wait_ge(s["dfull_ready"], 1)
                pool.wait_ge(s["slots_ready"], 1)
                fill = -(-EC // (L3_STEPS - 1))
                done = 0
                for k in range(1, L3_STEPS):
                    n = min(fill, EC - done)
                    scatter(out, lambda q: XD[:, q, :], icols["outD"], N - 1, s["dfull_out"], n, done)
                    done += n
                    pool.wait_ge(s["uc_stored"], 16 * (k + 1))
                    gather(lambda q: Mc[:, q, :], u3_dram, pf1, P * EC + P * W - 1, s["mc_in"], GW)
                assert done == EC
                pool.wait_ge(s["dc_ready"], 1)
                scatter(out, lambda k: Oc[:, k, :], homei, N - 1, s["dc_out"], GW)
                pool.wait_ge(s["dfull_out"], 16 * EC)
                pool.wait_ge(s["dc_out"], 16 * GW)
            with pool.Else():
                with pool.Fori(0, L3_STEPS) as i:
                    pool.wait_ge(s["u3_stored"], 16 * i + 16)
                    pool.wait_ge(s["turn3"], i + 1)
                    G.tensor_tensor(idle[:, 2:3], idle[:, 1:2], idle[:, 1:2], ALU.add).then_inc(s["turn3"], 1)
                    gather(lambda k: M[:, k, :], u3_dram[0:P * EC], icols["l3"], P * EC - 1, s["m3_in"])
                pool.wait_ge(s["d_final"], 1)
                scatter(out, lambda k: XD[:, k, :], icols["outD"], N - 1, s["outd_scattered"])
                pool.wait_ge(s["outd_scattered"], 16 * EC)
            pool.wait_ge(s["outs_scattered"], 16 * EC)

        @block.vector
        def _(dve):
            link = Chain(dve, s["dve"])

            def tt(o, a, b, op):
                return V.tensor_tensor(o, a, b, op)

            def ts(o, a, s1, s2, op0, op1=None):
                return V.tensor_scalar(o, a, s1, s2, op0, op1) if op1 is not None else V.tensor_scalar(o, a, s1, None, op0)

            def roots(sin, sout):
                count = [0]

                def root(chain, o, a, w=EC):
                    count[0] += 1
                    V.tensor_copy(c["sq_in"][:, 0:w], a).then_inc(s[sin], 1)
                    dve.wait_ge(s[sout], count[0])
                    chain(V.reciprocal(o, c["sq_out"][:, 0:w]))
                return root

            root_main = roots("root_in", "root_out")

            def layernorm(xin, hout, tmp, chain=link, root=root_main, w=EC):
                m, v = c["st1"][:, 0:w], c["st2"][:, 0:w]
                chain(V.tensor_reduce(m, xin, AX.X, ALU.add))
                chain(ts(m, m, 1.0 / D, None, ALU.mult))
                chain(tt(tmp, xin, bc(m), ALU.subtract))
                chain(tt(hout, tmp, tmp, ALU.mult))
                chain(V.tensor_reduce(v, hout, AX.X, ALU.add))
                chain(ts(v, v, 1.0 / D, EPS, ALU.mult, ALU.add))
                root(chain, m, v, w)
                chain(V.scalar_tensor_tensor(out=hout, in0=tmp, scalar=0.0, in1=bc(m), op0=ALU.max, op1=ALU.mult))

            def root(o, a):
                root_main(link, o, a)

            link(V.memset(xd_t[:], 0.0))
            link(V.memset(xs_t[:], 0.0))
            link(V.memset(z16, 0.0))
            link(V.memset(onesn, 1.0))
            for n in ("kp0", "kc0", "kn", "et"):
                link(V.memset(c[n][:], 0.0))
            link(V.memset(XY[:, EC:EC + 2, :], 0.0))
            link(V.memset(rxy_sb[:], 0.0))
            link(V.memset(rw_sb[:, NBAS + 2 * D:RC], 0.0))
            V.memset(small[:], 0.0).then_inc(s["dve_setup"], 1)
            dve.wait_ge(s["edges_in"], 16 * 9)
            dve.wait_ge(s["pool_consts"], 1)
            for k, name in enumerate(("src", "dst")):
                kp, kc = col(f"kp{k}"), col(f"kc{k}")
                link(V.tensor_copy(col("kn"), icols[name][:]))
                link(ts(kp, col("kn"), 1.0 / NCOL, 0.5 / NCOL - 0.5, ALU.mult, ALU.add))
                link(ts(kp, kp, MAGIC, None, ALU.add))
                link(ts(kp, kp, MAGIC, None, ALU.subtract))
                link(V.scalar_tensor_tensor(out=kc, in0=kp, scalar=-float(NCOL), in1=col("kn"), op0=ALU.mult, op1=ALU.add))
            link(V.tensor_copy(col("kn"), icols["src"][:]))
            link(V.tensor_copy(col("et"), icols["et"][:]))
            hist_keys = [("kp0", "kc0"), ("kp1", "kc1")]
            with dve.Fori(0, EC // 2) as i:
                for b in range(2):
                    t = 2 * i + b
                    dve.wait_ge(s["hist_free"], t + 1)
                    for k, (kp, kc) in enumerate(hist_keys):
                        op_, oc_ = onehot(2 * b + k)
                        V.tensor_scalar(op_, iota_p[:], c[kp][:, bass.ds(t, 1)], None, ALU.is_equal)
                        last = V.tensor_scalar(oc_, iota_c[:], c[kc][:, bass.ds(t, 1)], None, ALU.is_equal)
                    last.then_inc(s["hist_built"], 1)
            dve.wait_ge(s["hist_done"], 1)
            for k in range(2):
                link(V.tensor_copy(cnt, hist[k][:, 0:NCOL]))
                link(V.tensor_tensor_scan(inc, onesn, cnt, 0.0, ALU.mult, ALU.add))
                V.tensor_copy(small[:, 0:1], inc[:, NCOL - 1:NCOL]).then_inc(s["prefix_in"], 1)
                dve.wait_ge(s["prefix_out"], k + 1)
                link(V.tensor_copy(small[:, 1:2], MISC[:, 0:1]))
                link(ts(inc, inc, small[:, 1:2], None, ALU.add))
                if k == 0:
                    link(tt(start_tab, inc, cnt, ALU.subtract))
                link(ts(none, cnt, 0.0, FAR, ALU.is_equal, ALU.mult))
                link(V.scalar_tensor_tensor(out=REC[:, :, 2 * k], in0=inc, scalar=-1.0, in1=none, op0=ALU.add, op1=ALU.add))
                link(V.tensor_copy(REC[:, :, 2 * k + 1], cnt))
            V.memset(small[:, 2:3], 0.0).then_inc(s["rec_ready"], 1)
            def build_tile(t, b, freed):
                dve.wait_ge(s["tile_free"], freed)
                op_, oc_ = onehot(b)
                V.tensor_scalar(op_, iota_p[:], c["kp0"][:, bass.ds(t, 1)], None, ALU.is_equal)
                V.tensor_copy(key_col[:, b:b + 1], c["kn"][:, bass.ds(t, 1)])
                V.tensor_scalar(oc_, iota_c[:], c["kc0"][:, bass.ds(t, 1)], None, ALU.is_equal).then_inc(s["tile_built"], 1)

            build_tile(0, 0, 2)
            build_tile(1, 1, 2)
            link(V.memset(small[:, 3:4], 0.0))
            V.memset(small[:, 3:4], 0.0).then_inc(s["tile_looked"], 2)
            V.memset(small[:, 2:3], 0.0).then_inc(s["ranked"], 1)
            with dve.Fori(0, EC // 4) as i:
                for b in range(4):
                    t = 4 * i + b
                    dve.wait_ge(s["tile_looked"], t + 1)
                    build_tile(t + 2, (b + 2) % 4, t + 1)
                    if b == 0:
                        dve.wait_ge(s["ranked"], i + 1)
                    dve.wait_ge(s["tile_counted"], t + 1)
                    V.tensor_tensor_reduce(out=scratch_b[b % 2], in0=LK[b % 2][:, 0:NCOL], in1=onehot(b)[1], scale=1.0,
                                           scalar=0.0, op0=ALU.mult, op1=ALU.add, accum_out=sums[:, b:b + 1])
                    V.scalar_tensor_tensor(out=same[b % 2], in0=KR[b % 2], scalar=key_col[:, b:b + 1], in1=lower[:],
                                           op0=ALU.is_equal, op1=ALU.mult,
                                           accum_out=sums[:, 4 + b:5 + b]).then_inc(s["tile_looked"], 1)
                dve.wait_ge(s["tile_looked"], 4 * i + 6)
                tt(c["score"][:, bass.ds(4 * i, 4)], sums[:, 0:4], sums[:, 4:8], ALU.add).then_inc(s["ranked"], 1)
            dve.wait_ge(s["ranked"], EC // 4 + 1)
            link(V.tensor_copy(icols["rank"][:], col("score")))
            dve.wait_ge(s["xdst_in"], 16 * EC)
            layernorm(XD, OUT, Z)
            dve.wait_ge(s["rec_src_in"], 16 * EC)
            dve.wait_ge(s["rec_dst_in"], 16 * EC)
            link(ts(col("tmp"), PAY[:, :, D + 5], 1.0, None, ALU.add))
            root(col("nsrc"), col("tmp"))
            link(tt(PAY[:, :, 0:D], OUT, bc(col("nsrc")), ALU.mult))
            link(V.tensor_copy(PAY[:, :, PAYLOAD - 1], col("kn")))
            link(V.tensor_copy(icols["srcX"][:], PAY[:, :, D]))
            link(V.tensor_copy(icols["l3"][:], PAY[:, :, D + 2]))
            link(V.tensor_copy(icols["dstX"][:], PAY[:, :, D + 4]))
            link(tt(col("tmp"), PAY[:, :, D + 6], col("linear"), ALU.not_equal))
            link(V.tensor_copy(col("score"), icols["dst"][:]))
            link(V.scalar_tensor_tensor(out=icols["outD"][:], in0=col("tmp"), scalar=FAR, in1=col("score"), op0=ALU.mult, op1=ALU.add))
            link(V.tensor_copy(col("dcnt"), PAY[:, :, D + 7]))
            link(V.tensor_copy(col("own"), PAY[:, :, D + 6]))
            V.memset(small[:, 3:4], 0.0).then_inc(s["payload_ready"], 1)
            link(tt(XD, XD, OUT, ALU.add))
            dve.wait_ge(s["weights_in"], 16 * 9)
            link(V.tensor_reduce(theta_sum[:], theta_sb[:], AX.X, ALU.add))
            link(tt(rw_sb[:, NBAS:NBAS + D], rw_sb[:, NBAS:NBAS + D], b2_sb[:], ALU.add))
            layernorm(XD, OUT, Z)
            link(V.scalar_tensor_tensor(out=XD, in0=OUT, scalar=theta_sum[:], in1=XD, op0=ALU.mult, op1=ALU.add))
            def dense_pair(slots, pn, cn, chain, number):
                nb = len(slots)
                w = cn * D
                X = [dx[sl][0:pn, 0:w] for sl in slots]
                for l in range(3):
                    for b in range(nb):
                        X3 = X[b].rearrange("p (c f) -> p c f", f=D)
                        chain(V.tensor_reduce(dst1[b][0:pn, 0:cn], X3, AX.X, ALU.add))
                        chain(ts(dst1[b][0:pn, 0:cn], dst1[b][0:pn, 0:cn], 1.0 / D, None, ALU.mult))
                        tt(rows(dxc[b][0:pn, 0:w]), X3, bc(dst1[b][0:pn, 0:cn]), ALU.subtract).then_inc(s["dense_xc"], 1)
                    for b in range(nb):
                        dve.wait_ge(s["dense_sq"], number(l, b))
                        chain(V.tensor_reduce(dst2[b][0:pn, 0:cn], rows(dsq[b][0:pn, 0:w]), AX.X, ALU.add))
                        ts(dst2[b][0:pn, 0:cn], dst2[b][0:pn, 0:cn], 1.0 / D, EPS, ALU.mult, ALU.add).then_inc(s["dense_var"], 1)
                    for b in range(nb):
                        X3 = X[b].rearrange("p (c f) -> p c f", f=D)
                        dve.wait_ge(s["dense_root"], number(l, b))
                        chain(V.reciprocal(dst1[b][0:pn, 0:cn], dst3[b][0:pn, 0:cn]))
                        if l == 1:
                            chain(ts(dst1[b][0:pn, 0:cn], dst1[b][0:pn, 0:cn], theta_sum[0:pn], None, ALU.mult))
                        if l == 2:
                            chain(ts(dst1[b][0:pn, 0:cn], dst1[b][0:pn, 0:cn], ALPHA, None, ALU.mult))
                        dve.wait_ge(s["dense_xc"], number(l, b))
                        chain(V.scalar_tensor_tensor(out=rows(dxc[b][0:pn, 0:w]), in0=rows(dxc[b][0:pn, 0:w]), scalar=0.0,
                                                     in1=bc(dst1[b][0:pn, 0:cn]), op0=ALU.max, op1=ALU.mult))
                        if l < 2:
                            chain(tt(X[b], X[b], dxc[b][0:pn, 0:w], ALU.add))
                        else:
                            tt(X[b], X[b], dxc[b][0:pn, 0:w], ALU.add).then_inc(s["dense_done"], 1)

            tail_chain = Chain(dve, s["dense_chain"])
            V.memset(small[:, 2:3], 0.0).then_inc(s["dense_go"], 1)
            dve.wait_ge(s["tail_in"], 16)
            dense_pair([0], TAIL_P, TAIL_C, tail_chain, lambda l, b: l + 1)
            dve.wait_ge(s["dense_done"], 1)
            PER = 2 * 2 * (3 * 5 + 2 + 2)
            with dve.Fori(0, DCHUNKS // UNROLL) as i:
                ch = Chain(dve, s["dense_chain"], tail_chain.n, i, PER)
                for h in range(2):
                    dve.wait_ge(s[f"dense_in{h}"], 32 * i + 32)
                    dense_pair([2 * h, 2 * h + 1], P, DCH, ch,
                               lambda l, b: 12 * i + (3 + 6 * h + 2 * l + b + 1))
                assert ch.n == PER, ch.n
            dve.wait_ge(s["payload_in"], 16)
            SRC, SEND_S, CNT_S, CNT_D = PAY[:, :, PAYLOAD - 1], PAY[:, :, D], PAY[:, :, D + 1], PAY[:, :, D + 3]
            link(V.tensor_copy(icols["l1"][:], PAY[:, :, D + 4]))
            link(tt(col("tmp"), SEND_S, col("linear"), ALU.not_equal))
            link(ts(col("tmp2"), CNT_D, 0.0, None, ALU.is_gt))
            link(tt(col("tmp"), col("tmp"), col("tmp2"), ALU.max))
            link(V.scalar_tensor_tensor(out=icols["outS"][:], in0=col("tmp"), scalar=FAR, in1=SRC, op0=ALU.mult, op1=ALU.add))
            link(V.tensor_copy(col("kn"), SRC))
            link(ts(col("scalef"), CNT_S, 1.0, None, ALU.add))
            root(col("nsrc"), col("scalef"))
            link(V.tensor_copy(col("scalef"), CNT_S))
            root(col("dis"), col("scalef"))

            seg = [0]

            def segments():
                seg[0] += 1
                kn = col("kn")
                link(V.memset(c["cont"][:], 0.0))
                link(tt(c["cont"][:, 1:EC], kn[:, 1:EC], kn[:, 0:EC - 1], ALU.is_equal))
                link(ts(col("head"), kn, kn[:, 0:1], None, ALU.is_equal))
                V.tensor_copy(small[:, 0:1], kn[:, 0:1]).then_inc(s["keys_in"], 1)
                dve.wait_ge(s["keys_out"], seg[0])
                link(V.scalar_tensor_tensor(out=wcarry[:], in0=MISC, scalar=kn[:, EC - 1:EC], in1=upper[:],
                                            op0=ALU.is_equal, op1=ALU.mult))

            def segment_sums(chain, m, ins, outs, number, tmp):
                chain.many([V.tensor_tensor_scan(Z[:, :, f], col("cont"), m[:, :, f], 0.0, ALU.mult, ALU.add)
                            for f in range(D)])
                V.tensor_copy(last_row[:], Z[:, EC - 1, :]).then_inc(ins, 1)
                dve.wait_ge(outs, number)
                chain(tt(tmp, bf(CAR), bc(col("head")), ALU.mult))
                chain(tt(Z, Z, tmp, ALU.add))

            listed = [0]

            def ask(column):
                listed[0] += 1
                V.tensor_copy(small[:, 3:4], column).then_inc(s["list_in"], 1)
                dve.wait_ge(s["list_out"], listed[0])

            def compact(ptr, own, outi):
                last8 = slice(EC, EC + 4)
                rev, act, code, vals = c["tmp"], c["tmp2"], c["st1"], c["st2"][:, 0:W]
                valid, ownf, aux, keep = (c["sq_out"][:, 0:W], c["sq_out"][:, W:2 * W], c["sq_out"][:, 2 * W:3 * W],
                                          c["st2"][:, W:2 * W])
                lin = col("linear")
                link(ts(rev[:, 0:EC], lin, lin[:, 0:1], -1.0, ALU.subtract, ALU.mult))
                link(ts(rev[:, 0:EC], rev[:, 0:EC], float(EC), SPLIT, ALU.add, ALU.mult))
                link(ts(act[:, 0:EC], ptr, FAR / 2, None, ALU.is_lt))
                link(V.scalar_tensor_tensor(out=act[:, 0:EC], in0=lin, scalar=E - 0.5, in1=act[:, 0:EC],
                                            op0=ALU.is_lt, op1=ALU.mult))
                link(V.tensor_reduce(small[:, 0:1], act[:, 0:EC], AX.X, ALU.add))
                ask(small[:, 0:1])
                link(V.tensor_reduce(small[:, 1:2], MISC, AX.X, ALU.max))
                link(ts(small[:, 0:1], small[:, 1:2], GW + 0.5, FAR, ALU.is_lt, ALU.mult))
                link(V.tensor_copy(fits[0:1, 0:1], small[0:1, 1:2]))
                link(V.tensor_tensor_scan(code[:, 0:EC], col("cont"), act[:, 0:EC], 0.0, ALU.mult, ALU.add))
                ask(code[:, EC - 1:EC])
                link(V.tensor_copy(small[:, 1:2], MISC[:, 0:1]))
                link(V.scalar_tensor_tensor(out=code[:, 0:EC], in0=col("head"), scalar=small[:, 1:2], in1=code[:, 0:EC],
                                            op0=ALU.mult, op1=ALU.add))
                link(ts(code[:, 0:EC], code[:, 0:EC], 0.0, small[:, 0:1], ALU.is_gt, ALU.mult))
                link(V.tensor_copy(col("sq_in"), outi))
                link(tt(col("sq_in"), col("sq_in"), code[:, 0:EC], ALU.add))
                link(V.tensor_copy(outi, col("sq_in")))

                def extract(value, idx):
                    link(V.memset(code[:, last8], 0.0))
                    link(tt(code[:, 0:EC], rev[:, 0:EC], value, ALU.add))
                    link(tt(code[:, 0:EC], code[:, 0:EC], act[:, 0:EC], ALU.mult))
                    for r in range(W // 8):
                        link(V.max(out=vals[:, 8 * r:8 * r + 8], in_=code[:]))
                        link(V.match_replace(out=code[:], in_to_replace=vals[:, 8 * r:8 * r + 8], in_values=code[:],
                                             imm_value=0.0))
                    link(ts(aux, vals, 1.0 / SPLIT, -0.4, ALU.mult, ALU.add))
                    link(ts(aux, aux, MAGIC, None, ALU.add))
                    link(ts(aux, aux, MAGIC, None, ALU.subtract))
                    link(V.scalar_tensor_tensor(out=ownf, in0=aux, scalar=-SPLIT, in1=vals, op0=ALU.mult, op1=ALU.add))
                    link(ts(valid, vals, 0.0, None, ALU.is_gt))
                    link(ts(aux, vals, 0.0, FAR, ALU.is_le, ALU.mult))
                    link(tt(idx, ownf, aux, ALU.add))

                extract(ptr, pf0)
                extract(own, owni)
                link(V.scalar_tensor_tensor(out=keep, in0=valid, scalar=-1.0, in1=ownf, op0=ALU.add, op1=ALU.add))
                link(V.memset(contc, 0.0))
                link(tt(contc[:, 1:W], keep[:, 1:W], keep[:, 0:W - 1], ALU.is_equal))
                link(ts(headc, keep, own[:, 0:1], None, ALU.is_equal))
                link(V.tensor_reduce(small[:, 0:1], keep, AX.X, ALU.max))
                link(tt(small[:, 0:1], small[:, 0:1], own[:, EC - 1:EC], ALU.is_equal))
                link(V.tensor_reduce(small[:, 1:2], headc, AX.X, ALU.max))
                ask(small[:, 1:2])
                link(V.tensor_copy(wt, MISC))
                ask(small[:, 1:2])
                link(ts(small[:, 2:3], MISC[:, 0:1], 0.0, None, ALU.is_gt))
                link(ts(wc[:], wcarry[:], small[:, 0:1], None, ALU.mult))
                link(V.tensor_copy(small[:, 1:2], own[:, EC - 1:EC]))
                link(ts(aux, keep, small[:, 1:2], small[:, 2:3], ALU.is_equal, ALU.mult))
                link(tt(aux[:, 0:W - 1], aux[:, 0:W - 1], contc[:, 1:W], ALU.max))
                link(tt(aux, valid, aux, ALU.is_gt))
                link(ts(nohome, aux, -FAR, FAR, ALU.mult, ALU.add))
                link(tt(homei, ownf, nohome, ALU.add))
                link(ts(aux, valid, -1.0, 1.0, ALU.mult, ALU.add))
                link(tt(contc[:, 1:W], contc[:, 1:W], aux[:, 1:W], ALU.max))
                link(V.memset(ac, 2 * FAR))

            def compact_sums(chain, number):
                chain.many([V.tensor_tensor_scan(Zc[:, :, f], contc, Mc[:, :, f], 0.0, ALU.mult, ALU.add)
                            for f in range(D)])
                V.tensor_copy(last_row[:], Zc[:, W - 1, :]).then_inc(s["lc_carry_in"], 1)
                dve.wait_ge(s["lc_carry_in"], number)

            segments()
            dve.wait_ge(s["dense_out"], 16 * (DCHUNKS + 1))
            segment_sums(link, PAY[:, :, 0:D], s["carry_in"], s["carry_out"], 1, OUT)
            dve.wait_ge(s["xsrc_in"], 16 * EC)
            layernorm(XS, F, OUT)
            link(tt(OUT, F, bc(col("nsrc")), ALU.mult))
            link(tt(Z, Z, OUT, ALU.add))
            link(tt(Z, Z, bc(col("nsrc")), ALU.mult))
            link(tt(XS, XS, Z, ALU.add))
            layernorm(XS, F, Z)
            link(V.memset(M_f, 0.0))
            link(tt(U, F, bc(col("dis")), ALU.mult))
            V.tensor_copy(small[:, 2:3], small[:, 3:4]).then_inc(s["u1_ready"], 1)
            link(ts(OUT, F, theta_sb[:, 0:1], None, ALU.mult))
            PER1 = D + 2 + 4
            with dve.Fori(0, L1_STEPS) as i:
                ch = Chain(dve, s["l1_chain"], 0, i, PER1)
                dve.wait_ge(s["m1_in"], 16 * EC * i + 16 * EC)
                segment_sums(ch, M, s["carry1_in"], s["carry1_out"], i + 1, U)
                ch(tt(Z, Z, bc(col("dis")), ALU.mult))
                ch(tt(F, F, Z, ALU.subtract))
                ch(tt(U, F, bc(col("dis")), ALU.mult))
                V.tensor_copy(small[:, 2:3], small[:, 3:4]).then_inc(s["u1_ready"], 1)
                ch(V.scalar_tensor_tensor(out=OUT, in0=F, scalar=theta_sb[:, bass.ds(i + 1, 1)], in1=OUT, op0=ALU.mult, op1=ALU.add))
                assert ch.n == PER1
            link(tt(XS, XS, OUT, ALU.add))
            layernorm(XS, F, Z)
            V.tensor_copy(small[:, 2:3], small[:, 3:4]).then_inc(s["s2_ready"], 1)
            V.scalar_tensor_tensor(out=OUT, in0=F, scalar=ALPHA, in1=XS, op0=ALU.mult, op1=ALU.add).then_inc(s["s_final"], 1)
            link(V.tensor_copy(col("kn"), icols["dst"][:]))
            segments()
            root(col("dis"), col("dcnt"))
            link(V.tensor_copy(col("dst_out"), icols["outD"][:]))
            link(V.tensor_copy(col("nsrc"), icols["l3"][:]))
            compact(col("nsrc"), col("own"), icols["outD"][:])
            V.tensor_copy(small[:, 3:4], small[:, 1:2]).then_inc(s["fits_set"], 1)
            V.tensor_copy(small[:, 2:3], small[:, 1:2]).then_inc(s["list_ready"], 1)
            dve.wait_ge(s["x2dst_in"], 16 * EC)
            dve.wait_ge(s["h2src_in"], 16 * EC)
            dve.wait_ge(s["s2_stored"], 32)
            layernorm(XD, XY[:, 0:EC, D:2 * D], Z)

            def build_types(t, b):
                V.tensor_scalar(oh[b], iota_r[:], c["et"][:, bass.ds(t, 1)], None, ALU.is_equal).then_inc(s["l2_oh"], 1)

            CUR = XS
            V.memset(small[:, 2:3], 0.0).then_inc(s["l2_xin"], 1)
            V.memset(sums[:, 7:8], 0.0).then_inc(s["l2_prod"], 2)
            V.memset(sums[:, 6:7], 0.0).then_inc(s["l2_scored"], 1)
            build_types(0, 0)
            build_types(1, 1)
            with dve.Fori(0, EC // 4) as i:
                for b in range(4):
                    t = 4 * i + b
                    dve.wait_ge(s["l2_tr"], t + 1)
                    build_types(t + 2, (b + 2) % 4)
                    if b == 0:
                        dve.wait_ge(s["l2_scored"], i + 1)
                    dve.wait_ge(s["l2_cs"], t + 1)
                    V.tensor_tensor_reduce(out=sprod[b % 2], in0=cs[b][:, NBAS:NBAS + D], in1=cs[b][:, NBAS + D:NBAS + 2 * D],
                                           scale=1.0, scalar=0.0, op0=ALU.mult, op1=ALU.add,
                                           accum_out=sums[:, b:b + 1])
                    tt(prod[b % 2].rearrange("p (b o) -> p b o", o=D), PWm[b % 2].rearrange("p (b o) -> p b o", o=D),
                       bc(cs[b][:, 0:NBAS]), ALU.mult).then_inc(s["l2_prod"], 1)
                    dve.wait_ge(s["l2_prod"], t + 3)
                    V.tensor_reduce(Z[:, bass.ds(t, 1), :], prod[b % 2].rearrange("p (b o) -> p o b", o=D),
                                    AX.X, ALU.add).then_inc(s["l2_done"], 1)
                V.tensor_copy(c["score"][:, bass.ds(4 * i, 4)], sums[:, 0:4]).then_inc(s["l2_scored"], 1)
            dve.wait_ge(s["l2_scored"], EC // 4 + 1)
            dve.wait_ge(s["l2_done"], EC)
            ts(col("score"), col("score"), float(D) ** -0.5, 0.0, ALU.mult, ALU.max).then_inc(s["gate_in"], 1)
            dve.wait_ge(s["gate_out"], 1)
            link(tt(M, Z, bc(col("sq_out")), ALU.mult))
            segment_sums(link, M, s["carry_in"], s["carry_out"], 2, F)
            dve.wait_ge(s["l2_cs"], EC)
            link(tt(Z, Z, CUR, ALU.add))
            link(V.scalar_tensor_tensor(out=XD, in0=Z, scalar=0.0, in1=XD, op0=ALU.max, op1=ALU.add))
            longest = dve.value_load(fits[0:1, 0:1], min_val=0, max_val=EC)
            with dve.If(longest <= GW):
                ch = Chain(dve, s["lc_chain"])
                rootc = roots("rootc_in", "rootc_out")
                ch(V.tensor_copy(OWNT[:, :, 0:D], XD))
                ch(V.tensor_copy(OWNT[:, :, D], col("dcnt")))
                ch(V.memset(ownc_f, 0.0))
                V.tensor_copy(OWNT[:, :, D + 1], col("dst_out")).then_inc(s["own_ready"], 1)
                layernorm(XD, F, Z, ch, rootc)
                ch(V.memset(Mc_f, 0.0))
                V.tensor_copy(small[:, 2:3], small[:, 3:4]).then_inc(s["first_zero"], 1)
                tt(Z, F, bc(col("dis")), ALU.mult).then_inc(s["uc_ready"], 1)
                V.scalar_tensor_tensor(out=XD, in0=F, scalar=ALPHA, in1=XD, op0=ALU.mult, op1=ALU.add).then_inc(s["dfull_ready"], 1)
                dve.wait_ge(s["uc_ready"], 1)
                dve.wait_ge(s["dfull_ready"], 1)
                ts(F, Z, ALPHA, None, ALU.mult).then_inc(s["uc_ready"], 1)
                dve.wait_ge(s["slots_in"], 16 * GW)
                V.tensor_copy(pf1, ac).then_inc(s["slots_ready"], 1)
                dve.wait_ge(s["slots_ready"], 1)
                dve.wait_ge(s["own_in"], 16 * GW)
                dve.wait_ge(s["own_stored"], 16)
                dve.wait_ge(s["u0_stored"], 16)
                dve.wait_ge(s["uc_stored"], 16)
                x3c = OWNC[:, :, 0:D]
                ch(ts(disc, OWNC[:, :, D], 1.0, None, ALU.max))
                rootc(ch, disc, disc, W)
                layernorm(x3c, Bc, Tc, ch, rootc, W)
                ch(V.scalar_tensor_tensor(out=x3c, in0=Bc, scalar=ALPHA, in1=x3c, op0=ALU.mult, op1=ALU.add))
                ch(V.scalar_tensor_tensor(out=Bc, in0=Bc, scalar=ALPHA, in1=bc(disc), op0=ALU.mult, op1=ALU.mult))
                ch(V.scalar_tensor_tensor(out=ac, in0=disc, scalar=1.0 - ALPHA, in1=disc, op0=ALU.mult, op1=ALU.mult))
                ch(tt(ahc, ac, headc, ALU.mult))
                base = ch.n
                PERC = D + 4
                with dve.Fori(0, L3_STEPS - 1) as i:
                    chl = Chain(dve, s["lc_chain"], base, i, PERC)
                    dve.wait_ge(s["mc_in"], 16 * GW * i + 16 * GW)
                    compact_sums(chl, i + 1)
                    chl(tt(Zc, Zc, bc(ac), ALU.mult))
                    chl(tt(Zc, Zc, Bc, ALU.add))
                    dve.wait_ge(s["lc_carry_out"], i + 1)
                    chl(tt(Tc, bf(CAR, W), bc(ahc), ALU.mult))
                    chl(tt(Uc, Zc, Tc, ALU.add))
                    V.tensor_copy(small[:, 2:3], small[:, 3:4]).then_inc(s["uc_ready"], 1)
                    assert chl.n == PERC
                ch = Chain(dve, s["lc_chain"], base + (L3_STEPS - 1) * PERC)
                ch(ts(disc, disc, 1.0 - ALPHA, None, ALU.mult))
                ch(tt(ahc, disc, headc, ALU.mult))
                ch(tt(nohome, nohome, OWNC[:, :, D + 1], ALU.add))
                ch(V.tensor_copy(homei, nohome))
                dve.wait_ge(s["mc_in"], 16 * GW * L3_STEPS)
                compact_sums(ch, L3_STEPS)
                ch(tt(Zc, Zc, bc(disc), ALU.mult))
                ch(tt(Zc, Zc, x3c, ALU.add))
                dve.wait_ge(s["lc_carry_out"], L3_STEPS)
                ch(tt(Tc, bf(CAR, W), bc(ahc), ALU.mult))
                tt(Oc, Zc, Tc, ALU.add).then_inc(s["dc_ready"], 1)
            with dve.Else():
                ch = Chain(dve, s["l3_chain"])
                layernorm(XD, F, Z, ch, roots("rootf_in", "rootf_out"))
                ch(tt(U, F, bc(col("dis")), ALU.mult))
                ch(V.memset(M_f, 0.0))
                V.tensor_copy(small[:, 2:3], small[:, 3:4]).then_inc(s["u3_ready"], 1)
                ch(ts(col("scalef"), col("dis"), 1.0 - ALPHA, None, ALU.mult))
                ch(ts(F, F, ALPHA, None, ALU.mult))
                base = ch.n
                PER3 = D + 2 + 3
                with dve.Fori(0, L3_STEPS) as i:
                    ch = Chain(dve, s["l3_chain"], base, i, PER3)
                    dve.wait_ge(s["m3_in"], 16 * EC * i + 16 * EC)
                    segment_sums(ch, M, s["carry3_in"], s["carry3_out"], i + 1, U)
                    ch(tt(Z, Z, bc(col("scalef")), ALU.mult))
                    ch(tt(Z, Z, F, ALU.add))
                    ch(tt(U, Z, bc(col("dis")), ALU.mult))
                    V.tensor_copy(small[:, 2:3], small[:, 3:4]).then_inc(s["u3_ready"], 1)
                    assert ch.n == PER3
                tt(XD, XD, Z, ALU.add).then_inc(s["d_final"], 1)

        @block.scalar
        def _(act):
            roots = [0]

            def root(n):
                for _ in range(n):
                    roots[0] += 1
                    act.wait_ge(s["root_in"], roots[0])
                    S.activation(col("sq_out"), col("sq_in"), ACT.Sqrt).then_inc(s["root_out"], 1)

            with act.Fori(0, EC // 4) as i:
                for b in range(4):
                    t = 4 * i + b
                    act.wait_ge(s["tile_turned"], t + 1)
                    S.copy(ot[b], TP[b % 2])
                    act.wait_ge(s["tile_free"], t + 2)
                    S.copy(rs[b % 2], R[:, 0:NCOL]).then_inc(s["tile_copied"], 1)
            root(3)
            xt = x[P * DROWS:N].rearrange("(p c) f -> p (c f)", p=TAIL_P)
            outt = out[P * DROWS:N].rearrange("(p c) f -> p (c f)", p=TAIL_P)
            xflat = x[0:P * DROWS].rearrange("(p q) f -> p (q f)", p=P)
            oflat = out[0:P * DROWS].rearrange("(p q) f -> p (q f)", p=P)

            def dense_act(nb, pn, cn, number):
                w = cn * D
                for l in range(3):
                    for b in range(nb):
                        act.wait_ge(s["dense_xc"], number(l, b))
                        S.activation(dsq[b][0:pn, 0:w], dxc[b][0:pn, 0:w], ACT.Square).then_inc(s["dense_sq"], 1)
                    for b in range(nb):
                        act.wait_ge(s["dense_var"], number(l, b))
                        S.activation(dst3[b][0:pn, 0:cn], dst2[b][0:pn, 0:cn], ACT.Sqrt).then_inc(s["dense_root"], 1)

            act.wait_ge(s["dense_go"], 1)
            act.dma_start(dx[0][0:TAIL_P, 0:TAIL_C * D], xt).then_inc(s["tail_in"], 16)
            dense_act(1, TAIL_P, TAIL_C, lambda l, b: l + 1)
            act.wait_ge(s["dense_done"], 1)
            act.dma_start(outt, dx[0][0:TAIL_P, 0:TAIL_C * D]).then_inc(s["dense_out"], 16)
            act.wait_ge(s["dense_out"], 16)
            for b in range(2):
                act.dma_start(dx[b], xflat[:, b * DW:(b + 1) * DW]).then_inc(s["dense_in0"], 16)

            def dense_turn(i, last):
                for h in range(2):
                    if not (last and h == 1):
                        act.wait_ge(s["dense_out"], 64 * i + 16 * (1 + 2 * h))
                        for b in range(2):
                            act.dma_start(dx[(2 * h + 2 + b) % 4],
                                          xflat[:, bass.ds(UNROLL * DW * i + DW * (2 * h + 2 + b), DW)]
                                          ).then_inc(s[f"dense_in{1 - h}"], 16)
                    dense_act(2, P, DCH, lambda l, b: 12 * i + (3 + 6 * h + 2 * l + b + 1))
                    for b in range(2):
                        act.wait_ge(s["dense_done"], 4 * i + (1 + 2 * h + b + 1))
                        act.dma_start(oflat[:, bass.ds(UNROLL * DW * i + DW * (2 * h + b), DW)],
                                      dx[2 * h + b]).then_inc(s["dense_out"], 16)

            with act.Fori(0, DCHUNKS // UNROLL - 1) as i:
                dense_turn(i, False)
            dense_turn(DCHUNKS // UNROLL - 1, True)
            root(2)
            root(1)
            root(1)
            root(1)
            root(1)
            root(1)
            act.wait_ge(s["h2src_in"], 16 * EC)
            act.wait_ge(s["l2_xin"], 1)
            for b in range(2):
                S.copy(xyc[b], XY[:, b, :]).then_inc(s["l2_xy"], 1)

            def turned(t, b):
                act.wait_ge(s["l2_tr"], t + 2)
                S.copy(xyt[b], XYTp[b % 2])
                S.copy(oht[b], OTp[b % 2]).then_inc(s["l2_tc"], 1)

            turned(0, 0)
            with act.Fori(0, EC // 4) as i:
                for b in range(4):
                    t = 4 * i + b
                    S.copy(xyc[(b + 2) % 4].unsqueeze(1), XY[:, bass.ds(t + 2, 1), :]).then_inc(s["l2_xy"], 1)
                    turned(t + 1, (b + 1) % 4)
                    act.wait_ge(s["l2_mm"], t + 1)
                    S.copy(XS[:, bass.ds(t, 1), :], PSm[b % 2][:, RC - D:RC].unsqueeze(1))
                    S.copy(cs[b][:, 0:RC - D], PSm[b % 2][:, 0:RC - D]).then_inc(s["l2_cs"], 1)
            act.wait_ge(s["gate_in"], 1)
            S.activation(col("sq_out"), col("score"), ACT.Tanh).then_inc(s["gate_out"], 1)
            longest = act.value_load(fits[0:1, 0:1], min_val=0, max_val=EC)

            def branch_roots(sin, sout, widths):
                for k, w in enumerate(widths):
                    act.wait_ge(s[sin], k + 1)
                    S.activation(c["sq_out"][:, 0:w], c["sq_in"][:, 0:w], ACT.Sqrt).then_inc(s[sout], 1)

            with act.If(longest <= GW):
                branch_roots("rootc_in", "rootc_out", [EC, W, W])
            with act.Else():
                branch_roots("rootf_in", "rootf_out", [EC])

        @block.tensor
        def _(pe):
            H0 = 512
            halves = ((0, H0), (H0, NCOL))

            def zeros(start, k):
                for a, b in halves:
                    ins = T.matmul(hist[k][:, a:b], z16[:, 0:P], z16[:, 0:b - a], start=start, stop=not start)
                return ins

            pe.wait_ge(s["pool_consts"], 1)
            pe.wait_ge(s["dve_setup"], 1)
            zeros(True, 0)
            zeros(True, 1).then_inc(s["hist_free"], 2)
            with pe.Fori(0, EC // 2) as i:
                for b in range(2):
                    pe.wait_ge(s["hist_built"], 2 * i + (b + 1))
                    for k in range(2):
                        op_, oc_ = onehot(2 * b + k)
                        for lo, hi in halves:
                            ins = T.matmul(hist[k][:, lo:hi], op_, oc_[:, lo:hi], start=False, stop=False)
                    ins.then_inc(s["hist_free"], 1)
            zeros(False, 0)
            zeros(False, 1).then_inc(s["hist_done"], 1)
            for k in range(2):
                pe.wait_ge(s["prefix_in"], k + 1)
                T.matmul(MISC[:, 0:1], upper[:], small[:, 0:1], start=True, stop=True).then_inc(s["prefix_out"], 1)
            pe.wait_ge(s["rec_ready"], 1)
            for lo, hi in halves:
                ins = T.matmul(R[:, lo:hi], ident[:], start_tab[:, lo:hi], start=True, stop=True, skip_group_check=True)
            ins.then_inc(s["tile_free"], 2)

            def turn(t, b):
                pe.wait_ge(s["tile_built"], t + 1)
                T.transpose(TP[b % 2], onehot(b)[0], ident16[:]).then_inc(s["tile_turned"], 1)

            turn(0, 0)
            with pe.Fori(0, EC // 4) as i:
                for b in range(4):
                    t = 4 * i + b
                    op_, oc_ = onehot(b)
                    pe.wait_ge(s["tile_copied"], t + 1)
                    for lo, hi in halves:
                        ins = T.matmul(R[:, lo:hi], op_, oc_[:, lo:hi], start=False, stop=True, skip_group_check=True)
                    ins.then_inc(s["tile_free"], 1)
                    turn(t + 1, (b + 1) % 4)
                    pe.wait_ge(s["tile_looked"], t + 1)
                    for lo, hi in halves:
                        T.matmul(LK[b % 2][:, lo:hi], ot[b], rs[b % 2][:, lo:hi], start=True, stop=True)
                    ins = T.matmul(KR[b % 2], key_col[:, b:b + 1].to_broadcast([P, P]), ident[:], start=True, stop=True)
                    ins.then_inc(s["tile_counted"], 1)

            def first_keys(k):
                pe.wait_ge(s["keys_in"], k)
                T.matmul(MISC, small[:, 0:1].to_broadcast([P, P]), ident[:], start=True, stop=True).then_inc(s["keys_out"], 1)

            def carry(ins, outs, number):
                pe.wait_ge(ins, number)
                T.matmul(CAR, wcarry[:], last_row[:], start=True, stop=True).then_inc(outs, 1)

            first_keys(1)
            carry(s["carry_in"], s["carry_out"], 1)
            with pe.Fori(0, L1_STEPS) as i:
                carry(s["carry1_in"], s["carry1_out"], i + 1)
            first_keys(2)
            pe.wait_ge(s["list_in"], 1)
            T.matmul(MISC, small[:, 3:4].to_broadcast([P, P]), ident[:], start=True, stop=True).then_inc(s["list_out"], 1)
            pe.wait_ge(s["list_in"], 2)
            T.matmul(MISC[:, 0:1], wcarry[:], small[:, 3:4], start=True, stop=True).then_inc(s["list_out"], 1)
            pe.wait_ge(s["list_in"], 3)
            T.transpose(MISC, wcarry[:], ident[:]).then_inc(s["list_out"], 1)
            pe.wait_ge(s["list_in"], 4)
            T.matmul(MISC[:, 0:1], wt, small[:, 3:4], start=True, stop=True).then_inc(s["list_out"], 1)
            pe.wait_ge(s["h2src_in"], 16 * EC)

            def l2_turn(t, b, ahead=1):
                pe.wait_ge(s["l2_oh"], t + 1)
                pe.wait_ge(s["l2_xy"], t + 1)
                T.transpose(OTp[b % 2], oh[b], ident[:])
                T.transpose(XYTp[b % 2], xyc[b], ident[:]).then_inc(s["l2_tr"], ahead)

            l2_turn(0, 0, 2)
            with pe.Fori(0, EC // 4) as i:
                for b in range(4):
                    t = 4 * i + b
                    l2_turn(t + 1, (b + 1) % 4)
                    pe.wait_ge(s["l2_tc"], t + 1)
                    pe.wait_ge(s["l2_prod"], t + 1)
                    T.matmul(PWm[b % 2], xyt[b][0:D, :], w_sb[:], start=True, stop=True)
                    T.matmul(PSm[b % 2], oht[b], rw_sb[:], start=True, stop=False)
                    T.matmul(PSm[b % 2], xyt[b], rxy_sb[:], start=False, stop=True).then_inc(s["l2_mm"], 1)
            carry(s["carry_in"], s["carry_out"], 2)
            longest = pe.value_load(fits[0:1, 0:1], min_val=0, max_val=EC)
            with pe.If(longest <= GW):
                with pe.Fori(0, L3_STEPS) as i:
                    pe.wait_ge(s["lc_carry_in"], i + 1)
                    T.matmul(CAR, wc[:], last_row[:], start=True, stop=True).then_inc(s["lc_carry_out"], 1)
            with pe.Else():
                with pe.Fori(0, L3_STEPS) as i:
                    carry(s["carry3_in"], s["carry3_out"], i + 1)


def kernel(x, src, dst, edge_type_86, L1_gnn_theta, L2_gnn_weight, L2_gnn_w_comp, L2_gnn_self_loop_weight,
           L2_gnn_A1_w, L2_gnn_A1_b, L2_gnn_A2_w, L2_gnn_A2_b, L2_gnn_rel_emb):
    import numpy as np
    import concourse.bacc as bacc
    from concourse.bass_utils import run_bass_kernel_spmd

    nc = bacc.Bacc("TRN2", target_bir_lowering=False, num_devices=1)
    given = {
        "x": x, "src": src, "dst": dst, "etype": edge_type_86, "theta": L1_gnn_theta,
        "w_basis": np.transpose(np.asarray(L2_gnn_weight), (1, 0, 2)), "w_comp": L2_gnn_w_comp,
        "w_self": L2_gnn_self_loop_weight, "a1t": np.transpose(np.asarray(L2_gnn_A1_w)), "a1b": L2_gnn_A1_b,
        "a2t": np.transpose(np.asarray(L2_gnn_A2_w)), "a2b": L2_gnn_A2_b, "rel": L2_gnn_rel_emb,
    }
    arrays, args = {}, {}
    for name, a in given.items():
        a = np.ascontiguousarray(a)
        arrays["in_" + name] = a
        args[name] = nc.dram_tensor("in_" + name, a.shape, mybir.dt.from_np(a.dtype), kind="ExternalInput").ap()
    args["out"] = nc.dram_tensor("out_0", (N, D), mybir.dt.float32, kind="ExternalOutput").ap()
    build(nc, **args)
    r = run_bass_kernel_spmd(nc, [arrays], core_ids=[0])
    return r.results[0]["out_0"]
```

```python
import concourse.bass as bass
from concourse import mybir
from contextlib import ExitStack

N = 100000
E = 25000
D = 32
NREL, NBAS = 86, 16
L1_STEPS, L3_STEPS = 4, 10
ALPHA = 0.1
EPS = 1e-5

P = 128
EC = -(-E // P)
EW = EC * D
NCOL = -(-N // P)
NPAD = P * NCOL
PADNODE = NPAD - 1
FAR = 1.0e6
MAGIC = 12582912.0
PAYLOAD = D + 4 + 4 + 1
W = 64
GW1, GW = 64, 60
SPLIT = 32768.0
OWNW = D + 2
LAST_ROWS = E - (P - 1) * EC

DCH = 39
DCHUNKS = 20
DROWS = DCH * DCHUNKS
TAIL_P, TAIL_C = 32, 5
assert P * DROWS + TAIL_P * TAIL_C == N
PAY_PARTS = ((0, 68), (68, EC))
L2_PARTS = ((0, 100), (100, EC))
L2_TURNS = ((0, 24), (24, EC // 4))
UNROLL = 4
TURNS = DCHUNKS // UNROLL
EARLY = 3


def build(nc, x, src, dst, etype, theta, w_basis, w_comp, w_self, a1t, a1b, a2t, a2b, rel, out):
    f32, f16, i32 = mybir.dt.float32, mybir.dt.float16, mybir.dt.int32
    ALU, ACT, AX = mybir.AluOpType, mybir.ActivationFunctionType, mybir.AxisListType
    V, S, T, G = nc.vector, nc.scalar, nc.tensor, nc.gpsimd

    rec_dram = nc.dram_tensor("node_records", (NPAD, 4), f32, kind="Internal").ap()
    pay_dram = nc.dram_tensor("payload_by_src", (P * EC, PAYLOAD), f32, kind="Internal").ap()
    u1_dram = nc.dram_tensor("l1_rows", (P * EC + P * W, D), f32, kind="Internal").ap()
    x2_dram = nc.dram_tensor("x2_rows", (P * EC, D), f32, kind="Internal").ap()
    own1_dram = nc.dram_tensor("l1_own_rows", (P * EC, OWNW), f32, kind="Internal").ap()
    map1_dram = nc.dram_tensor("l1_slots", (P * EC, 1), f32, kind="Internal").ap()
    u0_dram = nc.dram_tensor("l3_first_rows", (P * EC, D), f32, kind="Internal").ap()
    own_dram = nc.dram_tensor("l3_own_rows", (P * EC, OWNW), f32, kind="Internal").ap()
    map_dram = nc.dram_tensor("l3_slots", (P * EC, 1), f32, kind="Internal").ap()
    u3_dram = nc.dram_tensor("l3_rows", (P * EC + P * W, D), f32, kind="Internal").ap()

    ctx = ExitStack()
    with ctx:
        def sb(name, cols, dt=f32, parts=P):
            return ctx.enter_context(nc.sbuf_tensor(name, [parts, cols], dt))

        def sem(name):
            return ctx.enter_context(nc.semaphore(name))

        pay = sb("pay", EC * PAYLOAD)
        mf = sb("mf", 2 * EW + 4 * D)
        xd_t = sb("xd", EW)
        xs_t = sb("xs", EW)
        z_t = sb("z", EW)
        out_t = sb("outs", EW)

        def rows(ap):
            return ap.rearrange("p (c f) -> p c f", f=D)

        PAY = pay[:].rearrange("p (c w) -> p c w", w=PAYLOAD)
        M_f, F_f = mf[:, 0:EW], mf[:, EW:2 * EW]
        M, F = rows(M_f), rows(F_f)
        XY = mf[:].rearrange("p (c w) -> p c w", w=2 * D)
        XD, XS, Z, OUT = rows(xd_t[:]), rows(xs_t[:]), rows(z_t[:]), rows(out_t[:])
        U_f = pay[:, 0:EW]
        U = rows(U_f)

        names = ["kn", "kp0", "kc0", "et", "tmp", "tmp2", "st1", "st2", "sq_in", "sq_out", "linear", "cont", "head",
                 "dis", "nsrc", "scalef", "score", "dcnt"]
        c = {n: sb(n, EC + 4) for n in names}
        c["kp1"], c["kc1"] = c["dis"], c["scalef"]

        def col(n):
            return c[n][:, 0:EC]

        icols = {n: sb("i_" + n, EC, i32) for n in ["src", "dst", "et", "rank", "srcX", "dstX", "outD", "outS"]}
        icols["srcS"] = icols["src"]
        icols["l1"] = icols["rank"]
        icols["l3"] = icols["et"]

        c["own"] = c["kp0"]
        c["dst_out"] = c["scalef"]
        c["src_out"] = c["scalef"]
        c["src_count"] = c["score"]
        iota_c = sb("iota_c", NCOL, f16)
        lists = iota_c[:].bitcast(f32)
        listi = iota_c[:].bitcast(i32)
        extra = sb("extra", 3 * W)
        pf0, pf1, owni, homei = (listi[:, k * W:(k + 1) * W] for k in range(4))
        contc, headc = lists[:, 4 * W:5 * W], lists[:, 5 * W:6 * W]
        disc, ac, ahc = (c["kc0"][:, k * W:(k + 1) * W] for k in range(3))
        slotf, nohome = extra[:, 0:W], extra[:, W:2 * W]
        outSc = extra[:, 2 * W:3 * W].bitcast(i32)
        fits = sb("fits", 2, i32, 1)

        iota_p = sb("iota_p", P, f16)
        iota_r = sb("iota_r", NREL)
        ident = sb("ident", P)
        ident16 = sb("ident16", P, f16)
        upper = sb("upper", P)
        lower = sb("lower", P)
        wcarry = sb("wcarry", P)
        theta_sb = sb("theta_sb", L1_STEPS + 1)
        theta_sum = sb("theta_sum", 1)
        w_sb = sb("w_sb", NBAS * D, f32, 2 * D)
        RC = NBAS + 3 * D
        rw_sb = sb("rw_sb", RC, f32, NREL)
        rxy_sb = sb("rxy_sb", RC, f32, 4 * D)
        b2_sb = sb("b2_sb", D, f32, NREL)
        small = sb("small", 4)
        last_row = sb("last_row", D)
        idle = sb("idle", 3)
        key_col = sb("key_col", 4)
        sums = sb("sums", 8)

        h16 = z_t[:].bitcast(f16)
        ONEHOT_W = P + NCOL

        def onehot(b):
            o = b * ONEHOT_W
            return h16[:, o:o + P], h16[:, o + P:o + P + NCOL]

        z16 = h16[:, 4 * ONEHOT_W:4 * ONEHOT_W + 512]
        rs = [out_t[:, b * NCOL:(b + 1) * NCOL] for b in range(2)]
        start_tab = out_t[:, 2 * NCOL:3 * NCOL]
        scratch_b = [out_t[:, (3 + b) * NCOL:(4 + b) * NCOL] for b in range(2)]
        ot = [out_t[:, 5 * NCOL + b * P:5 * NCOL + (b + 1) * P] for b in range(4)]
        same = [out_t[:, 5 * NCOL + (4 + b) * P:5 * NCOL + (5 + b) * P] for b in range(2)]
        rec_sb = mf[:, 0:4 * NCOL]
        REC = rec_sb.rearrange("p (c w) -> p c w", w=4)
        cnt = mf[:, 4 * NCOL:5 * NCOL]
        inc = mf[:, 5 * NCOL:6 * NCOL]
        none = mf[:, 6 * NCOL:7 * NCOL]
        onesn = mf[:, 7 * NCOL:8 * NCOL]

        DW = DCH * D
        def chunks(tile):
            return [tile[:, b * DW:(b + 1) * DW] for b in range(4)]

        dense_x = [chunks(z_t), chunks(z_t), chunks(F_f)]

        def dense_temps(wide, narrow):
            return ([[wide[:, (2 * k + b) * DW:(2 * k + b + 1) * DW] for b in range(2)] for k in range(2)]
                    + [[narrow[:, (2 * k + b) * DCH:(2 * k + b + 1) * DCH] for b in range(2)] for k in range(3)])

        beside = pay[:, W * D:]
        temps = [dense_temps(out_t[:], mf[:]), dense_temps(pay[:], pay[:, 4 * DW:]),
                 dense_temps(beside, beside[:, 4 * DW:])]
        EARLY_IN, LATE_IN, BESIDE_IN = range(3)

        CW = W * D
        wc = lower
        Mc_f, Uc_f = mf[:, 0:CW], mf[:, CW:2 * CW]
        Mc, Uc, Bc = (rows(mf[:, k * CW:(k + 1) * CW]) for k in range(3))
        ownc_f = xs_t[:, 0:W * OWNW]
        OWNC = ownc_f.rearrange("p (q w) -> p q w", w=OWNW)
        Fc = rows(pay[:, 0:CW])
        Zc, Tc, Oc = (rows(z_t[:, k * CW:(k + 1) * CW]) for k in range(3))
        own1_f = mf[:, 2 * CW:2 * CW + W * OWNW]
        OWN1 = own1_f.rearrange("p (q w) -> p q w", w=OWNW)
        x4c_at = 4 * DW + 6 * DCH
        x4c = rows(pay[:, x4c_at:x4c_at + CW])
        ownt_f = pay[:, 0:EC * OWNW]
        OWNT = ownt_f.rearrange("p (c w) -> p c w", w=OWNW)
        wt = z_t[:, EW - P:EW]
        assert 4 * DW <= EW - P and 2 * CW + W * OWNW <= EW

        XY16 = mf[:].bitcast(f16).rearrange("p (c w) -> p c w", w=4 * D)
        pay16 = pay[:, 0:2 * NREL + 6 * P].bitcast(f16)
        oh = [pay16[:, b * NREL:(b + 1) * NREL] for b in range(4)]
        o1 = 4 * NREL
        xyt = [pay16[:, o1 + b * P:o1 + (b + 1) * P] for b in range(4)]
        o2 = o1 + 4 * P
        oht = [pay16[0:NREL, o2 + b * P:o2 + (b + 1) * P] for b in range(4)]
        o2 += 4 * P
        xyc = [pay16[:, o2 + b * P:o2 + (b + 1) * P] for b in range(4)]
        o3 = 2 * NREL + 6 * P
        cs = [pay[:, o3 + b * RC:o3 + (b + 1) * RC] for b in range(4)]
        o4 = o3 + 4 * RC
        prod = [pay[:, o4 + b * NBAS * D:o4 + (b + 1) * NBAS * D] for b in range(2)]
        o5 = o4 + 2 * NBAS * D
        o6 = o5 + 2 * D
        w16 = pay[:, o6:o6 + NBAS * D + 2 * RC].bitcast(f16)
        w_high, w_low = (w16[0:2 * D, k * NBAS * D:(k + 1) * NBAS * D] for k in range(2))
        o7 = 2 * NBAS * D
        rw_high, rw_low = (w16[0:NREL, o7 + k * RC:o7 + (k + 1) * RC] for k in range(2))
        rxy_high, rxy_low = (w16[:, o7 + (2 + k) * RC:o7 + (3 + k) * RC] for k in range(2))
        assert o6 + NBAS * D + 2 * RC <= x4c_at
        sprod = [pay[:, o5 + b * D:o5 + (b + 1) * D] for b in range(2)]

        ps = [ctx.enter_context(nc.psum_tensor(f"ps{k}", [P, 1024], f32)) for k in range(4)]
        hist = [ps[0], ps[1]]
        R = ps[0]
        LK = [ps[1], ps[2]]
        KR = [LK[b][:, NCOL:NCOL + P] for b in range(2)]
        TP = [ps[3][:, 512 * b:512 * b + 64].bitcast(f16) for b in range(2)]
        MISC = ps[3][:, 768:768 + P]
        CAR = ps[3][:, 768 + P:768 + P + D]
        PWm = [ps[0][:, 0:512], ps[0][:, 512:1024]]
        PSm = [ps[1][:, 0:RC], ps[1][:, 512:512 + RC]]
        XYTp = [ps[2][:, 512 * b:512 * b + P // 2].bitcast(f16) for b in range(2)]
        OTp = [ps[2][0:NREL, 512 * b + P:512 * b + P + P // 2].bitcast(f16) for b in range(2)]

        SEMS = """padded edges_in weights_in pool_filled pool_consts dve_setup dve
            hist_free hist_built hist_done prefix_in prefix_out rec_ready rec_stored
            tile_free tile_built tile_turned tile_copied tile_counted tile_looked ranked
            xdst_in rec_src_in rec_dst_in payload_ready records_kept payload_out payload_in srows_idx xsrc_in
            root_in root_out
            dense_go tail_in dense_in0 dense_in1 dense_xc dense_sq dense_var dense_root dense_done dense_out dense_chain
            keys_in keys_out carry_in carry_out carry1_in carry1_out carry3_in carry3_out
            u1_ready u1_stored m1_in l1_chain s2_ready s2_stored s_final
            x2src_in0 x2src_in1 x2dst_in0 x2dst_in1 l2_oh l2_xin l2_xy l2_tr l2_tc l2_mm l2_cs l2_prod l2_done l2_scored gate_in gate_out
            list_in list_out fits1_set maps_stored fits_set list_ready
            own1_ready own1_stored own1_in u1c_ready u1f_stored u1c_stored m1c_in l1c_chain l1c_carry_in l1c_carry_out
            map1_out slots1_in slots1_ready own1_zero x2c_ready x2c_out root1c_in root1c_out root1f_in root1f_out outsc_out
            own_ready own_stored own_in u0_stored uc_ready uc_stored mc_in lc_chain lc_carry_in lc_carry_out
            map_out slots_in slots_ready first_zero dfull_ready dfull_out dc_ready dc_out rootc_in rootc_out rootf_in rootf_out
            turn1 turn3 u3_ready u3_stored m3_in l3_chain d_final outs_scattered outd_scattered""".split()
        s = {n: sem(n) for n in SEMS}

        block = ctx.enter_context(nc.Block())

        class Chain:
            def __init__(self, eng, sm, base=0, loop=None, per=0):
                self.eng, self.sm, self.n, self.base, self.loop, self.per = eng, sm, 0, base, loop, per

            def at(self, n):
                v = self.base + n
                return v if self.loop is None else self.loop * self.per + v

            def __call__(self, ins):
                self.n += 1
                ins.then_inc(self.sm, 1)
                self.eng.wait_ge(self.sm, self.at(self.n))

            def many(self, inss):
                for ins in inss:
                    self.n += 1
                    ins.then_inc(self.sm, 1)
                self.eng.wait_ge(self.sm, self.at(self.n))

        def bc(ap, n=D):
            return ap.unsqueeze(2).to_broadcast([ap.shape[0], ap.shape[1], n])

        def bf(ap, n=EC):
            return ap.unsqueeze(1).to_broadcast([ap.shape[0], n, ap.shape[1]])

        @block.sync
        def _(sp):
            for tile, arr in ((icols["src"], src), (icols["dst"], dst), (icols["et"], etype)):
                sp.wait_ge(s["padded"], 1)
                full = P - 16
                sp.dma_start(tile[0:full, :], arr[0:full * EC].rearrange("(p c) -> p c", c=EC)).then_inc(s["edges_in"], 16)
                sp.dma_start(tile[full:P - 1, :],
                             arr[full * EC:(P - 1) * EC].rearrange("(p c) -> p c", c=EC)).then_inc(s["edges_in"], 16)
                sp.dma_start(tile[P - 1:P, 0:LAST_ROWS],
                             arr[(P - 1) * EC:E].rearrange("(p c) -> p c", p=1)).then_inc(s["edges_in"], 16)
            sp.wait_ge(s["dve_setup"], 1)
            for k in range(2):
                sp.dma_start(w_sb[k * D:(k + 1) * D, :], w_basis.rearrange("i b o -> i (b o)")).then_inc(s["weights_in"], 16)
                sp.dma_start(rxy_sb[k * D:(k + 1) * D, NBAS + D:NBAS + 2 * D], a1t).then_inc(s["weights_in"], 16)
                sp.dma_start(rxy_sb[k * D:(k + 1) * D, NBAS + 2 * D:RC], w_self).then_inc(s["weights_in"], 16)
                sp.dma_start(rxy_sb[(2 + k) * D:(3 + k) * D, NBAS:NBAS + D], a2t).then_inc(s["weights_in"], 16)
            sp.dma_start(rw_sb[:, 0:NBAS], w_comp).then_inc(s["weights_in"], 16)
            sp.dma_start(rw_sb[:, NBAS:NBAS + D], rel).then_inc(s["weights_in"], 16)
            sp.dma_start(rw_sb[:, NBAS + D:NBAS + 2 * D],
                         a1b.unsqueeze(0).to_broadcast([NREL, D])).then_inc(s["weights_in"], 16)
            sp.dma_start(b2_sb[:], a2b.unsqueeze(0).to_broadcast([NREL, D])).then_inc(s["weights_in"], 16)
            sp.dma_start(theta_sb[:], theta.unsqueeze(0).to_broadcast([P, L1_STEPS + 1])).then_inc(s["weights_in"], 16)
            sp.wait_ge(s["pool_consts"], 1)
            for m in (map1_dram, map_dram):
                sp.dma_start(m.rearrange("(p c) w -> p (c w)", p=P), col("linear")).then_inc(s["maps_stored"], 16)
            sp.wait_ge(s["rec_ready"], 1)
            sp.dma_start(rec_dram.rearrange("(p c) w -> p (c w)", p=P), rec_sb).then_inc(s["rec_stored"], 16)
            sp.wait_ge(s["payload_out"], 16 * EC)
            sp.wait_ge(s["records_kept"], 1)
            sp.dma_start(pay[:], pay_dram.rearrange("(p c) w -> p (c w)", p=P)).then_inc(s["payload_in"], 16)
            sp.wait_ge(s["fits1_set"], 1)
            longest = sp.value_load(fits[0:1, 0:1], min_val=0, max_val=EC)
            with sp.If(longest <= GW1):
                sp.wait_ge(s["own1_ready"], 1)
                sp.dma_start(own1_dram.rearrange("(p c) w -> p (c w)", p=P), ownt_f).then_inc(s["own1_stored"], 16)
                sp.wait_ge(s["u1c_ready"], 1)
                sp.dma_start(u1_dram[0:P * EC].rearrange("(p c) w -> p (c w)", p=P), out_t[:]).then_inc(s["u1f_stored"], 16)
                sp.wait_ge(s["s2_ready"], 1)
                sp.dma_start(x2_dram.rearrange("(p c) w -> p (c w)", p=P), xs_t[:]).then_inc(s["s2_stored"], 16)
                with sp.Fori(0, L1_STEPS - 1) as i:
                    sp.wait_ge(s["u1c_ready"], i + 2)
                    sp.dma_start(u1_dram[P * EC:P * EC + P * W].rearrange("(p c) w -> p (c w)", p=P),
                                 Uc_f).then_inc(s["u1c_stored"], 16)
            with sp.Else():
                with sp.Fori(0, L1_STEPS) as i:
                    sp.wait_ge(s["u1_ready"], i + 1)
                    sp.dma_start(u1_dram[0:P * EC].rearrange("(p c) w -> p (c w)", p=P), U_f).then_inc(s["u1_stored"], 16)
                sp.wait_ge(s["s2_ready"], 1)
                sp.dma_start(x2_dram.rearrange("(p c) w -> p (c w)", p=P), xs_t[:]).then_inc(s["s2_stored"], 16)
            sp.wait_ge(s["fits_set"], 1)
            longest = sp.value_load(fits[0:1, 1:2], min_val=0, max_val=EC)
            with sp.If(longest <= GW):
                sp.wait_ge(s["own_ready"], 1)
                sp.dma_start(own_dram.rearrange("(p c) w -> p (c w)", p=P), ownt_f).then_inc(s["own_stored"], 16)
                sp.wait_ge(s["uc_ready"], 1)
                sp.dma_start(u0_dram.rearrange("(p c) w -> p (c w)", p=P), z_t[:]).then_inc(s["u0_stored"], 16)
                sp.wait_ge(s["uc_ready"], 2)
                sp.dma_start(u3_dram[0:P * EC].rearrange("(p c) w -> p (c w)", p=P), F_f).then_inc(s["uc_stored"], 16)
                with sp.Fori(0, L3_STEPS - 1) as i:
                    sp.wait_ge(s["uc_ready"], i + 3)
                    sp.dma_start(u3_dram[P * EC:P * EC + P * W].rearrange("(p c) w -> p (c w)", p=P),
                                 Uc_f).then_inc(s["uc_stored"], 16)
            with sp.Else():
                with sp.Fori(0, L3_STEPS) as i:
                    sp.wait_ge(s["u3_ready"], i + 1)
                    sp.dma_start(u3_dram[0:P * EC].rearrange("(p c) w -> p (c w)", p=P), U_f).then_inc(s["u3_stored"], 16)

        @block.gpsimd
        def _(pool):
            def gather(dest, table, idx, bound, sm, n=EC, first=0):
                for k in range(first, first + n):
                    G.indirect_dma_start(out=dest(k), out_offset=None, in_=table,
                                         in_offset=bass.IndirectOffsetOnAxis(ap=idx[:, k:k + 1], axis=0),
                                         bounds_check=bound, oob_is_err=False).then_inc(sm, 16)

            def scatter(table, source, idx, bound, sm, n=EC, first=0):
                for k in range(first, first + n):
                    G.indirect_dma_start(out=table, out_offset=bass.IndirectOffsetOnAxis(ap=idx[:, k:k + 1], axis=0),
                                         in_=source(k), in_offset=None,
                                         bounds_check=bound, oob_is_err=False).then_inc(sm, 16)

            for k in ("src", "dst"):
                G.memset(icols[k][:], PADNODE)
            G.memset(icols["et"][:], 0).then_inc(s["padded"], 1)
            G.iota(iota_c[:], [[1, NCOL]], base=0, channel_multiplier=0, allow_small_or_imprecise_dtypes=True)
            G.iota(iota_p[:], [[1, P]], base=0, channel_multiplier=0, allow_small_or_imprecise_dtypes=True)
            G.iota(slotf, [[1, W]], base=P * EC, channel_multiplier=W, allow_small_or_imprecise_dtypes=True)
            G.iota(iota_r[:], [[1, NREL]], base=0, channel_multiplier=0, allow_small_or_imprecise_dtypes=True)
            G.iota(col("linear"), [[1, EC]], base=0, channel_multiplier=EC, allow_small_or_imprecise_dtypes=True)
            G.memset(ident[:], 0.0)
            G.memset(upper[:], 1.0)
            G.memset(idle[:], 0.0).then_inc(s["turn1"], 1)
            G.memset(ident16[:], 0.0).then_inc(s["turn3"], 1)
            G.memset(lower[:], 1.0).then_inc(s["pool_filled"], 1)
            pool.wait_ge(s["pool_filled"], 1)
            for t in (ident, ident16):
                G.affine_select(out=t[:], in_=t[:], compare_op=ALU.not_equal, fill=1.0, base=0,
                                pattern=[[-1, P]], channel_multiplier=1)
            G.affine_select(out=upper[:], in_=upper[:], compare_op=ALU.is_gt, fill=0.0, base=0,
                            pattern=[[1, P]], channel_multiplier=-1)
            G.affine_select(out=lower[:], in_=lower[:], compare_op=ALU.is_gt, fill=0.0, base=0,
                            pattern=[[-1, P]], channel_multiplier=1).then_inc(s["pool_consts"], 1)
            pool.wait_ge(s["edges_in"], 16 * 9)
            pool.wait_ge(s["dve"], 1)
            gather(lambda k: XD[:, k, :], x, icols["dst"], N - 1, s["xdst_in"])
            pool.wait_ge(s["rec_stored"], 16)
            gather(lambda k: PAY[:, k, D:D + 4], rec_dram, icols["src"], NPAD - 1, s["rec_src_in"])
            gather(lambda k: PAY[:, k, D + 4:D + 8], rec_dram, icols["dst"], NPAD - 1, s["rec_dst_in"])
            for part, (lo, hi) in enumerate(PAY_PARTS):
                pool.wait_ge(s["payload_ready"], part + 1)
                scatter(pay_dram, lambda k: PAY[:, k, :], icols["rank"], P * EC - 1, s["payload_out"], hi - lo, lo)
            pool.wait_ge(s["payload_in"], 16)
            G.tensor_copy(icols["srcS"][:], PAY[:, :, PAYLOAD - 1]).then_inc(s["srows_idx"], 1)
            pool.wait_ge(s["srows_idx"], 1)
            gather(lambda k: XS[:, k, :], x, icols["srcS"], N - 1, s["xsrc_in"])
            pool.wait_ge(s["fits1_set"], 1)
            longest = pool.value_load(fits[0:1, 0:1], min_val=0, max_val=EC)
            with pool.If(longest <= GW1):
                pool.wait_ge(s["maps_stored"], 32)
                scatter(map1_dram, lambda k: slotf[:, k:k + 1], homei, P * EC - 1, s["map1_out"], GW1)
                pool.wait_ge(s["map1_out"], 16 * GW1)
                gather(lambda k: ac[:, k:k + 1], map1_dram, pf0, P * EC - 1, s["slots1_in"], GW1)
                pool.wait_ge(s["own1_zero"], 1)
                pool.wait_ge(s["own1_stored"], 16)
                gather(lambda k: OWN1[:, k, :], own1_dram, owni, P * EC - 1, s["own1_in"], GW1)
                pool.wait_ge(s["u1f_stored"], 16)
                gather(lambda k: Mc[:, k, :], u1_dram[0:P * EC], pf0, P * EC - 1, s["m1c_in"], GW1)
                pool.wait_ge(s["slots1_ready"], 1)
                with pool.Fori(0, L1_STEPS - 1) as i:
                    pool.wait_ge(s["u1c_stored"], 16 * i + 16)
                    pool.wait_ge(s["turn1"], i + 1)
                    G.tensor_tensor(idle[:, 0:1], idle[:, 1:2], idle[:, 1:2], ALU.add).then_inc(s["turn1"], 1)
                    gather(lambda k: Mc[:, k, :], u1_dram, pf1, P * EC + P * W - 1, s["m1c_in"], GW1)
                pool.wait_ge(s["s2_stored"], 16)
                pool.wait_ge(s["x2c_ready"], 1)
                scatter(x2_dram, lambda k: Oc[:, k, :], homei, P * EC - 1, s["x2c_out"], GW1)
                pool.wait_ge(s["x2c_out"], 16 * GW1)
            with pool.Else():
                with pool.Fori(0, L1_STEPS) as i:
                    pool.wait_ge(s["u1_stored"], 16 * i + 16)
                    pool.wait_ge(s["turn1"], i + 1)
                    G.tensor_tensor(idle[:, 0:1], idle[:, 1:2], idle[:, 1:2], ALU.add).then_inc(s["turn1"], 1)
                    gather(lambda k: M[:, k, :], u1_dram[0:P * EC], icols["l1"], P * EC - 1, s["m1_in"])
                pool.wait_ge(s["s2_stored"], 16)
            pool.wait_ge(s["s_final"], 1)
            for part, (lo, hi) in enumerate(L2_PARTS):
                gather(lambda k: XY[:, k, 0:D], x2_dram, icols["srcX"], P * EC - 1, s[f"x2src_in{part}"], hi - lo, lo)
                gather(lambda k: XD[:, k, :], x2_dram, icols["dstX"], P * EC - 1, s[f"x2dst_in{part}"], hi - lo, lo)
            pool.wait_ge(s["dense_out"], 16 * (DCHUNKS + 1))
            scatter(out, lambda k: x4c[:, k, :], outSc, N - 1, s["outsc_out"], GW1)
            scatter(out, lambda k: OUT[:, k, :], icols["outS"], N - 1, s["outs_scattered"])
            pool.wait_ge(s["list_ready"], 1)
            longest = pool.value_load(fits[0:1, 1:2], min_val=0, max_val=EC)
            with pool.If(longest <= GW):
                pool.wait_ge(s["maps_stored"], 32)
                scatter(map_dram, lambda k: slotf[:, k:k + 1], homei, P * EC - 1, s["map_out"], GW)
                pool.wait_ge(s["map_out"], 16 * GW)
                gather(lambda k: ac[:, k:k + 1], map_dram, pf0, P * EC - 1, s["slots_in"], GW)
                pool.wait_ge(s["u0_stored"], 16)
                pool.wait_ge(s["first_zero"], 1)
                gather(lambda k: Mc[:, k, :], u0_dram, pf0, P * EC - 1, s["mc_in"], GW)
                pool.wait_ge(s["own_stored"], 16)
                gather(lambda k: OWNC[:, k, :], own_dram, owni, P * EC - 1, s["own_in"], GW)
                pool.wait_ge(s["dfull_ready"], 1)
                pool.wait_ge(s["slots_ready"], 1)
                fill = -(-EC // (L3_STEPS - 1))
                done = 0
                for k in range(1, L3_STEPS):
                    n = min(fill, EC - done)
                    scatter(out, lambda q: XD[:, q, :], icols["outD"], N - 1, s["dfull_out"], n, done)
                    done += n
                    pool.wait_ge(s["uc_stored"], 16 * (k + 1))
                    gather(lambda q: Mc[:, q, :], u3_dram, pf1, P * EC + P * W - 1, s["mc_in"], GW)
                assert done == EC
                pool.wait_ge(s["dc_ready"], 1)
                scatter(out, lambda k: Oc[:, k, :], homei, N - 1, s["dc_out"], GW)
                pool.wait_ge(s["dfull_out"], 16 * EC)
                pool.wait_ge(s["dc_out"], 16 * GW)
            with pool.Else():
                with pool.Fori(0, L3_STEPS) as i:
                    pool.wait_ge(s["u3_stored"], 16 * i + 16)
                    pool.wait_ge(s["turn3"], i + 1)
                    G.tensor_tensor(idle[:, 2:3], idle[:, 1:2], idle[:, 1:2], ALU.add).then_inc(s["turn3"], 1)
                    gather(lambda k: M[:, k, :], u3_dram[0:P * EC], icols["l3"], P * EC - 1, s["m3_in"])
                pool.wait_ge(s["d_final"], 1)
                scatter(out, lambda k: XD[:, k, :], icols["outD"], N - 1, s["outd_scattered"])
                pool.wait_ge(s["outd_scattered"], 16 * EC)
            pool.wait_ge(s["outs_scattered"], 16 * EC)
            pool.wait_ge(s["outsc_out"], 16 * GW1)

        @block.vector
        def _(dve):
            link = Chain(dve, s["dve"])

            def tt(o, a, b, op):
                return V.tensor_tensor(o, a, b, op)

            def ts(o, a, s1, s2, op0, op1=None):
                return V.tensor_scalar(o, a, s1, s2, op0, op1) if op1 is not None else V.tensor_scalar(o, a, s1, None, op0)

            def roots(sin, sout):
                count = [0]

                def root(chain, o, a, w=EC):
                    count[0] += 1
                    V.tensor_copy(c["sq_in"][:, 0:w], a).then_inc(s[sin], 1)
                    dve.wait_ge(s[sout], count[0])
                    chain(V.reciprocal(o, c["sq_out"][:, 0:w]))
                return root

            root_main = roots("root_in", "root_out")

            def layernorm(xin, hout, tmp, chain=link, root=root_main, w=EC):
                m, v = c["st1"][:, 0:w], c["st2"][:, 0:w]
                chain(V.tensor_reduce(m, xin, AX.X, ALU.add))
                chain(ts(m, m, 1.0 / D, None, ALU.mult))
                chain(tt(tmp, xin, bc(m), ALU.subtract))
                chain(tt(hout, tmp, tmp, ALU.mult))
                chain(V.tensor_reduce(v, hout, AX.X, ALU.add))
                chain(ts(v, v, 1.0 / D, EPS, ALU.mult, ALU.add))
                root(chain, m, v, w)
                chain(V.scalar_tensor_tensor(out=hout, in0=tmp, scalar=0.0, in1=bc(m), op0=ALU.max, op1=ALU.mult))

            def root(o, a):
                root_main(link, o, a)

            link(V.memset(xd_t[:], 0.0))
            link(V.memset(xs_t[:], 0.0))
            link(V.memset(z16, 0.0))
            link(V.memset(onesn, 1.0))
            for n in ("kp0", "kc0", "kn", "et"):
                link(V.memset(c[n][:], 0.0))
            link(V.memset(XY[:, EC:EC + 2, :], 0.0))
            link(V.memset(rxy_sb[:], 0.0))
            link(V.memset(rw_sb[:, NBAS + 2 * D:RC], 0.0))
            V.memset(small[:], 0.0).then_inc(s["dve_setup"], 1)
            dve.wait_ge(s["edges_in"], 16 * 9)
            dve.wait_ge(s["pool_consts"], 1)
            for k, name in enumerate(("src", "dst")):
                kp, kc = col(f"kp{k}"), col(f"kc{k}")
                link(V.tensor_copy(col("kn"), icols[name][:]))
                link(ts(kp, col("kn"), 1.0 / NCOL, 0.5 / NCOL - 0.5, ALU.mult, ALU.add))
                link(ts(kp, kp, MAGIC, None, ALU.add))
                link(ts(kp, kp, MAGIC, None, ALU.subtract))
                link(V.scalar_tensor_tensor(out=kc, in0=kp, scalar=-float(NCOL), in1=col("kn"), op0=ALU.mult, op1=ALU.add))
            link(V.tensor_copy(col("kn"), icols["src"][:]))
            link(V.tensor_copy(col("et"), icols["et"][:]))
            hist_keys = [("kp0", "kc0"), ("kp1", "kc1")]
            with dve.Fori(0, EC // 2) as i:
                for b in range(2):
                    t = 2 * i + b
                    dve.wait_ge(s["hist_free"], t + 1)
                    for k, (kp, kc) in enumerate(hist_keys):
                        op_, oc_ = onehot(2 * b + k)
                        V.tensor_scalar(op_, iota_p[:], c[kp][:, bass.ds(t, 1)], None, ALU.is_equal)
                        last = V.tensor_scalar(oc_, iota_c[:], c[kc][:, bass.ds(t, 1)], None, ALU.is_equal)
                    last.then_inc(s["hist_built"], 1)
            dve.wait_ge(s["hist_done"], 1)
            for k in range(2):
                link(V.tensor_copy(cnt, hist[k][:, 0:NCOL]))
                link(V.tensor_tensor_scan(inc, onesn, cnt, 0.0, ALU.mult, ALU.add))
                V.tensor_copy(small[:, 0:1], inc[:, NCOL - 1:NCOL]).then_inc(s["prefix_in"], 1)
                dve.wait_ge(s["prefix_out"], k + 1)
                link(V.tensor_copy(small[:, 1:2], MISC[:, 0:1]))
                link(ts(inc, inc, small[:, 1:2], None, ALU.add))
                if k == 0:
                    link(tt(start_tab, inc, cnt, ALU.subtract))
                link(ts(none, cnt, 0.0, FAR, ALU.is_equal, ALU.mult))
                link(V.scalar_tensor_tensor(out=REC[:, :, 2 * k], in0=inc, scalar=-1.0, in1=none, op0=ALU.add, op1=ALU.add))
                link(V.tensor_copy(REC[:, :, 2 * k + 1], cnt))
            V.memset(small[:, 2:3], 0.0).then_inc(s["rec_ready"], 1)
            def build_tile(t, b, freed):
                dve.wait_ge(s["tile_free"], freed)
                op_, oc_ = onehot(b)
                V.tensor_scalar(op_, iota_p[:], c["kp0"][:, bass.ds(t, 1)], None, ALU.is_equal)
                V.tensor_copy(key_col[:, b:b + 1], c["kn"][:, bass.ds(t, 1)])
                V.tensor_scalar(oc_, iota_c[:], c["kc0"][:, bass.ds(t, 1)], None, ALU.is_equal).then_inc(s["tile_built"], 1)

            build_tile(0, 0, 2)
            build_tile(1, 1, 2)
            link(V.memset(small[:, 3:4], 0.0))
            V.memset(small[:, 3:4], 0.0).then_inc(s["tile_looked"], 2)
            V.memset(small[:, 2:3], 0.0).then_inc(s["ranked"], 1)
            with dve.Fori(0, EC // 4) as i:
                for b in range(4):
                    t = 4 * i + b
                    dve.wait_ge(s["tile_looked"], t + 1)
                    build_tile(t + 2, (b + 2) % 4, t + 1)
                    if b == 0:
                        dve.wait_ge(s["ranked"], i + 1)
                    dve.wait_ge(s["tile_counted"], t + 1)
                    V.tensor_tensor_reduce(out=scratch_b[b % 2], in0=LK[b % 2][:, 0:NCOL], in1=onehot(b)[1], scale=1.0,
                                           scalar=0.0, op0=ALU.mult, op1=ALU.add, accum_out=sums[:, b:b + 1])
                    V.scalar_tensor_tensor(out=same[b % 2], in0=KR[b % 2], scalar=key_col[:, b:b + 1], in1=lower[:],
                                           op0=ALU.is_equal, op1=ALU.mult,
                                           accum_out=sums[:, 4 + b:5 + b]).then_inc(s["tile_looked"], 1)
                dve.wait_ge(s["tile_looked"], 4 * i + 6)
                tt(c["score"][:, bass.ds(4 * i, 4)], sums[:, 0:4], sums[:, 4:8], ALU.add).then_inc(s["ranked"], 1)
            dve.wait_ge(s["ranked"], EC // 4 + 1)
            link(V.tensor_copy(icols["rank"][:], col("score")))
            dve.wait_ge(s["xdst_in"], 16 * EC)
            dve.wait_ge(s["rec_src_in"], 16 * EC)
            dve.wait_ge(s["rec_dst_in"], 16 * EC)
            link(ts(col("tmp"), PAY[:, :, D + 5], 1.0, None, ALU.add))
            root(col("nsrc"), col("tmp"))
            link(V.tensor_copy(PAY[:, :, PAYLOAD - 1], col("kn")))
            for lo, hi in PAY_PARTS:
                layernorm(XD[:, lo:hi, :], OUT[:, lo:hi, :], Z[:, lo:hi, :], w=hi - lo)
                tt(PAY[:, lo:hi, 0:D], OUT[:, lo:hi, :], bc(col("nsrc")[:, lo:hi]), ALU.mult).then_inc(s["payload_ready"], 1)
            link(V.tensor_copy(icols["srcX"][:], PAY[:, :, D]))
            link(V.tensor_copy(icols["l3"][:], PAY[:, :, D + 2]))
            link(V.tensor_copy(icols["dstX"][:], PAY[:, :, D + 4]))
            link(tt(col("tmp"), PAY[:, :, D + 6], col("linear"), ALU.not_equal))
            link(V.tensor_copy(col("score"), icols["dst"][:]))
            link(V.scalar_tensor_tensor(out=icols["outD"][:], in0=col("tmp"), scalar=FAR, in1=col("score"), op0=ALU.mult, op1=ALU.add))
            link(V.tensor_copy(col("dcnt"), PAY[:, :, D + 7]))
            link(V.tensor_copy(col("own"), PAY[:, :, D + 6]))
            V.memset(small[:, 3:4], 0.0).then_inc(s["records_kept"], 1)
            link(tt(XD, XD, OUT, ALU.add))
            dve.wait_ge(s["weights_in"], 16 * 13)
            link(V.tensor_reduce(theta_sum[:], theta_sb[:], AX.X, ALU.add))
            link(tt(rw_sb[:, NBAS:NBAS + D], rw_sb[:, NBAS:NBAS + D], b2_sb[:], ALU.add))
            layernorm(XD, OUT, Z)
            link(V.scalar_tensor_tensor(out=XD, in0=OUT, scalar=theta_sum[:], in1=XD, op0=ALU.mult, op1=ALU.add))
            def dense_pair(slots, pn, cn, chain, number, place=EARLY_IN):
                nb = len(slots)
                w = cn * D
                dxc, dsq, dst1, dst2, dst3 = temps[place]
                X = [dense_x[place][sl][0:pn, 0:w] for sl in slots]
                for l in range(3):
                    for b in range(nb):
                        X3 = X[b].rearrange("p (c f) -> p c f", f=D)
                        chain(V.tensor_reduce(dst1[b][0:pn, 0:cn], X3, AX.X, ALU.add))
                        chain(ts(dst1[b][0:pn, 0:cn], dst1[b][0:pn, 0:cn], 1.0 / D, None, ALU.mult))
                        tt(rows(dxc[b][0:pn, 0:w]), X3, bc(dst1[b][0:pn, 0:cn]), ALU.subtract).then_inc(s["dense_xc"], 1)
                    for b in range(nb):
                        dve.wait_ge(s["dense_sq"], number(l, b))
                        chain(V.tensor_reduce(dst2[b][0:pn, 0:cn], rows(dsq[b][0:pn, 0:w]), AX.X, ALU.add))
                        ts(dst2[b][0:pn, 0:cn], dst2[b][0:pn, 0:cn], 1.0 / D, EPS, ALU.mult, ALU.add).then_inc(s["dense_var"], 1)
                    for b in range(nb):
                        X3 = X[b].rearrange("p (c f) -> p c f", f=D)
                        dve.wait_ge(s["dense_root"], number(l, b))
                        chain(V.reciprocal(dst1[b][0:pn, 0:cn], dst3[b][0:pn, 0:cn]))
                        if l == 1:
                            chain(ts(dst1[b][0:pn, 0:cn], dst1[b][0:pn, 0:cn], theta_sum[0:pn], None, ALU.mult))
                        if l == 2:
                            chain(ts(dst1[b][0:pn, 0:cn], dst1[b][0:pn, 0:cn], ALPHA, None, ALU.mult))
                        dve.wait_ge(s["dense_xc"], number(l, b))
                        chain(V.scalar_tensor_tensor(out=rows(dxc[b][0:pn, 0:w]), in0=rows(dxc[b][0:pn, 0:w]), scalar=0.0,
                                                     in1=bc(dst1[b][0:pn, 0:cn]), op0=ALU.max, op1=ALU.mult))
                        if l < 2:
                            chain(tt(X[b], X[b], dxc[b][0:pn, 0:w], ALU.add))
                        else:
                            tt(X[b], X[b], dxc[b][0:pn, 0:w], ALU.add).then_inc(s["dense_done"], 1)

            tail_chain = Chain(dve, s["dense_chain"])
            V.memset(small[:, 2:3], 0.0).then_inc(s["dense_go"], 1)
            dve.wait_ge(s["tail_in"], 16)
            dense_pair([0], TAIL_P, TAIL_C, tail_chain, lambda l, b: l + 1)
            dve.wait_ge(s["dense_done"], 1)
            PER = 2 * 2 * (3 * 5 + 2 + 2)

            def turn_half(i, h, chain, place):
                dve.wait_ge(s[f"dense_in{h}"], 32 * i + 32)
                dense_pair([2 * h, 2 * h + 1], P, DCH, chain, lambda l, b: 12 * i + (3 + 6 * h + 2 * l + b + 1), place)

            def dense_turns(first, last, place):
                with dve.Fori(first, last) as i:
                    ch = Chain(dve, s["dense_chain"], tail_chain.n, i, PER)
                    for h in range(2):
                        turn_half(i, h, ch, place)
                    assert ch.n == PER, ch.n
                dve.wait_ge(s["dense_done"], UNROLL * last + 1)

            dense_turns(0, EARLY, EARLY_IN)
            dve.wait_ge(s["payload_in"], 16)
            SRC, SEND_S, CNT_S, CNT_D = PAY[:, :, PAYLOAD - 1], PAY[:, :, D], PAY[:, :, D + 1], PAY[:, :, D + 3]
            link(V.tensor_copy(icols["l1"][:], PAY[:, :, D + 4]))
            link(tt(col("tmp"), SEND_S, col("linear"), ALU.not_equal))
            link(ts(col("tmp2"), CNT_D, 0.0, None, ALU.is_gt))
            link(tt(col("tmp"), col("tmp"), col("tmp2"), ALU.max))
            link(V.scalar_tensor_tensor(out=icols["outS"][:], in0=col("tmp"), scalar=FAR, in1=SRC, op0=ALU.mult, op1=ALU.add))
            link(V.tensor_copy(col("kn"), SRC))
            link(ts(col("scalef"), CNT_S, 1.0, None, ALU.add))
            root(col("nsrc"), col("scalef"))
            link(V.tensor_copy(col("scalef"), CNT_S))
            root(col("dis"), col("scalef"))
            link(V.tensor_copy(col("src_count"), CNT_S))
            link(V.scalar_tensor_tensor(out=col("src_out"), in0=col("tmp2"), scalar=FAR, in1=SRC, op0=ALU.mult, op1=ALU.add))

            seg = [0]

            def segments():
                seg[0] += 1
                kn = col("kn")
                link(V.memset(c["cont"][:], 0.0))
                link(tt(c["cont"][:, 1:EC], kn[:, 1:EC], kn[:, 0:EC - 1], ALU.is_equal))
                link(ts(col("head"), kn, kn[:, 0:1], None, ALU.is_equal))
                V.tensor_copy(small[:, 0:1], kn[:, 0:1]).then_inc(s["keys_in"], 1)
                dve.wait_ge(s["keys_out"], seg[0])
                link(V.scalar_tensor_tensor(out=wcarry[:], in0=MISC, scalar=kn[:, EC - 1:EC], in1=upper[:],
                                            op0=ALU.is_equal, op1=ALU.mult))

            def segment_sums(chain, m, ins, outs, number, tmp):
                chain.many([V.tensor_tensor_scan(Z[:, :, f], col("cont"), m[:, :, f], 0.0, ALU.mult, ALU.add)
                            for f in range(D)])
                V.tensor_copy(last_row[:], Z[:, EC - 1, :]).then_inc(ins, 1)
                dve.wait_ge(outs, number)
                chain(tt(tmp, bf(CAR), bc(col("head")), ALU.mult))
                chain(tt(Z, Z, tmp, ALU.add))

            listed = [0]

            def ask(column):
                listed[0] += 1
                V.tensor_copy(small[:, 3:4], column).then_inc(s["list_in"], 1)
                dve.wait_ge(s["list_out"], listed[0])

            def compact(ptr, own, outi, k, most):
                last8 = slice(EC, EC + 4)
                rev, act, code, vals = c["tmp"], c["tmp2"], c["st1"], c["st2"][:, 0:W]
                valid, ownf, aux, keep = (c["sq_out"][:, 0:W], c["sq_out"][:, W:2 * W], c["sq_out"][:, 2 * W:3 * W],
                                          c["st2"][:, W:2 * W])
                lin = col("linear")
                link(ts(rev[:, 0:EC], lin, lin[:, 0:1], -1.0, ALU.subtract, ALU.mult))
                link(ts(rev[:, 0:EC], rev[:, 0:EC], float(EC), SPLIT, ALU.add, ALU.mult))
                link(ts(act[:, 0:EC], ptr, FAR / 2, None, ALU.is_lt))
                link(V.scalar_tensor_tensor(out=act[:, 0:EC], in0=lin, scalar=E - 0.5, in1=act[:, 0:EC],
                                            op0=ALU.is_lt, op1=ALU.mult))
                link(V.tensor_reduce(small[:, 0:1], act[:, 0:EC], AX.X, ALU.add))
                ask(small[:, 0:1])
                link(V.tensor_reduce(small[:, 1:2], MISC, AX.X, ALU.max))
                link(ts(small[:, 0:1], small[:, 1:2], most + 0.5, FAR, ALU.is_lt, ALU.mult))
                link(V.tensor_copy(fits[0:1, k:k + 1], small[0:1, 1:2]))
                link(V.tensor_tensor_scan(code[:, 0:EC], col("cont"), act[:, 0:EC], 0.0, ALU.mult, ALU.add))
                ask(code[:, EC - 1:EC])
                link(V.tensor_copy(small[:, 1:2], MISC[:, 0:1]))
                link(V.scalar_tensor_tensor(out=code[:, 0:EC], in0=col("head"), scalar=small[:, 1:2], in1=code[:, 0:EC],
                                            op0=ALU.mult, op1=ALU.add))
                link(ts(code[:, 0:EC], code[:, 0:EC], 0.0, small[:, 0:1], ALU.is_gt, ALU.mult))
                link(V.tensor_copy(col("sq_in"), outi))
                link(tt(col("sq_in"), col("sq_in"), code[:, 0:EC], ALU.add))
                link(V.tensor_copy(outi, col("sq_in")))

                def extract(value, idx):
                    link(V.memset(code[:, last8], 0.0))
                    link(tt(code[:, 0:EC], rev[:, 0:EC], value, ALU.add))
                    link(tt(code[:, 0:EC], code[:, 0:EC], act[:, 0:EC], ALU.mult))
                    for r in range(W // 8):
                        link(V.max(out=vals[:, 8 * r:8 * r + 8], in_=code[:]))
                        link(V.match_replace(out=code[:], in_to_replace=vals[:, 8 * r:8 * r + 8], in_values=code[:],
                                             imm_value=0.0))
                    link(ts(aux, vals, 1.0 / SPLIT, -0.4, ALU.mult, ALU.add))
                    link(ts(aux, aux, MAGIC, None, ALU.add))
                    link(ts(aux, aux, MAGIC, None, ALU.subtract))
                    link(V.scalar_tensor_tensor(out=ownf, in0=aux, scalar=-SPLIT, in1=vals, op0=ALU.mult, op1=ALU.add))
                    link(ts(valid, vals, 0.0, None, ALU.is_gt))
                    link(ts(aux, vals, 0.0, FAR, ALU.is_le, ALU.mult))
                    link(tt(idx, ownf, aux, ALU.add))

                extract(ptr, pf0)
                extract(own, owni)
                link(V.scalar_tensor_tensor(out=keep, in0=valid, scalar=-1.0, in1=ownf, op0=ALU.add, op1=ALU.add))
                link(V.memset(contc, 0.0))
                link(tt(contc[:, 1:W], keep[:, 1:W], keep[:, 0:W - 1], ALU.is_equal))
                link(ts(headc, keep, own[:, 0:1], None, ALU.is_equal))
                link(V.tensor_reduce(small[:, 0:1], keep, AX.X, ALU.max))
                link(tt(small[:, 0:1], small[:, 0:1], own[:, EC - 1:EC], ALU.is_equal))
                link(V.tensor_reduce(small[:, 1:2], headc, AX.X, ALU.max))
                ask(small[:, 1:2])
                link(V.tensor_copy(wt, MISC))
                ask(small[:, 1:2])
                link(ts(small[:, 2:3], MISC[:, 0:1], 0.0, None, ALU.is_gt))
                link(ts(wc[:], wcarry[:], small[:, 0:1], None, ALU.mult))
                link(V.tensor_copy(small[:, 1:2], own[:, EC - 1:EC]))
                link(ts(aux, keep, small[:, 1:2], small[:, 2:3], ALU.is_equal, ALU.mult))
                link(tt(aux[:, 0:W - 1], aux[:, 0:W - 1], contc[:, 1:W], ALU.max))
                link(tt(aux, valid, aux, ALU.is_gt))
                link(ts(nohome, aux, -FAR, FAR, ALU.mult, ALU.add))
                link(tt(homei, ownf, nohome, ALU.add))
                link(ts(aux, valid, -1.0, 1.0, ALU.mult, ALU.add))
                link(tt(contc[:, 1:W], contc[:, 1:W], aux[:, 1:W], ALU.max))
                link(V.memset(ac, 2 * FAR))

            def compact_sums(chain, ins, number):
                chain.many([V.tensor_tensor_scan(Zc[:, :, f], contc, Mc[:, :, f], 0.0, ALU.mult, ALU.add)
                            for f in range(D)])
                V.tensor_copy(last_row[:], Zc[:, W - 1, :]).then_inc(s[ins], 1)
                dve.wait_ge(s[ins], number)

            segments()
            dve.wait_ge(s["dense_out"], 16 * (UNROLL * EARLY + 1))
            compact(PAY[:, :, D + 4], SEND_S, icols["outS"][:], 0, GW1)
            V.tensor_copy(small[:, 2:3], small[:, 1:2]).then_inc(s["fits1_set"], 1)
            segment_sums(link, PAY[:, :, 0:D], s["carry_in"], s["carry_out"], 1, OUT)
            dve.wait_ge(s["xsrc_in"], 16 * EC)
            layernorm(XS, F, OUT)
            link(tt(OUT, F, bc(col("nsrc")), ALU.mult))
            link(tt(Z, Z, OUT, ALU.add))
            link(tt(Z, Z, bc(col("nsrc")), ALU.mult))
            link(tt(XS, XS, Z, ALU.add))
            longest = dve.value_load(fits[0:1, 0:1], min_val=0, max_val=EC)
            with dve.If(longest <= GW1):
                ch = Chain(dve, s["l1c_chain"])
                rootc = roots("root1c_in", "root1c_out")
                ch(V.tensor_copy(OWNT[:, :, 0:D], XS))
                ch(V.tensor_copy(OWNT[:, :, D], col("src_count")))
                V.tensor_copy(OWNT[:, :, D + 1], col("src_out")).then_inc(s["own1_ready"], 1)
                ch(V.memset(Mc_f, 0.0))
                V.memset(own1_f, 0.0).then_inc(s["own1_zero"], 1)
                layernorm(XS, F, Z, ch, rootc)
                tt(OUT, F, bc(col("dis")), ALU.mult).then_inc(s["u1c_ready"], 1)
                ch(V.scalar_tensor_tensor(out=XS, in0=F, scalar=theta_sum[:], in1=XS, op0=ALU.mult, op1=ALU.add))
                V.tensor_copy(small[:, 2:3], small[:, 3:4]).then_inc(s["s2_ready"], 1)
                dve.wait_ge(s["u1c_ready"], 1)
                layernorm(XS, F, Z, ch, rootc)
                dve.wait_ge(s["u1f_stored"], 16)
                ch(V.scalar_tensor_tensor(out=OUT, in0=F, scalar=ALPHA, in1=XS, op0=ALU.mult, op1=ALU.add))
                dve.wait_ge(s["slots1_in"], 16 * GW1)
                V.tensor_copy(pf1, ac).then_inc(s["slots1_ready"], 1)
                dve.wait_ge(s["own1_stored"], 16)
                dve.wait_ge(s["own1_in"], 16 * GW1)
                x1c = OWN1[:, :, 0:D]
                ch(ts(disc, OWN1[:, :, D], 1.0, None, ALU.max))
                rootc(ch, disc, disc, W)
                layernorm(x1c, Fc, Tc, ch, rootc, W)
                ch(ts(Oc, Fc, theta_sb[:, 0:1], None, ALU.mult))
                base = ch.n
                PER1C = D + 6
                V.memset(small[:, 2:3], 0.0).then_inc(s["dense_go"], 1)

                def l1_step(i):
                    chl = Chain(dve, s["l1c_chain"], base, i, PER1C)
                    dve.wait_ge(s["m1c_in"], 16 * GW1 * i + 16 * GW1)
                    compact_sums(chl, "l1c_carry_in", i + 1)
                    dve.wait_ge(s["l1c_carry_out"], i + 1)
                    chl(tt(Tc, bf(CAR, W), bc(headc), ALU.mult))
                    chl(tt(Zc, Zc, Tc, ALU.add))
                    chl(tt(Zc, Zc, bc(disc), ALU.mult))
                    chl(tt(Fc, Fc, Zc, ALU.subtract))
                    chl(tt(Uc, Fc, bc(disc), ALU.mult))
                    V.tensor_copy(small[:, 2:3], small[:, 3:4]).then_inc(s["u1c_ready"], 1)
                    chl(V.scalar_tensor_tensor(out=Oc, in0=Fc, scalar=theta_sb[:, bass.ds(i + 1, 1)], in1=Oc,
                                               op0=ALU.mult, op1=ALU.add))
                    assert chl.n == PER1C

                side = Chain(dve, s["dense_chain"], tail_chain.n, EARLY, PER)
                for h in range(2):
                    l1_step(h)
                    turn_half(EARLY, h, side, BESIDE_IN)
                with dve.Fori(2, L1_STEPS) as i:
                    l1_step(i)
                dve.wait_ge(s["dense_done"], UNROLL * (EARLY + 1) + 1)
                dve.wait_ge(s["dense_out"], 16 * (UNROLL * (EARLY + 1) + 1))
                ch = Chain(dve, s["l1c_chain"], base + L1_STEPS * PER1C)
                ch(tt(Oc, Oc, x1c, ALU.add))
                V.tensor_copy(small[:, 2:3], small[:, 3:4]).then_inc(s["x2c_ready"], 1)
                layernorm(Oc, Fc, Tc, ch, rootc, W)
                ch(V.scalar_tensor_tensor(out=x4c, in0=Fc, scalar=ALPHA, in1=Oc, op0=ALU.mult, op1=ALU.add))
                ch(tt(nohome, nohome, OWN1[:, :, D + 1], ALU.add))
                V.tensor_copy(outSc, nohome).then_inc(s["s_final"], 1)
                dve.wait_ge(s["x2c_out"], 16 * GW1)
                dve.wait_ge(s["s_final"], 1)
                V.memset(small[:, 2:3], 0.0).then_inc(s["dense_go"], 1)
                dense_turns(EARLY + 1, TURNS, LATE_IN)
            with dve.Else():
                ch = Chain(dve, s["l1_chain"])
                rootf = roots("root1f_in", "root1f_out")
                layernorm(XS, F, Z, ch, rootf)
                ch(V.memset(M_f, 0.0))
                ch(tt(U, F, bc(col("dis")), ALU.mult))
                V.tensor_copy(small[:, 2:3], small[:, 3:4]).then_inc(s["u1_ready"], 1)
                ch(ts(OUT, F, theta_sb[:, 0:1], None, ALU.mult))
                base = ch.n
                PER1 = D + 2 + 4
                with dve.Fori(0, L1_STEPS) as i:
                    chl = Chain(dve, s["l1_chain"], base, i, PER1)
                    dve.wait_ge(s["m1_in"], 16 * EC * i + 16 * EC)
                    segment_sums(chl, M, s["carry1_in"], s["carry1_out"], i + 1, U)
                    chl(tt(Z, Z, bc(col("dis")), ALU.mult))
                    chl(tt(F, F, Z, ALU.subtract))
                    chl(tt(U, F, bc(col("dis")), ALU.mult))
                    V.tensor_copy(small[:, 2:3], small[:, 3:4]).then_inc(s["u1_ready"], 1)
                    chl(V.scalar_tensor_tensor(out=OUT, in0=F, scalar=theta_sb[:, bass.ds(i + 1, 1)], in1=OUT,
                                               op0=ALU.mult, op1=ALU.add))
                    assert chl.n == PER1
                ch = Chain(dve, s["l1_chain"], base + L1_STEPS * PER1)
                ch(tt(XS, XS, OUT, ALU.add))
                V.tensor_copy(small[:, 2:3], small[:, 3:4]).then_inc(s["s2_ready"], 1)
                layernorm(XS, F, Z, ch, rootf)
                ch(V.scalar_tensor_tensor(out=OUT, in0=F, scalar=ALPHA, in1=XS, op0=ALU.mult, op1=ALU.add))
                ch(V.memset(nohome, 2 * FAR))
                V.tensor_copy(outSc, nohome).then_inc(s["s_final"], 1)
                dve.wait_ge(s["u1_stored"], 16 * L1_STEPS)
                dve.wait_ge(s["s2_ready"], 1)
                dve.wait_ge(s["s_final"], 1)
                V.memset(small[:, 2:3], 0.0).then_inc(s["dense_go"], 1)
                dense_turns(EARLY, TURNS, LATE_IN)
            link(V.tensor_copy(col("kn"), icols["dst"][:]))
            segments()
            root(col("dis"), col("dcnt"))
            link(V.tensor_copy(col("dst_out"), icols["outD"][:]))
            link(V.tensor_copy(col("nsrc"), icols["l3"][:]))
            compact(col("nsrc"), col("own"), icols["outD"][:], 1, GW)
            V.tensor_copy(small[:, 3:4], small[:, 1:2]).then_inc(s["fits_set"], 1)
            V.tensor_copy(small[:, 2:3], small[:, 1:2]).then_inc(s["list_ready"], 1)
            dve.wait_ge(s["dense_out"], 16 * (DCHUNKS + 1))
            dve.wait_ge(s["s2_stored"], 16)

            def halves_of(high, low, whole):
                link(V.tensor_copy(high, whole))
                link(tt(low, whole, high, ALU.subtract))

            halves_of(w_high, w_low, w_sb[:])
            halves_of(rw_high, rw_low, rw_sb[:])
            halves_of(rxy_high, rxy_low, rxy_sb[:])

            def l2_inputs(part):
                lo, hi = L2_PARTS[part]
                w = hi - lo
                xy, xy16, z, xd = XY[:, lo:hi, :], XY16[:, lo:hi, :], Z[:, lo:hi, :], XD[:, lo:hi, :]
                dve.wait_ge(s[f"x2src_in{part}"], 16 * w)
                layernorm(xy[:, :, 0:D], xy[:, :, D:2 * D], z, w=w)
                halves_of(xy16[:, :, 0:D], xy16[:, :, D:2 * D], xy[:, :, D:2 * D])
                dve.wait_ge(s[f"x2dst_in{part}"], 16 * w)
                layernorm(xd, z, xy[:, :, D:2 * D], w=w)
                halves_of(xy16[:, :, 2 * D:3 * D], xy16[:, :, 3 * D:4 * D], z)
                V.tensor_copy(small[:, 2:3], small[:, 3:4]).then_inc(s["l2_xin"], 1)

            l2_inputs(0)

            def build_types(t, b):
                V.tensor_scalar(oh[b], iota_r[:], c["et"][:, bass.ds(t, 1)], None, ALU.is_equal).then_inc(s["l2_oh"], 1)

            CUR = XS
            V.memset(sums[:, 7:8], 0.0).then_inc(s["l2_prod"], 2)
            V.memset(sums[:, 6:7], 0.0).then_inc(s["l2_scored"], 1)
            V.memset(sums[:, 5:6], 0.0).then_inc(s["l2_done"], 2)
            build_types(0, 0)
            build_types(1, 1)

            def add_bases(t, slot):
                dve.wait_ge(s["l2_prod"], t + 3)
                V.tensor_reduce(Z[:, bass.ds(t, 1), :], prod[slot].rearrange("p (b o) -> p o b", o=D),
                                AX.X, ALU.add).then_inc(s["l2_done"], 1)

            def l2_turns(first, last):
                with dve.Fori(first, last) as i:
                    for b in range(4):
                        t = 4 * i + b
                        dve.wait_ge(s["l2_tr"], t + 1)
                        build_types(t + 2, (b + 2) % 4)
                        if b == 0:
                            dve.wait_ge(s["l2_scored"], i + 1)
                        dve.wait_ge(s["l2_cs"], t + 1)
                        V.tensor_tensor_reduce(out=sprod[b % 2], in0=cs[b][:, NBAS:NBAS + D], in1=cs[b][:, NBAS + D:NBAS + 2 * D],
                                               scale=1.0, scalar=0.0, op0=ALU.mult, op1=ALU.add,
                                               accum_out=sums[:, b:b + 1])
                        dve.wait_ge(s["l2_done"], t + 1)
                        tt(prod[b % 2].rearrange("p (b o) -> p b o", o=D), PWm[b % 2].rearrange("p (b o) -> p b o", o=D),
                           bc(cs[b][:, 0:NBAS]), ALU.mult).then_inc(s["l2_prod"], 1)
                        if b > 0:
                            add_bases(t - 1, (b - 1) % 2)
                    add_bases(4 * i + 3, 1)
                    V.tensor_copy(c["score"][:, bass.ds(4 * i, 4)], sums[:, 0:4]).then_inc(s["l2_scored"], 1)

            l2_turns(*L2_TURNS[0])
            l2_inputs(1)
            l2_turns(*L2_TURNS[1])
            dve.wait_ge(s["l2_scored"], EC // 4 + 1)
            dve.wait_ge(s["l2_done"], EC + 2)
            ts(col("score"), col("score"), float(D) ** -0.5, 0.0, ALU.mult, ALU.max).then_inc(s["gate_in"], 1)
            dve.wait_ge(s["gate_out"], 1)
            link(tt(M, Z, bc(col("sq_out")), ALU.mult))
            segment_sums(link, M, s["carry_in"], s["carry_out"], 2, F)
            dve.wait_ge(s["l2_cs"], EC)
            link(tt(Z, Z, CUR, ALU.add))
            link(V.scalar_tensor_tensor(out=XD, in0=Z, scalar=0.0, in1=XD, op0=ALU.max, op1=ALU.add))
            dve.wait_ge(s["outsc_out"], 16 * GW1)
            longest = dve.value_load(fits[0:1, 1:2], min_val=0, max_val=EC)
            with dve.If(longest <= GW):
                ch = Chain(dve, s["lc_chain"])
                rootc = roots("rootc_in", "rootc_out")
                ch(V.tensor_copy(OWNT[:, :, 0:D], XD))
                ch(V.tensor_copy(OWNT[:, :, D], col("dcnt")))
                ch(V.memset(ownc_f, 0.0))
                V.tensor_copy(OWNT[:, :, D + 1], col("dst_out")).then_inc(s["own_ready"], 1)
                layernorm(XD, F, Z, ch, rootc)
                ch(V.memset(Mc_f, 0.0))
                V.tensor_copy(small[:, 2:3], small[:, 3:4]).then_inc(s["first_zero"], 1)
                tt(Z, F, bc(col("dis")), ALU.mult).then_inc(s["uc_ready"], 1)
                V.scalar_tensor_tensor(out=XD, in0=F, scalar=ALPHA, in1=XD, op0=ALU.mult, op1=ALU.add).then_inc(s["dfull_ready"], 1)
                dve.wait_ge(s["uc_ready"], 1)
                dve.wait_ge(s["dfull_ready"], 1)
                ts(F, Z, ALPHA, None, ALU.mult).then_inc(s["uc_ready"], 1)
                dve.wait_ge(s["slots_in"], 16 * GW)
                V.tensor_copy(pf1, ac).then_inc(s["slots_ready"], 1)
                dve.wait_ge(s["slots_ready"], 1)
                dve.wait_ge(s["own_in"], 16 * GW)
                dve.wait_ge(s["own_stored"], 16)
                dve.wait_ge(s["u0_stored"], 16)
                dve.wait_ge(s["uc_stored"], 16)
                x3c = OWNC[:, :, 0:D]
                ch(ts(disc, OWNC[:, :, D], 1.0, None, ALU.max))
                rootc(ch, disc, disc, W)
                layernorm(x3c, Bc, Tc, ch, rootc, W)
                ch(V.scalar_tensor_tensor(out=x3c, in0=Bc, scalar=ALPHA, in1=x3c, op0=ALU.mult, op1=ALU.add))
                ch(V.scalar_tensor_tensor(out=Bc, in0=Bc, scalar=ALPHA, in1=bc(disc), op0=ALU.mult, op1=ALU.mult))
                ch(V.scalar_tensor_tensor(out=ac, in0=disc, scalar=1.0 - ALPHA, in1=disc, op0=ALU.mult, op1=ALU.mult))
                ch(tt(ahc, ac, headc, ALU.mult))
                base = ch.n
                PERC = D + 4
                with dve.Fori(0, L3_STEPS - 1) as i:
                    chl = Chain(dve, s["lc_chain"], base, i, PERC)
                    dve.wait_ge(s["mc_in"], 16 * GW * i + 16 * GW)
                    compact_sums(chl, "lc_carry_in", i + 1)
                    chl(tt(Zc, Zc, bc(ac), ALU.mult))
                    chl(tt(Zc, Zc, Bc, ALU.add))
                    dve.wait_ge(s["lc_carry_out"], i + 1)
                    chl(tt(Tc, bf(CAR, W), bc(ahc), ALU.mult))
                    chl(tt(Uc, Zc, Tc, ALU.add))
                    V.tensor_copy(small[:, 2:3], small[:, 3:4]).then_inc(s["uc_ready"], 1)
                    assert chl.n == PERC
                ch = Chain(dve, s["lc_chain"], base + (L3_STEPS - 1) * PERC)
                ch(ts(disc, disc, 1.0 - ALPHA, None, ALU.mult))
                ch(tt(ahc, disc, headc, ALU.mult))
                ch(tt(nohome, nohome, OWNC[:, :, D + 1], ALU.add))
                ch(V.tensor_copy(homei, nohome))
                dve.wait_ge(s["mc_in"], 16 * GW * L3_STEPS)
                compact_sums(ch, "lc_carry_in", L3_STEPS)
                ch(tt(Zc, Zc, bc(disc), ALU.mult))
                ch(tt(Zc, Zc, x3c, ALU.add))
                dve.wait_ge(s["lc_carry_out"], L3_STEPS)
                ch(tt(Tc, bf(CAR, W), bc(ahc), ALU.mult))
                tt(Oc, Zc, Tc, ALU.add).then_inc(s["dc_ready"], 1)
            with dve.Else():
                ch = Chain(dve, s["l3_chain"])
                layernorm(XD, F, Z, ch, roots("rootf_in", "rootf_out"))
                ch(tt(U, F, bc(col("dis")), ALU.mult))
                ch(V.memset(M_f, 0.0))
                V.tensor_copy(small[:, 2:3], small[:, 3:4]).then_inc(s["u3_ready"], 1)
                ch(ts(col("scalef"), col("dis"), 1.0 - ALPHA, None, ALU.mult))
                ch(ts(F, F, ALPHA, None, ALU.mult))
                base = ch.n
                PER3 = D + 2 + 3
                with dve.Fori(0, L3_STEPS) as i:
                    ch = Chain(dve, s["l3_chain"], base, i, PER3)
                    dve.wait_ge(s["m3_in"], 16 * EC * i + 16 * EC)
                    segment_sums(ch, M, s["carry3_in"], s["carry3_out"], i + 1, U)
                    ch(tt(Z, Z, bc(col("scalef")), ALU.mult))
                    ch(tt(Z, Z, F, ALU.add))
                    ch(tt(U, Z, bc(col("dis")), ALU.mult))
                    V.tensor_copy(small[:, 2:3], small[:, 3:4]).then_inc(s["u3_ready"], 1)
                    assert ch.n == PER3
                tt(XD, XD, Z, ALU.add).then_inc(s["d_final"], 1)

        @block.scalar
        def _(act):
            roots = [0]

            def root(n):
                for _ in range(n):
                    roots[0] += 1
                    act.wait_ge(s["root_in"], roots[0])
                    S.activation(col("sq_out"), col("sq_in"), ACT.Sqrt).then_inc(s["root_out"], 1)

            with act.Fori(0, EC // 4) as i:
                for b in range(4):
                    t = 4 * i + b
                    act.wait_ge(s["tile_turned"], t + 1)
                    S.copy(ot[b], TP[b % 2])
                    act.wait_ge(s["tile_free"], t + 2)
                    S.copy(rs[b % 2], R[:, 0:NCOL]).then_inc(s["tile_copied"], 1)
            root(1 + len(PAY_PARTS) + 1)
            xt = x[P * DROWS:N].rearrange("(p c) f -> p (c f)", p=TAIL_P)
            outt = out[P * DROWS:N].rearrange("(p c) f -> p (c f)", p=TAIL_P)
            xflat = x[0:P * DROWS].rearrange("(p q) f -> p (q f)", p=P)
            oflat = out[0:P * DROWS].rearrange("(p q) f -> p (q f)", p=P)

            def dense_act(nb, pn, cn, number, place=EARLY_IN):
                w = cn * D
                dxc, dsq, dst1, dst2, dst3 = temps[place]
                for l in range(3):
                    for b in range(nb):
                        act.wait_ge(s["dense_xc"], number(l, b))
                        S.activation(dsq[b][0:pn, 0:w], dxc[b][0:pn, 0:w], ACT.Square).then_inc(s["dense_sq"], 1)
                    for b in range(nb):
                        act.wait_ge(s["dense_var"], number(l, b))
                        S.activation(dst3[b][0:pn, 0:cn], dst2[b][0:pn, 0:cn], ACT.Sqrt).then_inc(s["dense_root"], 1)

            act.wait_ge(s["dense_go"], 1)
            dx = dense_x[EARLY_IN]
            act.dma_start(dx[0][0:TAIL_P, 0:TAIL_C * D], xt).then_inc(s["tail_in"], 16)
            dense_act(1, TAIL_P, TAIL_C, lambda l, b: l + 1)
            act.wait_ge(s["dense_done"], 1)
            act.dma_start(outt, dx[0][0:TAIL_P, 0:TAIL_C * D]).then_inc(s["dense_out"], 16)
            act.wait_ge(s["dense_out"], 16)

            def dense_turn(i, last, place):
                dx = dense_x[place]
                for h in range(2):
                    if not (last and h == 1):
                        act.wait_ge(s["dense_out"], 64 * i + 16 * (1 + 2 * h))
                        for b in range(2):
                            act.dma_start(dx[(2 * h + 2 + b) % 4],
                                          xflat[:, bass.ds(UNROLL * DW * i + DW * (2 * h + 2 + b), DW)]
                                          ).then_inc(s[f"dense_in{1 - h}"], 16)
                    dense_act(2, P, DCH, lambda l, b: 12 * i + (3 + 6 * h + 2 * l + b + 1), place)
                    for b in range(2):
                        act.wait_ge(s["dense_done"], 4 * i + (1 + 2 * h + b + 1))
                        act.dma_start(oflat[:, bass.ds(UNROLL * DW * i + DW * (2 * h + b), DW)],
                                      dx[2 * h + b]).then_inc(s["dense_out"], 16)

            def dense_turns(first, last, place):
                dx = dense_x[place]
                for b in range(2):
                    o = (UNROLL * first + b) * DW
                    act.dma_start(dx[b], xflat[:, o:o + DW]).then_inc(s["dense_in0"], 16)
                if last - 1 > first:
                    with act.Fori(first, last - 1) as i:
                        dense_turn(i, False, place)
                dense_turn(last - 1, True, place)

            dense_turns(0, EARLY, EARLY_IN)
            root(2)
            root(1)

            def branch_roots(sin, sout, widths, before=0):
                for k, w in enumerate(widths, before):
                    act.wait_ge(s[sin], k + 1)
                    S.activation(c["sq_out"][:, 0:w], c["sq_in"][:, 0:w], ACT.Sqrt).then_inc(s[sout], 1)

            longest = act.value_load(fits[0:1, 0:1], min_val=0, max_val=EC)
            with act.If(longest <= GW1):
                branch_roots("root1c_in", "root1c_out", [EC, EC, W, W])
                act.wait_ge(s["dense_go"], 2)
                dense_turns(EARLY, EARLY + 1, BESIDE_IN)
                branch_roots("root1c_in", "root1c_out", [W], 4)
                act.wait_ge(s["dense_go"], 3)
                dense_turns(EARLY + 1, TURNS, LATE_IN)
            with act.Else():
                branch_roots("root1f_in", "root1f_out", [EC, EC])
                act.wait_ge(s["dense_go"], 2)
                dense_turns(EARLY, TURNS, LATE_IN)
            root(1)
            root(2)
            act.wait_ge(s["l2_xin"], 1)
            for b in range(2):
                S.copy(xyc[b], XY16[:, b, :]).then_inc(s["l2_xy"], 1)

            def turned(t, b):
                act.wait_ge(s["l2_tr"], t + 2)
                S.copy(xyt[b], XYTp[b % 2])
                S.copy(oht[b], OTp[b % 2]).then_inc(s["l2_tc"], 1)

            turned(0, 0)

            def l2_turns(first, last):
                with act.Fori(first, last) as i:
                    for b in range(4):
                        t = 4 * i + b
                        S.copy(xyc[(b + 2) % 4].unsqueeze(1), XY16[:, bass.ds(t + 2, 1), :]).then_inc(s["l2_xy"], 1)
                        turned(t + 1, (b + 1) % 4)
                        act.wait_ge(s["l2_mm"], t + 1)
                        S.copy(XS[:, bass.ds(t, 1), :], PSm[b % 2][:, RC - D:RC].unsqueeze(1))
                        S.copy(cs[b][:, 0:RC - D], PSm[b % 2][:, 0:RC - D]).then_inc(s["l2_cs"], 1)

            l2_turns(*L2_TURNS[0])
            root(2)
            act.wait_ge(s["l2_xin"], 2)
            l2_turns(*L2_TURNS[1])
            act.wait_ge(s["gate_in"], 1)
            S.activation(col("sq_out"), col("score"), ACT.Tanh).then_inc(s["gate_out"], 1)
            longest = act.value_load(fits[0:1, 1:2], min_val=0, max_val=EC)

            with act.If(longest <= GW):
                branch_roots("rootc_in", "rootc_out", [EC, W, W])
            with act.Else():
                branch_roots("rootf_in", "rootf_out", [EC])

        @block.tensor
        def _(pe):
            H0 = 512
            halves = ((0, H0), (H0, NCOL))

            def zeros(start, k):
                for a, b in halves:
                    ins = T.matmul(hist[k][:, a:b], z16[:, 0:P], z16[:, 0:b - a], start=start, stop=not start)
                return ins

            pe.wait_ge(s["pool_consts"], 1)
            pe.wait_ge(s["dve_setup"], 1)
            zeros(True, 0)
            zeros(True, 1).then_inc(s["hist_free"], 2)
            with pe.Fori(0, EC // 2) as i:
                for b in range(2):
                    pe.wait_ge(s["hist_built"], 2 * i + (b + 1))
                    for k in range(2):
                        op_, oc_ = onehot(2 * b + k)
                        for lo, hi in halves:
                            ins = T.matmul(hist[k][:, lo:hi], op_, oc_[:, lo:hi], start=False, stop=False)
                    ins.then_inc(s["hist_free"], 1)
            zeros(False, 0)
            zeros(False, 1).then_inc(s["hist_done"], 1)
            for k in range(2):
                pe.wait_ge(s["prefix_in"], k + 1)
                T.matmul(MISC[:, 0:1], upper[:], small[:, 0:1], start=True, stop=True).then_inc(s["prefix_out"], 1)
            pe.wait_ge(s["rec_ready"], 1)
            for lo, hi in halves:
                ins = T.matmul(R[:, lo:hi], ident[:], start_tab[:, lo:hi], start=True, stop=True, skip_group_check=True)
            ins.then_inc(s["tile_free"], 2)

            def turn(t, b):
                pe.wait_ge(s["tile_built"], t + 1)
                T.transpose(TP[b % 2], onehot(b)[0], ident16[:]).then_inc(s["tile_turned"], 1)

            turn(0, 0)
            with pe.Fori(0, EC // 4) as i:
                for b in range(4):
                    t = 4 * i + b
                    op_, oc_ = onehot(b)
                    pe.wait_ge(s["tile_copied"], t + 1)
                    for lo, hi in halves:
                        ins = T.matmul(R[:, lo:hi], op_, oc_[:, lo:hi], start=False, stop=True, skip_group_check=True)
                    ins.then_inc(s["tile_free"], 1)
                    turn(t + 1, (b + 1) % 4)
                    pe.wait_ge(s["tile_looked"], t + 1)
                    for lo, hi in halves:
                        T.matmul(LK[b % 2][:, lo:hi], ot[b], rs[b % 2][:, lo:hi], start=True, stop=True)
                    ins = T.matmul(KR[b % 2], key_col[:, b:b + 1].to_broadcast([P, P]), ident[:], start=True, stop=True)
                    ins.then_inc(s["tile_counted"], 1)

            def first_keys(k):
                pe.wait_ge(s["keys_in"], k)
                T.matmul(MISC, small[:, 0:1].to_broadcast([P, P]), ident[:], start=True, stop=True).then_inc(s["keys_out"], 1)

            def carry(ins, outs, number):
                pe.wait_ge(ins, number)
                T.matmul(CAR, wcarry[:], last_row[:], start=True, stop=True).then_inc(outs, 1)

            def compact_list(before):
                pe.wait_ge(s["list_in"], before + 1)
                T.matmul(MISC, small[:, 3:4].to_broadcast([P, P]), ident[:], start=True, stop=True).then_inc(s["list_out"], 1)
                pe.wait_ge(s["list_in"], before + 2)
                T.matmul(MISC[:, 0:1], wcarry[:], small[:, 3:4], start=True, stop=True).then_inc(s["list_out"], 1)
                pe.wait_ge(s["list_in"], before + 3)
                T.transpose(MISC, wcarry[:], ident[:]).then_inc(s["list_out"], 1)
                pe.wait_ge(s["list_in"], before + 4)
                T.matmul(MISC[:, 0:1], wt, small[:, 3:4], start=True, stop=True).then_inc(s["list_out"], 1)

            first_keys(1)
            compact_list(0)
            carry(s["carry_in"], s["carry_out"], 1)
            longest = pe.value_load(fits[0:1, 0:1], min_val=0, max_val=EC)
            with pe.If(longest <= GW1):
                with pe.Fori(0, L1_STEPS) as i:
                    pe.wait_ge(s["l1c_carry_in"], i + 1)
                    T.matmul(CAR, wc[:], last_row[:], start=True, stop=True).then_inc(s["l1c_carry_out"], 1)
            with pe.Else():
                with pe.Fori(0, L1_STEPS) as i:
                    carry(s["carry1_in"], s["carry1_out"], i + 1)
            first_keys(2)
            compact_list(4)

            def l2_turn(t, b, ahead=1):
                pe.wait_ge(s["l2_oh"], t + 1)
                pe.wait_ge(s["l2_xy"], t + 1)
                T.transpose(OTp[b % 2], oh[b], ident16[:])
                T.transpose(XYTp[b % 2], xyc[b], ident16[:]).then_inc(s["l2_tr"], ahead)

            l2_turn(0, 0, 2)
            with pe.Fori(0, EC // 4) as i:
                for b in range(4):
                    t = 4 * i + b
                    l2_turn(t + 1, (b + 1) % 4)
                    pe.wait_ge(s["l2_tc"], t + 1)
                    pe.wait_ge(s["l2_prod"], t + 1)
                    T.matmul(PWm[b % 2], xyt[b][0:2 * D, :], w_high, start=True, stop=False)
                    T.matmul(PWm[b % 2], xyt[b][0:2 * D, :], w_low, start=False, stop=True)
                    T.matmul(PSm[b % 2], oht[b], rw_high, start=True, stop=False)
                    T.matmul(PSm[b % 2], oht[b], rw_low, start=False, stop=False)
                    T.matmul(PSm[b % 2], xyt[b], rxy_high, start=False, stop=False)
                    T.matmul(PSm[b % 2], xyt[b], rxy_low, start=False, stop=True).then_inc(s["l2_mm"], 1)
            carry(s["carry_in"], s["carry_out"], 2)
            longest = pe.value_load(fits[0:1, 1:2], min_val=0, max_val=EC)
            with pe.If(longest <= GW):
                with pe.Fori(0, L3_STEPS) as i:
                    pe.wait_ge(s["lc_carry_in"], i + 1)
                    T.matmul(CAR, wc[:], last_row[:], start=True, stop=True).then_inc(s["lc_carry_out"], 1)
            with pe.Else():
                with pe.Fori(0, L3_STEPS) as i:
                    carry(s["carry3_in"], s["carry3_out"], i + 1)


def kernel(x, src, dst, edge_type_86, L1_gnn_theta, L2_gnn_weight, L2_gnn_w_comp, L2_gnn_self_loop_weight,
           L2_gnn_A1_w, L2_gnn_A1_b, L2_gnn_A2_w, L2_gnn_A2_b, L2_gnn_rel_emb):
    import numpy as np
    import concourse.bacc as bacc
    from concourse.bass_utils import run_bass_kernel_spmd

    nc = bacc.Bacc("TRN2", target_bir_lowering=False, num_devices=1)
    given = {
        "x": x, "src": src, "dst": dst, "etype": edge_type_86, "theta": L1_gnn_theta,
        "w_basis": np.transpose(np.asarray(L2_gnn_weight), (1, 0, 2)), "w_comp": L2_gnn_w_comp,
        "w_self": L2_gnn_self_loop_weight, "a1t": np.transpose(np.asarray(L2_gnn_A1_w)), "a1b": L2_gnn_A1_b,
        "a2t": np.transpose(np.asarray(L2_gnn_A2_w)), "a2b": L2_gnn_A2_b, "rel": L2_gnn_rel_emb,
    }
    arrays, args = {}, {}
    for name, a in given.items():
        a = np.ascontiguousarray(a)
        arrays["in_" + name] = a
        args[name] = nc.dram_tensor("in_" + name, a.shape, mybir.dt.from_np(a.dtype), kind="ExternalInput").ap()
    args["out"] = nc.dram_tensor("out_0", (N, D), mybir.dt.float32, kind="ExternalOutput").ap()
    build(nc, **args)
    r = run_bass_kernel_spmd(nc, [arrays], core_ids=[0])
    return r.results[0]["out_0"]
```
